# Optimizing a Trainium2 kernel written in Bass

```python
import numpy as np
import jax
import jax.numpy as jnp

def _softmax(x, axis=-1):
    return jax.nn.softmax(x, axis=axis)

def _gelu(x):
    return jax.nn.gelu(x, approximate=True)

def _silu(x):
    return jax.nn.silu(x)

def _sigmoid(x):
    return jax.nn.sigmoid(x)

def _layernorm(x, axis=-1, eps=1e-05):
    m = jnp.mean(x, axis=axis, keepdims=True)
    v = jnp.var(x, axis=axis, keepdims=True)
    return (x - m) / jnp.sqrt(v + eps)

def _scatter_add(tgt, idx, src, axis=0):
    return tgt.at[idx].add(src)

def _segment_sum(src, seg, n):
    return jax.ops.segment_sum(src, seg, n)
kernel_name = 'mk_adaln_d1_jaxref_r4_494acd'

def setup_inputs(seed: int=0):
    np.random.seed(seed)
    _w = jnp.asarray

    def _L0_attn_setup():
        import jax, jax.numpy as jnp
        import numpy as np
        B, T, D, H = (2, 512, 256, 16)
        DH = D // H
        ROPE_BASE = 10000.0

        def _rope(Xh, cos, sin):
            x0 = Xh[..., 0::2]
            x1 = Xh[..., 1::2]
            r0 = cos * x0 - sin * x1
            r1 = sin * x0 + cos * x1
            return jnp.stack((r0, r1), axis=-1).reshape(Xh.shape)
        key = jax.random.key(seed)
        ks = jax.random.split(key, 5)
        s = 1.0 / np.sqrt(D)
        return {'X': jax.random.normal(ks[0], (B, T, D), dtype=jnp.float32), 'W_q': jax.random.normal(ks[1], (D, D), dtype=jnp.float32) * s, 'W_k': jax.random.normal(ks[2], (D, D), dtype=jnp.float32) * s, 'W_v': jax.random.normal(ks[3], (D, D), dtype=jnp.float32) * s, 'W_o': jax.random.normal(ks[4], (D, D), dtype=jnp.float32) * s}
    _L0_attn_in = _L0_attn_setup()

    def _L0_ffn_setup():
        import jax, jax.numpy as jnp
        import numpy as np
        DIM = 256
        N_HEADS = 16
        N_KV_HEADS = 4
        HEAD_DIM = DIM // N_HEADS
        N_REP = N_HEADS // N_KV_HEADS
        N_EXPERTS = 4
        TOP_K = 2
        HIDDEN = 3 * DIM
        EPS = 1.1920928955078125e-07

        def _rmsnorm(x, g):
            var = jnp.mean(jnp.square(x), axis=-1, keepdims=True)
            return x * jax.lax.rsqrt(var + EPS) * g

        def _rotate_half(x):
            x1, x2 = jnp.split(x, 2, axis=-1)
            return jnp.concatenate([-x2, x1], axis=-1)

        def _rope_tables(S):
            inv_freq = 1.0 / 10000.0 ** (jnp.arange(0, HEAD_DIM, 2, dtype=jnp.float32) / HEAD_DIM)
            freqs = jnp.arange(S, dtype=jnp.float32)[:, None] * inv_freq[None, :]
            emb = jnp.concatenate([freqs, freqs], axis=-1)
            return (jnp.cos(emb), jnp.sin(emb))

        def _attention(x, wq, wk, wv, wo):
            B, S, D = x.shape
            q = (x @ wq).reshape(B, S, N_HEADS, HEAD_DIM).transpose(0, 2, 1, 3)
            k = (x @ wk).reshape(B, S, N_KV_HEADS, HEAD_DIM).transpose(0, 2, 1, 3)
            v = (x @ wv).reshape(B, S, N_KV_HEADS, HEAD_DIM).transpose(0, 2, 1, 3)
            cos, sin = _rope_tables(S)
            q = q * cos + _rotate_half(q) * sin
            k = k * cos + _rotate_half(k) * sin
            k = jnp.repeat(k, N_REP, axis=1)
            v = jnp.repeat(v, N_REP, axis=1)
            scores = jnp.einsum('bhqd,bhkd->bhqk', q, k) / jnp.sqrt(jnp.float32(HEAD_DIM))
            causal = jnp.tril(jnp.ones((S, S), dtype=bool))
            scores = jnp.where(causal, scores, -jnp.inf)
            attn = jax.nn.softmax(scores, axis=-1)
            out = jnp.einsum('bhqk,bhkd->bhqd', attn, v)
            return out.transpose(0, 2, 1, 3).reshape(B, S, D) @ wo

        def _moe(x, gate, w1, w2, w3):
            B, S, D = x.shape
            xf = x.reshape(-1, D)
            probs = jax.nn.softmax(xf @ gate, axis=-1)
            w, idx = jax.lax.top_k(probs, TOP_K)
            w = w / jnp.sum(w, axis=-1, keepdims=True)
            oh = jax.nn.one_hot(idx, N_EXPERTS, dtype=xf.dtype)
            comb = jnp.einsum('nk,nke->ne', w, oh)
            out = jnp.zeros_like(xf)
            for e in range(N_EXPERTS):
                h = jax.nn.silu(xf @ w1[e]) * (xf @ w3[e])
                out = out + comb[:, e:e + 1] * (h @ w2[e])
            return out.reshape(B, S, D)
        key = jax.random.key(seed)
        ks = jax.random.split(key, 12)
        s = 0.02
        B, S = (2, 512)
        return {'x': jax.random.normal(ks[0], (B, S, DIM), jnp.float32), 'g1': jnp.ones((DIM,), jnp.float32), 'g2': jnp.ones((DIM,), jnp.float32), 'wq': jax.random.normal(ks[1], (DIM, N_HEADS * HEAD_DIM), jnp.float32) * s, 'wk': jax.random.normal(ks[2], (DIM, N_KV_HEADS * HEAD_DIM), jnp.float32) * s, 'wv': jax.random.normal(ks[3], (DIM, N_KV_HEADS * HEAD_DIM), jnp.float32) * s, 'wo': jax.random.normal(ks[4], (N_HEADS * HEAD_DIM, DIM), jnp.float32) * s, 'gate': jax.random.normal(ks[5], (DIM, N_EXPERTS), jnp.float32) * s, 'w1': jax.random.normal(ks[6], (N_EXPERTS, DIM, HIDDEN), jnp.float32) * s, 'w2': jax.random.normal(ks[7], (N_EXPERTS, HIDDEN, DIM), jnp.float32) * s, 'w3': jax.random.normal(ks[8], (N_EXPERTS, DIM, HIDDEN), jnp.float32) * s}
    _L0_ffn_in = _L0_ffn_setup()
    _L0_c = _w((lambda *s: np.random.randn(*s).astype(np.float32) * 0.05)(1, 256))
    _L0_wmod = _w((lambda *s: np.random.randn(*s).astype(np.float32) * 0.05)(256, 6 * 256) * 256 ** (-0.5))
    _d = {'L0_attn_X': _L0_attn_in['X'], 'L0_attn_W_q': _L0_attn_in['W_q'], 'L0_attn_W_k': _L0_attn_in['W_k'], 'L0_attn_W_v': _L0_attn_in['W_v'], 'L0_attn_W_o': _L0_attn_in['W_o'], 'L0_ffn_g1': _L0_ffn_in['g1'], 'L0_ffn_g2': _L0_ffn_in['g2'], 'L0_ffn_wq': _L0_ffn_in['wq'], 'L0_ffn_wk': _L0_ffn_in['wk'], 'L0_ffn_wv': _L0_ffn_in['wv'], 'L0_ffn_wo': _L0_ffn_in['wo'], 'L0_ffn_gate': _L0_ffn_in['gate'], 'L0_ffn_w1': _L0_ffn_in['w1'], 'L0_ffn_w2': _L0_ffn_in['w2'], 'L0_ffn_w3': _L0_ffn_in['w3'], 'L0_c': _L0_c, 'L0_wmod': _L0_wmod}
    _x0 = _d['L0_attn_X']
    _d['L0_attn_X'] = jax.random.normal(jax.random.fold_in(jax.random.key(seed), 1), (1, 4096, 256), dtype=_x0.dtype)
    del _x0
    return _d

def reference(L0_attn_X, L0_attn_W_q, L0_attn_W_k, L0_attn_W_v, L0_attn_W_o, L0_ffn_g1, L0_ffn_g2, L0_ffn_wq, L0_ffn_wk, L0_ffn_wv, L0_ffn_wo, L0_ffn_gate, L0_ffn_w1, L0_ffn_w2, L0_ffn_w3, L0_c, L0_wmod):

    def _L0_attn_ref(X, W_q, W_k, W_v, W_o):
        import jax, jax.numpy as jnp
        import numpy as np
        B, T, D, H = (2, 512, 256, 16)
        DH = D // H
        ROPE_BASE = 10000.0

        def _rope(Xh, cos, sin):
            x0 = Xh[..., 0::2]
            x1 = Xh[..., 1::2]
            r0 = cos * x0 - sin * x1
            r1 = sin * x0 + cos * x1
            return jnp.stack((r0, r1), axis=-1).reshape(Xh.shape)
        b, t, d = X.shape
        Q = X @ W_q.T
        K = X @ W_k.T
        V = X @ W_v.T
        Qh = Q.reshape(b, t, H, DH).transpose(0, 2, 1, 3)
        Kh = K.reshape(b, t, H, DH).transpose(0, 2, 1, 3)
        Vh = V.reshape(b, t, H, DH).transpose(0, 2, 1, 3)
        theta = ROPE_BASE ** (-2.0 * jnp.arange(DH // 2, dtype=jnp.float32) / DH)
        pos = jnp.arange(t, dtype=jnp.float32)
        angles = pos[:, None] * theta[None, :]
        cos = jnp.cos(angles).astype(Qh.dtype)
        sin = jnp.sin(angles).astype(Qh.dtype)
        Qr = _rope(Qh, cos, sin)
        Kr = _rope(Kh, cos, sin)
        scores = jnp.einsum('bhqd,bhkd->bhqk', Qr, Kr) * DH ** (-0.5)
        causal = jnp.triu(jnp.ones((t, t), dtype=bool), 1)
        neg = jnp.finfo(scores.dtype).min
        scores = jnp.where(causal[None, None], neg, scores)
        pattern = jax.nn.softmax(scores, axis=-1)
        heads = jnp.einsum('bhqk,bhkd->bhqd', pattern, Vh)
        out = heads.transpose(0, 2, 1, 3).reshape(b, t, d)
        return out @ W_o.T

    def _L0_ffn_ref(x, g1, g2, wq, wk, wv, wo, gate, w1, w2, w3):
        import jax, jax.numpy as jnp
        import numpy as np
        DIM = 256
        N_HEADS = 16
        N_KV_HEADS = 4
        HEAD_DIM = DIM // N_HEADS
        N_REP = N_HEADS // N_KV_HEADS
        N_EXPERTS = 4
        TOP_K = 2
        HIDDEN = 3 * DIM
        EPS = 1.1920928955078125e-07

        def _rmsnorm(x, g):
            var = jnp.mean(jnp.square(x), axis=-1, keepdims=True)
            return x * jax.lax.rsqrt(var + EPS) * g

        def _rotate_half(x):
            x1, x2 = jnp.split(x, 2, axis=-1)
            return jnp.concatenate([-x2, x1], axis=-1)

        def _rope_tables(S):
            inv_freq = 1.0 / 10000.0 ** (jnp.arange(0, HEAD_DIM, 2, dtype=jnp.float32) / HEAD_DIM)
            freqs = jnp.arange(S, dtype=jnp.float32)[:, None] * inv_freq[None, :]
            emb = jnp.concatenate([freqs, freqs], axis=-1)
            return (jnp.cos(emb), jnp.sin(emb))

        def _attention(x, wq, wk, wv, wo):
            B, S, D = x.shape
            q = (x @ wq).reshape(B, S, N_HEADS, HEAD_DIM).transpose(0, 2, 1, 3)
            k = (x @ wk).reshape(B, S, N_KV_HEADS, HEAD_DIM).transpose(0, 2, 1, 3)
            v = (x @ wv).reshape(B, S, N_KV_HEADS, HEAD_DIM).transpose(0, 2, 1, 3)
            cos, sin = _rope_tables(S)
            q = q * cos + _rotate_half(q) * sin
            k = k * cos + _rotate_half(k) * sin
            k = jnp.repeat(k, N_REP, axis=1)
            v = jnp.repeat(v, N_REP, axis=1)
            scores = jnp.einsum('bhqd,bhkd->bhqk', q, k) / jnp.sqrt(jnp.float32(HEAD_DIM))
            causal = jnp.tril(jnp.ones((S, S), dtype=bool))
            scores = jnp.where(causal, scores, -jnp.inf)
            attn = jax.nn.softmax(scores, axis=-1)
            out = jnp.einsum('bhqk,bhkd->bhqd', attn, v)
            return out.transpose(0, 2, 1, 3).reshape(B, S, D) @ wo

        def _moe(x, gate, w1, w2, w3):
            B, S, D = x.shape
            xf = x.reshape(-1, D)
            probs = jax.nn.softmax(xf @ gate, axis=-1)
            w, idx = jax.lax.top_k(probs, TOP_K)
            w = w / jnp.sum(w, axis=-1, keepdims=True)
            oh = jax.nn.one_hot(idx, N_EXPERTS, dtype=xf.dtype)
            comb = jnp.einsum('nk,nke->ne', w, oh)
            out = jnp.zeros_like(xf)
            for e in range(N_EXPERTS):
                h = jax.nn.silu(xf @ w1[e]) * (xf @ w3[e])
                out = out + comb[:, e:e + 1] * (h @ w2[e])
            return out.reshape(B, S, D)
        x = x + _attention(_rmsnorm(x, g1), wq, wk, wv, wo)
        x = x + _moe(_rmsnorm(x, g2), gate, w1, w2, w3)
        return x
    x = L0_attn_X
    mod = (_silu(L0_c) @ L0_wmod).reshape(L0_c.shape[0], 6, 1, -1)
    sa, ca, ga, sb, cb, gb = (mod[:, 0], mod[:, 1], mod[:, 2], mod[:, 3], mod[:, 4], mod[:, 5])
    ga = (2 * (ga >= 0) - 1) * jnp.maximum(jnp.abs(ga), 0.25)
    gb = (2 * (gb >= 0) - 1) * jnp.maximum(jnp.abs(gb), 0.25)
    h = _layernorm(x, axis=-1) * (1 + ca) + sa
    x = x + ga * _L0_attn_ref(h, L0_attn_W_q, L0_attn_W_k, L0_attn_W_v, L0_attn_W_o)
    h = _layernorm(x, axis=-1) * (1 + cb) + sb
    x = x + gb * _L0_ffn_ref(h, L0_ffn_g1, L0_ffn_g2, L0_ffn_wq, L0_ffn_wk, L0_ffn_wv, L0_ffn_wo, L0_ffn_gate, L0_ffn_w1, L0_ffn_w2, L0_ffn_w3)
    return x

_drawn_inputs = setup_inputs


def setup_inputs(seed=0):
    import zlib

    import numpy as np

    out = dict(_drawn_inputs(seed))
    spreads = {'L0_ffn_g1': (1.0, 0.6), 'L0_ffn_g2': (1.0, 0.6)}
    factors = {'L0_attn_W_q': 3.5,
     'L0_attn_W_k': 3.173,
     'L0_attn_W_o': 2.7,
     'L0_ffn_wq': 8.0,
     'L0_ffn_wk': 8.0,
     'L0_ffn_wv': 8.0,
     'L0_ffn_wo': 8.0,
     'L0_ffn_gate': 8.0,
     'L0_ffn_w1': 8.0,
     'L0_ffn_w2': 8.0,
     'L0_ffn_w3': 8.0}
    for name, (base, spread) in spreads.items():
        noise = np.random.default_rng([zlib.crc32(name.encode()), seed]).standard_normal(out[name].shape)
        drawn = base * np.exp(spread * noise) if base else spread * noise
        out[name] = jnp.asarray(drawn.astype(out[name].dtype))
    for name, factor in factors.items():
        out[name] = (out[name] * factor).astype(out[name].dtype)
    return out
```

```python
from contextlib import ExitStack

import concourse.bass as bass
from concourse import mybir

P = 128
F32 = mybir.dt.float32
BF16 = mybir.dt.bfloat16
ACT = mybir.ActivationFunctionType
ALU = mybir.AluOpType
AX = mybir.AxisListType

HEADS = 16
DH = 16
GROUP = 4
PARTS = 3
Q_PART = (0, 0, 0, 1, 1, 2)
K_PART = (0, 1, 2, 0, 1, 0)
ROWS = len(Q_PART) * DH
ROWS_M = ROWS + 2
CHUNK = 512
LN_EPS = 1e-5
RMS_EPS = 1.1920928955078125e-07
PAIR_OF_ONES = 1.0 + 0x3F80 / 2.0 ** 23
HIDDEN_NEG = -1e30


class Blocks:

    def __init__(self, supers, more):
        self.supers, self.more = supers, more

    def of(self, each, plus):
        return self.supers * (CHUNK // P * each) + (self.more * each + plus)


def adaln_program(nc, x, wqkv, rope, wo, g12, wmod, c_col, gate, w1, w2, w3, ident, masks, lower, out):
    T, D = x.shape
    NT = T // P
    NCH = T // CHUNK
    TPC = CHUNK // P
    KD = D // P
    E = gate.shape[1]
    HID = w1.shape[2]
    HB = HID // P
    NGROUPS = HEADS // GROUP
    KVH = (HEADS, NGROUPS)

    x1_dram = nc.dram_tensor("x1_dram", (T, D), F32, kind="Internal").ap()
    h2_dram = nc.dram_tensor("h2_dram", (T, D), F32, kind="Internal").ap()
    q_dram = nc.dram_tensor("q_dram", (PARTS, D, T), BF16, kind="Internal").ap()
    k_dram = nc.dram_tensor("k_dram", (PARTS, D, T), BF16, kind="Internal").ap()

    def wait_apart(eng, sem, value):
        value = eng.to_reg(value)
        eng.wait_ge(begun, 1)
        eng.wait_ge(sem, value)

    def by_tile(dram):
        return dram.rearrange("(i p) f -> p i f", p=P)

    def tiles(c):
        return bass.ds(c * TPC, TPC)

    def cols(c):
        return bass.ds(c * CHUNK, CHUNK)

    def feature_major(a, c, k):
        return a[:, bass.ds(c * TPC + k * (TPC // KD), TPC // KD), :].rearrange("p a f -> p (a f)")

    def row_bcast(row, n):
        return row.unsqueeze(1).to_broadcast([P, n, row.shape[1]])

    def col_bcast(a, w):
        return a.unsqueeze(2).to_broadcast([P, a.shape[1], w])

    class Space:

        def __init__(self, name):
            self.name = name
            self.sems = []

        def __enter__(self):
            self.stack = ExitStack()
            return self

        def __exit__(self, *a):
            if a[0] is None:
                with nc.Block() as block:

                    @block.sync
                    def _(sp):
                        for handle in self.sems:
                            sp.sem_clear(handle)

            self.stack.close()

        def sb(self, name, shape, dt=F32):
            return self.stack.enter_context(nc.sbuf_tensor(f"{self.name}_{name}", shape, dt))

        def ps(self, name, shape, dt=F32):
            return self.stack.enter_context(nc.psum_tensor(f"{self.name}_{name}", shape, dt))

        def sem(self, name):
            self.sems.append(self.stack.enter_context(nc.semaphore(f"{self.name}_{name}")))
            return self.sems[-1]

    def setup(ident_f, ident_b, neg_ident_b, mask_k, mask_q, mod, gains, neg_half):
        with Space("set") as s:
            msk = s.sb("msk", [P, 2, P])
            cc = s.sb("cc", [P, KD])
            sc = s.sb("sc", [P, KD])
            scb = s.sb("scb", [P, KD, P])
            ones = s.sb("ones", [P, P])
            wm = s.sb("wm", [P, KD, 6 * D])
            grow = s.sb("grow", [1, 2 * D])
            raw = s.sb("raw", [P, 6 * D])
            sign = s.sb("sign", [P, 2, D])
            pm = [s.ps(f"pm{n}", [P, CHUNK]) for n in range(4)]
            loaded, ones_set, silu_done = s.sem("loaded"), s.sem("ones_set"), s.sem("silu_done")
            bc_done, mod_done, raw_done, dve = s.sem("bc_done"), s.sem("mod_done"), s.sem("raw_done"), s.sem("dve")
            ident_in = s.sem("ident_in")
            with nc.Block() as block:

                @block.sync
                def _(sp):
                    sp.nop().then_inc(begun, 1)
                    sp.dma_start(ident_f[:, :], ident).then_inc(ident_in, 16)
                    sp.dma_start(msk[:, :, :], masks.rearrange("a p n -> p a n")).then_inc(ident_in, 16)
                    sp.dma_start(cc[:, :], c_col).then_inc(loaded, 16)
                    sp.dma_start(grow[:, :], g12).then_inc(loaded, 16)
                    sp.dma_start(wm[:, :, :], wmod.rearrange("(k p) n -> p k n", p=P)).then_inc(loaded, 16)
                    sp.wait_ge(loaded, 48)

                @block.scalar
                def _(act):
                    act.wait_ge(loaded, 48)
                    nc.scalar.activation(sc[:, :], cc[:, :], ACT.Silu).then_inc(silu_done, 1)
                    for n in range(4):
                        act.wait_ge(mod_done, n + 1)
                        if n < 3:
                            nc.scalar.copy(raw[:, cols(n)], pm[n][:, :]).then_inc(raw_done, 1)
                        else:
                            nc.scalar.copy(gains[:, :, :].rearrange("p a f -> p (a f)"), pm[n][:, :]).then_inc(raw_done, 1)

                @block.vector
                def _(dve_e):
                    nc.vector.memset(ones[:, :], 1.0).then_inc(ones_set, 1)
                    nc.vector.memset(neg_half[:, :], -0.5).then_inc(ones_set, 1)
                    dve_e.wait_ge(ones_set, 1)
                    dve_e.wait_ge(silu_done, 1)
                    for k in range(KD):
                        nc.vector.tensor_scalar(scb[:, k, :], ones[:, :], sc[:, k:k + 1], None, ALU.mult).then_inc(bc_done, 1)
                    dve_e.wait_ge(ident_in, 32)
                    nc.vector.tensor_copy(ident_b[:, :], ident_f[:, :])
                    nc.vector.tensor_scalar(neg_ident_b[:, :], ident_f[:, :], -1.0, None, ALU.mult)
                    nc.vector.tensor_copy(mask_k[:, :], msk[:, 0, :])
                    nc.vector.tensor_copy(mask_q[:, :], msk[:, 1, :])
                    dve_e.wait_ge(raw_done, 4)
                    r = raw[:, :].rearrange("p (v f) -> p v f", v=6)
                    for v in (0, 3):
                        nc.vector.tensor_copy(mod[:, v, :], r[:, v, :])
                    for v in (1, 4):
                        nc.vector.tensor_scalar(mod[:, v, :], r[:, v, :], 1.0, None, ALU.add)
                    for n, v in enumerate((2, 5)):
                        nc.vector.tensor_scalar(sign[:, n, :], r[:, v, :], 0.0, 2.0, ALU.is_ge, ALU.mult).then_inc(dve, 1)
                        dve_e.wait_ge(dve, 4 * n + 1)
                        nc.vector.tensor_scalar(sign[:, n, :], sign[:, n, :], -1.0, None, ALU.add).then_inc(dve, 1)
                        nc.vector.scalar_tensor_tensor(out=mod[:, v, :], in0=r[:, v, :], scalar=-1.0, in1=r[:, v, :],
                                                       op0=ALU.mult, op1=ALU.max).then_inc(dve, 1)
                        dve_e.wait_ge(dve, 4 * n + 3)
                        nc.vector.scalar_tensor_tensor(out=mod[:, v, :], in0=mod[:, v, :], scalar=0.25, in1=sign[:, n, :],
                                                       op0=ALU.max, op1=ALU.mult).then_inc(dve, 1)
                    dve_e.wait_ge(dve, 8)

                @block.tensor
                def _(pe):
                    pe.wait_ge(bc_done, KD)
                    for n in range(3):
                        for k in range(KD):
                            mm = nc.tensor.matmul(pm[n][:, :], scb[:, k, :], wm[:, k, cols(n)], start=(k == 0), stop=(k == KD - 1))
                        mm.then_inc(mod_done, 1)
                    nc.tensor.matmul(pm[3][:, :], ones[0:1, :], grow[:, :], start=True, stop=True).then_inc(mod_done, 1)

    def norms(name, X, src, shift, scale, rms_gain, Y, keep, neg_half):
        with Space(name) as s:
            st = s.sb("st", [P, TPC, 6])
            mv = s.sb("mv", [P, TPC, 2])
            var = s.sb("var", [P, TPC])
            rstd = s.sb("rstd", [P, TPC])
            sq = s.sb("sq", [P, 2, D])
            ssq = s.sb("ssq", [P, TPC])
            ms = s.sb("ms", [P, TPC])
            rrms = s.sb("rrms", [P, TPC])
            loaded = s.sem("loaded")
            stats_done, aggr_done, var_done, rstd_done = s.sem("stats_done"), s.sem("aggr_done"), s.sem("var_done"), s.sem("rstd_done")
            centred, scaled, shifted = s.sem("centred"), s.sem("scaled"), s.sem("shifted")
            squared, ms_done, rrms_done, rms_out, stored = s.sem("squared"), s.sem("ms_done"), s.sem("rrms_done"), s.sem("rms_out"), s.sem("stored")
            ln = scale is not None
            with nc.Block() as block:

                @block.sync
                def _(sp):
                    if src is not None:
                        with sp.Fori(0, NCH) as c:
                            sp.dma_start(X[:, tiles(c), :], by_tile(src)[:, tiles(c), :]).then_inc(loaded, 16)
                            wait_apart(sp, loaded, c * 16 + 16)
                    if keep is not None:
                        with sp.Fori(0, NCH) as c:
                            wait_apart(sp, shifted, c + 1)
                            sp.dma_start(by_tile(keep)[:, tiles(c), :], X[:, tiles(c), :]).then_inc(stored, 16)
                            wait_apart(sp, stored, c * 16 + 16)

                @block.vector
                def _(dve):
                    if rms_gain is not None:
                        dve.nop().then_inc(rms_out, TPC)
                    with dve.Fori(0, NCH) as c:
                        if ln:
                            if src is not None:
                                dve.wait_ge(loaded, c * 16 + 16)
                            for j in range(TPC):
                                nc.vector.bn_stats(st[:, j, :], X[:, bass.ds(c * TPC + j, 1), :].rearrange("p a f -> p (a f)")).then_inc(stats_done, 1)
                            for j in range(TPC):
                                wait_apart(dve, stats_done, c * TPC + j + 1)
                                nc.vector.bn_aggr(mv[:, j, :], st[:, j, :]).then_inc(aggr_done, 1)
                            dve.wait_ge(rstd_done, c + 1)
                            for j in range(TPC):
                                xt = X[:, bass.ds(c * TPC + j, 1), :].rearrange("p a f -> p (a f)")
                                nc.vector.tensor_scalar(xt, xt, mv[:, j, 0:1], rstd[:, j:j + 1], ALU.subtract, ALU.mult).then_inc(centred, 1)
                            dve.wait_ge(centred, c * TPC + TPC)
                            nc.vector.tensor_tensor(X[:, tiles(c), :], X[:, tiles(c), :], row_bcast(scale, TPC), ALU.mult).then_inc(scaled, 1)
                        if rms_gain is not None:
                            dve.wait_ge(rrms_done, c + 1)
                            for j in range(TPC):
                                i = bass.ds(c * TPC + j, 1)
                                nc.vector.scalar_tensor_tensor(
                                    out=Y[:, i, :].rearrange("p a f -> p (a f)"), in0=X[:, i, :].rearrange("p a f -> p (a f)"),
                                    scalar=rrms[:, j:j + 1], in1=rms_gain, op0=ALU.mult, op1=ALU.mult).then_inc(rms_out, 1)

                @block.gpsimd
                def _(pool):
                    if rms_gain is not None:
                        pool.nop().then_inc(ms_done, 1)
                    with pool.Fori(0, NCH) as c:
                        if ln:
                            wait_apart(pool, aggr_done, c * TPC + TPC)
                            nc.gpsimd.tensor_scalar(var[:, :], mv[:, :, 1], LN_EPS, None, ALU.add).then_inc(var_done, 1)
                            pool.wait_ge(var_done, c + 1)
                            nc.gpsimd.tensor_tensor(rstd[:, :], var[:, :], neg_half[:, 0:TPC], ALU.pow).then_inc(rstd_done, 1)
                            pool.wait_ge(scaled, c + 1)
                            nc.gpsimd.tensor_tensor(X[:, tiles(c), :], X[:, tiles(c), :], row_bcast(shift, TPC), ALU.add).then_inc(shifted, 1)
                        if rms_gain is not None:
                            wait_apart(pool, squared, c * TPC + TPC + 2)
                            wait_apart(pool, rms_out, c * TPC + TPC)
                            nc.gpsimd.tensor_scalar(ms[:, :], ssq[:, :], 1.0 / D, RMS_EPS, ALU.mult, ALU.add).then_inc(ms_done, 1)
                            pool.wait_ge(ms_done, c + 2)
                            nc.gpsimd.tensor_tensor(rrms[:, :], ms[:, :], neg_half[:, 0:TPC], ALU.pow).then_inc(rrms_done, 1)

                if rms_gain is not None:

                    @block.scalar
                    def _(act):
                        act.nop().then_inc(squared, 2)
                        with act.Fori(0, NCH) as c:
                            if ln:
                                act.wait_ge(shifted, c + 1)
                            act.wait_ge(ms_done, c + 1)
                            for j in range(TPC):
                                act.wait_ge(squared, c * TPC + j + 1)
                                nc.scalar.activation(sq[:, j % 2, :], X[:, bass.ds(c * TPC + j, 1), :].rearrange("p a f -> p (a f)"),
                                                     ACT.Square, accum_out=ssq[:, j:j + 1]).then_inc(squared, 1)


    def projections(name, H, w_dram, rope_dram, V, kv_heads):
        KV = kv_heads * DH
        q_units = [("q", n, P) for n in range(KD)]
        k_units = [("k", n, min(KV, P)) for n in range(max(1, KV // P))]
        rope_units = q_units + k_units
        NV, VW = max(1, KV // P), min(KV, P)
        NR = len(rope_units)
        U = NV + NR
        assert U % 2 == 0
        off_k, off_qs, off_ks, off_v = D, D + KV, 2 * D + KV, 2 * D + 2 * KV
        with Space(name) as s:
            W = s.sb("W", [P, KD, 2 * D + 3 * KV])
            cos, sin = s.sb("cos", [P, T]), s.sb("sin", [P, T])
            Hs = s.sb("Hs", [P, TPC, D])
            hT = s.sb("hT", [P, KD, CHUNK])
            vT = s.sb("vT", [P, NV, CHUNK])
            direct, crossed = s.sb("direct", [P, 2, CHUNK]), s.sb("crossed", [P, 2, CHUNK])
            turned, rest = s.sb("turned", [P, 2, CHUNK]), s.sb("rest", [P, 2, CHUNK])
            parts = s.sb("parts", [P, NR, PARTS, CHUNK], BF16)
            ps_t = s.ps("ps_t", [P, KD, CHUNK])
            ps_a = [s.ps(f"ps_a{n}", [P, CHUNK]) for n in range(2)]
            ps_b = [s.ps(f"ps_b{n}", [P, CHUNK]) for n in range(2)]
            ps_v = s.ps("ps_v", [P, TPC, D])
            w_in, tab_in = s.sem("w_in"), s.sem("tab_in")
            staged, h_turned, hT_ready = s.sem("staged"), s.sem("h_turned"), s.sem("hT_ready")
            unit_ready, v_evac, rope_taken = s.sem("unit_ready"), s.sem("v_evac"), s.sem("rope_taken")
            v_turned, v_placed = s.sem("v_turned"), s.sem("v_placed")
            summed, part1, rest_done, part2, part3 = s.sem("summed"), s.sem("part1"), s.sem("rest_done"), s.sem("part2"), s.sem("part3")
            stored = [s.sem(f"stored{r}") for r in range(NR)]

            def slot_user(r):
                if r >= 2:
                    return r - 2 + 1 + 2
                q = NR - 1 if (NR - 1) % 2 == r % 2 else NR - 2
                return q - NR + 1 + 2

            with nc.Block() as block:

                @block.sync
                def _(sp):
                    sp.dma_start(W[:, :, :], w_dram.rearrange("(k p) n -> p k n", p=P)).then_inc(w_in, 16)
                    sp.dma_start(cos[:, :], rope_dram[0]).then_inc(tab_in, 16)
                    sp.dma_start(sin[:, :], rope_dram[1]).then_inc(tab_in, 16)
                    for r in range(NR):
                        sp.nop().then_inc(stored[r], 16)
                    with sp.Fori(0, NCH) as c:
                        for r, (kind, n, M) in enumerate(rope_units):
                            dst = (q_dram if kind == "q" else k_dram)[:, n * P:n * P + M, cols(c)]
                            wait_apart(sp, part3, c * NR + r + 1 + 2)
                            sp.dma_start(dst.rearrange("a f t -> f a t"), parts[0:M, r, :, :]).then_inc(stored[r], 16)
                    for r in range(NR):
                        sp.wait_ge(stored[r], 16 * NCH + 16)

                @block.gpsimd
                def _(pool):
                    pool.nop().then_inc(summed, 2)
                    pool.nop().then_inc(part3, 2)
                    with pool.Fori(0, NCH) as c:
                        wait_apart(pool, h_turned, c + 1)
                        nc.gpsimd.tensor_copy(Hs[:, :, :], H[:, tiles(c), :]).then_inc(staged, 1)
                        for r in range(NR + 1):
                            if r < NR:
                                M = rope_units[r][2]
                                pool.wait_ge(rope_taken, c * NR + r + 1 + 2)
                                pool.wait_ge(rest_done, c * NR + slot_user(r))
                                nc.gpsimd.tensor_tensor(turned[0:M, r % 2, :], direct[0:M, r % 2, :], crossed[0:M, r % 2, :],
                                                        ALU.add).then_inc(summed, 1)
                            if r >= 1:
                                M = rope_units[r - 1][2]
                                pool.wait_ge(part2, c * NR + r)
                                nc.gpsimd.tensor_tensor(parts[0:M, r - 1, 2, :], rest[0:M, (r - 1) % 2, :], parts[0:M, r - 1, 1, :],
                                                        ALU.subtract).then_inc(part3, 1)

                @block.scalar
                def _(act):
                    act.nop().then_inc(v_placed, 1)
                    with act.Fori(0, NCH) as c:
                        act.wait_ge(h_turned, c + 2)
                        act.wait_ge(v_turned, c + 1)
                        for k in range(KD):
                            nc.scalar.copy(hT[:, k, :], ps_t[:, k, :]).then_inc(hT_ready, 1)
                        for v in range(NV):
                            act.wait_ge(unit_ready, c * U + v + 1)
                            nc.scalar.copy(vT[0:VW, v, :], ps_a[v % 2][0:VW, :]).then_inc(v_evac, 1)
                        for r in range(NR + 1):
                            if r < NR:
                                M = rope_units[r][2]
                                act.wait_ge(summed, c * NR + r + 1 + 2)
                                act.wait_ge(stored[r], c * 16 + 16)
                                nc.scalar.copy(parts[0:M, r, 0, :], turned[0:M, r % 2, :]).then_inc(part1, 1)
                            if r >= 1:
                                M = rope_units[r - 1][2]
                                act.wait_ge(rest_done, c * NR + r + 2)
                                nc.scalar.copy(parts[0:M, r - 1, 1, :], rest[0:M, (r - 1) % 2, :]).then_inc(part2, 1)
                        act.wait_ge(v_turned, c + 2)
                        nc.scalar.copy(V[:, tiles(c), 0:KV], ps_v[:, :, 0:KV]).then_inc(v_placed, 1)

                @block.vector
                def _(dve):
                    dve.nop().then_inc(rope_taken, 2)
                    dve.nop().then_inc(rest_done, 2)
                    dve.wait_ge(tab_in, 32)
                    with dve.Fori(0, NCH) as c:
                        for r in range(NR + 1):
                            if r < NR:
                                M, slot = rope_units[r][2], (NV + r) % 2
                                dve.wait_ge(unit_ready, c * U + NV + r + 1)
                                dve.wait_ge(summed, c * NR + slot_user(r))
                                nc.vector.tensor_tensor(direct[0:M, r % 2, :], ps_a[slot][0:M, :], cos[0:M, cols(c)], ALU.mult)
                                nc.vector.tensor_tensor(crossed[0:M, r % 2, :], ps_b[slot][0:M, :], sin[0:M, cols(c)], ALU.mult).then_inc(rope_taken, 1)
                            if r >= 1:
                                M = rope_units[r - 1][2]
                                dve.wait_ge(part1, c * NR + r)
                                dve.wait_ge(part3, c * NR + slot_user(r - 1))
                                nc.vector.tensor_tensor(rest[0:M, (r - 1) % 2, :], turned[0:M, (r - 1) % 2, :], parts[0:M, r - 1, 0, :],
                                                        ALU.subtract).then_inc(rest_done, 1)

                @block.tensor
                def _(pe):
                    pe.nop().then_inc(h_turned, 1)
                    pe.nop().then_inc(v_turned, 1)
                    pe.wait_ge(w_in, 16)
                    with pe.Fori(0, NCH) as c:
                        pe.wait_ge(staged, c + 1)
                        for k in range(KD):
                            for j in range(TPC):
                                tr = nc.tensor.transpose(ps_t[:, k, j * P:(j + 1) * P], Hs[:, j, k * P:(k + 1) * P], ident_f[:, :])
                        tr.then_inc(h_turned, 1)
                        pe.wait_ge(hT_ready, c * KD + KD)
                        for u in range(U):
                            if u < 2:
                                pe.wait_ge(rope_taken, c * NR + u - 1 + 2)
                            elif u - 2 < NV:
                                pe.wait_ge(v_evac, c * NV + u - 2 + 1)
                            else:
                                pe.wait_ge(rope_taken, c * NR + u - 2 - NV + 1 + 2)
                            if u < NV:
                                todo = [(ps_a[u % 2], off_v + u * P, VW)]
                            else:
                                kind, n, M = rope_units[u - NV]
                                a, b = (0, off_qs) if kind == "q" else (off_k, off_ks)
                                todo = [(ps_a[u % 2], a + n * P, M), (ps_b[u % 2], b + n * P, M)]
                            for bank, at, M in todo:
                                for k in range(KD):
                                    mm = nc.tensor.matmul(bank[0:M, :], W[:, k, at:at + M], hT[:, k, :], start=(k == 0), stop=(k == KD - 1))
                            mm.then_inc(unit_ready, 1)
                        wait_apart(pe, v_evac, c * NV + NV)
                        pe.wait_ge(v_placed, c + 1)
                        for j in range(TPC):
                            for v in range(NV):
                                tr = nc.tensor.transpose(ps_v[:, j, v * P:v * P + VW], vT[0:VW, v, j * P:(j + 1) * P], ident_f[0:VW, 0:VW])
                        tr.then_inc(v_turned, 1)

    def attention(name, V, A, kv_heads):
        KH = GROUP if kv_heads == HEADS else 1
        VC = KH * DH
        LAST = NCH - 1
        unit0 = [2 * c * (c + 1) for c in range(NCH + 1)]
        UNITS = unit0[NCH]
        super0 = [n // TPC for n in unit0]
        SUPERS = super0[NCH]
        PAIRS = GROUP // 2
        QBUF = 4
        n_qdma = len(Q_PART)
        with Space(name) as s:
            K = s.sb("K", [ROWS_M, 2 * KH, T], BF16)
            Q = s.sb("Q", [ROWS_M, QBUF * GROUP, CHUNK], BF16)
            prob = s.sb("prob", [P, 2, GROUP, CHUNK])
            v_now = s.sb("v_now", [P, 2, KH, 32])
            o_sb = s.sb("o_sb", [P, CHUNK])
            part_max = s.sb("part_max", [P, GROUP, TPC, NCH])
            row_max = s.sb("row_max", [P, GROUP * TPC])
            max_hl = s.sb("max_hl", [P, GROUP * TPC, 2], BF16)
            recip = s.sb("recip", [P, TPC, GROUP])
            sT = [s.ps(f"sT{n}", [P, 2, CHUNK]) for n in range(PAIRS)]
            s_max = [s.ps(f"s_max{n}", [P, CHUNK]) for n in range(2)]
            o_acc = s.ps("o_acc", [P, CHUNK])
            o_tok = s.ps("o_tok", [P, TPC, P])
            k_in, q_in = s.sem("k_in"), s.sem("q_in")
            ones_set, v_clear, v_staged = s.sem("ones_set"), s.sem("v_clear"), s.sem("v_staged")
            scores_ready, exp_done, pv_done = s.sem("scores_ready"), s.sem("exp_done"), s.sem("pv_done")
            max_scores, max_taken, max_final = s.sem("max_scores"), s.sem("max_taken"), s.sem("max_final")
            hi_done, max_split, rows_ready = s.sem("hi_done"), s.sem("max_split"), s.sem("rows_ready")
            rows_a, rows_v = s.sem("rows_a"), s.sem("rows_v")
            o_copied, o_turned, recip_done, o_placed = s.sem("o_copied"), s.sem("o_turned"), s.sem("recip_done"), s.sem("o_placed")

            def at_stage(eng, g, c):
                return eng.snap(g * SUPERS + super0[c]), eng.snap(g * NCH + c)

            def kh(h):
                return h if KH == GROUP else 0

            with nc.Block() as block:

                @block.sync
                def _(sp):
                    def load_k(g, slot):
                        for b, part in enumerate(K_PART):
                            src = k_dram[part].rearrange("(h d) t -> d h t", d=DH)[:, bass.ds(g * KH, KH), :]
                            sp.dma_start(K[b * DH:(b + 1) * DH, bass.ds(slot * KH, KH), :], src).then_inc(k_in, 16)

                    load_k(0, 0)
                    sp.wait_ge(k_in, 16 * len(K_PART))
                    with sp.Fori(0, NGROUPS) as g:
                        for c in range(NCH):
                            wait_apart(sp, o_copied, g * NCH + c + 1)
                            for b, part in enumerate(Q_PART):
                                src = q_dram[part].rearrange("(h d) t -> d h t", d=DH)[:, bass.ds(g * GROUP, GROUP), c * CHUNK:(c + 1) * CHUNK]
                                buf = c % QBUF * GROUP
                                sp.dma_start(Q[b * DH:(b + 1) * DH, buf:buf + GROUP, :], src).then_inc(q_in, 16)
                            wait_apart(sp, q_in, (g * NCH + c + 1) * 16 * n_qdma)
                            if c == 3:
                                load_k((g + 1) % NGROUPS, (g + 1) % 2)
                                wait_apart(sp, k_in, (g + 2) * 16 * len(K_PART))

                @block.gpsimd
                def _(pool):
                    nc.gpsimd.memset(v_now[:, :, :, :], 0.0).then_inc(v_clear, 1)
                    pool.wait_ge(v_clear, 1)
                    nc.gpsimd.memset(v_now[:, :, :, DH:DH + 1], 1.0).then_inc(v_clear, 1)
                    pool.wait_ge(v_clear, 2)

                    def stage_v(g, block_of_keys, slot, unit):
                        wait_apart(pool, pv_done, unit.of(1, 1))
                        nc.gpsimd.tensor_copy(
                            v_now[:, slot, :, 0:DH],
                            V[:, bass.ds(block_of_keys, 1), bass.ds(g * VC, VC)].rearrange("p a (h d) -> p (a h) d", d=DH)).then_inc(v_staged, 1)

                    with pool.Fori(0, NGROUPS) as g:
                        for c in range(NCH):
                            supers, _ = at_stage(pool, g, c)
                            for n in range(TPC):
                                stage_v(g, TPC * c + TPC - 1 - n, n % 2, Blocks(supers, n))
                            if c:
                                with pool.Fori(0, c) as sb:
                                    now = pool.snap(supers + sb)
                                    for j in range(TPC):
                                        stage_v(g, sb * TPC + j, j % 2, Blocks(now, TPC + j))

                @block.scalar
                def _(act):
                    def exps(unit, slot, off):
                        for p in range(PAIRS):
                            act.wait_ge(scores_ready, unit.of(PAIRS, p + 1))
                            act.wait_ge(pv_done, unit.of(1, 1))
                            nc.scalar.activation(prob[:, slot, 2 * p:2 * p + 2, off:CHUNK], sT[p][:, :, off:CHUNK], ACT.Exp,
                                                 scale=DH ** -0.5).then_inc(exp_done, 1)

                    def place_rows(n, c):
                        act.wait_ge(rows_ready, n + 2)
                        buf = c % QBUF * GROUP
                        nc.scalar.copy(Q[ROWS:ROWS_M, buf:buf + 2, :], sT[0][ROWS:ROWS_M, :, :]).then_inc(rows_a, 1)

                    act.nop().then_inc(o_copied, 4)
                    act.nop().then_inc(exp_done, PAIRS)
                    with act.Fori(0, NGROUPS) as g:
                        place_rows(g * NCH, 0)
                        for c in range(NCH):
                            supers, chunks = at_stage(act, g, c)
                            for n in range(TPC):
                                exps(Blocks(supers, n), n % 2, (TPC - 1 - n) * P)
                            if c:
                                with act.Fori(0, c) as sb:
                                    now = act.snap(supers + sb)
                                    for j in range(TPC):
                                        exps(Blocks(now, TPC + j), j % 2, 0)
                            if c < LAST:
                                place_rows(chunks + 1, c + 1)
                            act.wait_ge(pv_done, Blocks(supers, TPC * (c + 1)).of(1, 2))
                            act.wait_ge(o_turned, chunks + 1)
                            nc.scalar.copy(o_sb[:, :], o_acc[:, :]).then_inc(o_copied, 1)

                @block.vector
                def _(dve):
                    def max_unit(unit, qb, sb, width):
                        for h in range(GROUP):
                            dve.wait_ge(max_scores, unit.of(GROUP, h + 1))
                            nc.vector.reduce_max(part_max[:, h, qb, bass.ds(sb, 1)], s_max[h % 2][:, 0:width], AX.X).then_inc(max_taken, 1)

                    def finish_max(n, c, end):
                        dve.wait_ge(max_taken, end.of(GROUP, 2))
                        dve.wait_ge(rows_ready, n + 1)
                        nc.vector.reduce_max(row_max[:, :], part_max[:, :, :, 0:c + 1].rearrange("p h q s -> p (h q) s"), AX.X).then_inc(max_final, 1)
                        dve.wait_ge(max_final, n + 1)
                        nc.vector.tensor_copy(max_hl[:, :, 0], row_max[:, :]).then_inc(hi_done, 1)
                        dve.wait_ge(hi_done, n + 1)
                        nc.vector.tensor_tensor(max_hl[:, :, 1], row_max[:, :], max_hl[:, :, 0], ALU.subtract).then_inc(max_split, 1)
                        dve.wait_ge(rows_ready, n + 2)
                        buf = c % QBUF * GROUP
                        nc.vector.tensor_copy(Q[ROWS:ROWS_M, buf + 2:buf + 4, :], sT[1][ROWS:ROWS_M, :, :]).then_inc(rows_v, 1)

                    def place_o(n, g, c):
                        dve.wait_ge(o_turned, n + 2)
                        o = o_tok[:, :, :].rearrange("p q (h d) -> p q h d", h=GROUP)
                        nc.vector.reciprocal(recip[:, :, :], o[:, :, :, DH]).then_inc(recip_done, 1)
                        dve.wait_ge(recip_done, n + 1)
                        dst = A[:, c * TPC:(c + 1) * TPC, bass.ds(g * GROUP * DH, GROUP * DH)].rearrange("p q (h d) -> p q h d", h=GROUP)
                        nc.vector.tensor_tensor(dst, o[:, :, :, 0:DH], recip[:, :, :].unsqueeze(3).to_broadcast([P, TPC, GROUP, DH]),
                                                ALU.mult).then_inc(o_placed, 1)

                    dve.nop().then_inc(max_taken, 2)
                    dve.nop().then_inc(o_placed, 1)
                    nc.vector.memset(K[ROWS:ROWS_M, :, :].bitcast(F32), PAIR_OF_ONES).then_inc(ones_set, 1)
                    with dve.Fori(0, NGROUPS) as g:
                        supers, chunks = at_stage(dve, g, 0)
                        for qb in range(TPC):
                            max_unit(Blocks(supers, qb), qb, 0, (qb + 1) * P)
                        finish_max(chunks, 0, Blocks(supers, TPC))
                        for c in range(NCH):
                            supers, chunks = at_stage(dve, g, c)
                            ahead = TPC * (c + 1)
                            for j in range(TPC):
                                if c < LAST:
                                    max_unit(Blocks(supers, ahead + 2 * j), j, c + 1, (j + 1) * P)
                                    max_unit(Blocks(supers, ahead + 2 * j + 1), j, c, CHUNK)
                                if j == 0 and c:
                                    place_o(chunks - 1, g, c - 1)
                            if c and c < LAST:
                                with dve.Fori(0, c) as sb:
                                    now = dve.snap(supers + sb)
                                    for j in range(TPC):
                                        max_unit(Blocks(now, ahead + 2 * TPC + j), j, sb, CHUNK)
                            if c < LAST:
                                finish_max(chunks + 1, c + 1, Blocks(supers, ahead + TPC * (c + 2)))
                        place_o(chunks, g, LAST)

                @block.tensor
                def _(pe):
                    def max_tile(k_slot, unit, h, c, qb, sb, width, diag):
                        pe.wait_ge(max_taken, unit.of(GROUP, h + 1))
                        q = Q[0:ROWS, c % QBUF * GROUP + h, qb * P:(qb + 1) * P]
                        k = K[0:ROWS, bass.ds(k_slot + kh(h), 1), bass.ds(sb * CHUNK, width)].rearrange("r a k -> r (a k)")
                        mm = nc.tensor.matmul(s_max[h % 2][:, 0:width], q, k, start=True, stop=not diag)
                        if diag:
                            mm = nc.tensor.matmul(s_max[h % 2][:, width - P:width], ident_b[:, :], mask_q[:, :], start=False, stop=True)
                        mm.then_inc(max_scores, 1)

                    def scores(k_slot, unit, c, block_of_keys, off, p, diag):
                        pe.wait_ge(exp_done, unit.of(PAIRS, p + 1))
                        for hh in range(2):
                            h = 2 * p + hh
                            k = K[:, bass.ds(k_slot + kh(h), 1), bass.ds(block_of_keys * P, P)].rearrange("r a k -> r (a k)")
                            mm = nc.tensor.matmul(sT[p][:, hh, off:CHUNK], k, Q[:, c % QBUF * GROUP + h, off:CHUNK], start=True, stop=not diag)
                            if diag:
                                mm = nc.tensor.matmul(sT[p][:, hh, off:off + P], ident_b[:, :], mask_k[:, :], start=False, stop=True)
                        mm.then_inc(scores_ready, 1)

                    def values(unit, slot, a, b, first, last):
                        if first is not None:
                            pe.wait_ge(o_copied, first + 4)
                        pe.wait_ge(exp_done, unit.of(PAIRS, PAIRS + 2))
                        pe.wait_ge(v_staged, unit.of(1, 1))
                        for h in range(GROUP):
                            mm = nc.tensor.matmul(o_acc[32 * h:32 * h + 32, a:b], v_now[:, slot, kh(h), :], prob[:, slot, h, a:b],
                                                  start=first is not None, stop=True, skip_group_check=True)
                        if last:
                            mm.then_inc(pv_done, 1)

                    def maxima(k_slot, c, items, quarter):
                        todo = [(item, h) for item in items for h in range(GROUP)]
                        n = len(todo) // 4
                        for (unit, qb, sb, width, diag), h in todo[quarter * n:(quarter + 1) * n]:
                            max_tile(k_slot, unit, h, c, qb, sb, width, diag)

                    def key_block(k_slot, c, unit, block_of_keys, off, diag, before, items):
                        maxima(k_slot, c + 1, items, 0)
                        scores(k_slot, unit, c, block_of_keys, off, 0, diag)
                        maxima(k_slot, c + 1, items, 1)
                        if before is not None:
                            pv_unit, slot, pv_off, first = before
                            mid = CHUNK // 2 if pv_off < CHUNK // 2 else CHUNK
                            values(pv_unit, slot, pv_off, mid, first, mid == CHUNK)
                        maxima(k_slot, c + 1, items, 2)
                        scores(k_slot, unit, c, block_of_keys, off, 1, diag)
                        maxima(k_slot, c + 1, items, 3)
                        if before is not None and mid < CHUNK:
                            values(pv_unit, slot, mid, CHUNK, None, True)

                    def rows(n, next_unit):
                        pe.wait_ge(max_split, n + 1)
                        pe.wait_ge(exp_done, next_unit.of(PAIRS, 2))
                        for h in range(GROUP):
                            for q in range(TPC):
                                mm = nc.tensor.matmul(sT[h // 2][ROWS:ROWS_M, h % 2, q * P:(q + 1) * P], max_hl[:, h * TPC + q, :],
                                                      neg_ident_b[:, :], start=True, stop=True)
                        mm.then_inc(rows_ready, 1)

                    def turn_o(n):
                        pe.wait_ge(o_copied, n + 1 + 4)
                        pe.wait_ge(o_placed, n + 1)
                        for q in range(TPC):
                            tr = nc.tensor.transpose(o_tok[:, q, :], o_sb[:, q * P:(q + 1) * P], ident_f[:, :])
                        tr.then_inc(o_turned, 1)

                    pe.nop().then_inc(rows_ready, 1)
                    pe.nop().then_inc(pv_done, 2)
                    pe.nop().then_inc(o_turned, 1)
                    pe.wait_ge(ones_set, 1)
                    with pe.Fori(0, NGROUPS) as g:
                        pe.wait_ge(k_in, (g + 1) * 16 * len(K_PART))
                        pe.wait_ge(q_in, (g * NCH + 1) * 16 * n_qdma)
                        k_slot = pe.snap(g % 2 * KH)
                        supers, chunks = at_stage(pe, g, 0)
                        for qb in range(TPC):
                            for h in range(GROUP):
                                max_tile(k_slot, Blocks(supers, qb), h, 0, qb, 0, (qb + 1) * P, True)
                        rows(chunks, Blocks(supers, 0))
                        for c in range(NCH):
                            supers, chunks = at_stage(pe, g, c)
                            ahead = TPC * (c + 1)
                            pe.wait_ge(rows_a, chunks + 1)
                            pe.wait_ge(rows_v, chunks + 1)
                            if c < LAST:
                                pe.wait_ge(q_in, chunks * (16 * n_qdma) + 2 * 16 * n_qdma)
                            for i in range(TPC):
                                off = (TPC - 1 - i) * P
                                before = None if i == 0 else (Blocks(supers, i - 1), (i - 1) % 2, off + P, chunks if i == 1 else None)
                                items = []
                                if c < LAST:
                                    items = [(Blocks(supers, ahead + 2 * i), i, c + 1, (i + 1) * P, True),
                                             (Blocks(supers, ahead + 2 * i + 1), i, c, CHUNK, False)]
                                key_block(k_slot, c, Blocks(supers, i), c * TPC + TPC - 1 - i, off, True, before, items)
                                if i == 0 and c:
                                    turn_o(chunks - 1)
                            if c:
                                with pe.Fori(0, c) as sb:
                                    now = pe.snap(supers + sb)
                                    for j in range(TPC):
                                        items = [(Blocks(now, ahead + 2 * TPC + j), j, sb, CHUNK, False)] if c < LAST else []
                                        key_block(k_slot, c, Blocks(now, TPC + j), sb * TPC + j, 0, False,
                                                  (Blocks(now, TPC + j - 1), (j + 1) % 2, 0, None), items)
                            end = Blocks(supers, ahead - 1)
                            values(end, (TPC - 1) % 2, 0, CHUNK // 2, None, False)
                            values(end, (TPC - 1) % 2, CHUNK // 2, CHUNK, None, True)
                            if c < LAST:
                                rows(chunks + 1, Blocks(supers, ahead))
                        turn_o(chunks)

    def out_projection(name, A, w_dram, gain, base_dram, X, keep):
        with Space(name) as s:
            W = s.sb("W", [P, KD, D])
            As = s.sb("As", [P, TPC, D])
            aT = s.sb("aT", [P, KD, CHUNK])
            ps_t = s.ps("ps_t", [P, KD, CHUNK])
            ps_o = s.ps("ps_o", [P, TPC, D])
            w_in, loaded, staged, turned, aT_ready = s.sem("w_in"), s.sem("loaded"), s.sem("staged"), s.sem("turned"), s.sem("aT_ready")
            product, gained, added, stored = s.sem("product"), s.sem("gained"), s.sem("added"), s.sem("stored")
            gain_out = s.sb("gain_out", [P, TPC, D])
            with nc.Block() as block:

                @block.sync
                def _(sp):
                    sp.dma_start(W[:, :, :], w_dram.rearrange("(k p) n -> p k n", p=P)).then_inc(w_in, 16)
                    with sp.Fori(0, NCH) as c:
                        sp.dma_start(X[:, tiles(c), :], by_tile(base_dram)[:, tiles(c), :]).then_inc(loaded, 16)
                        wait_apart(sp, loaded, c * 16 + 16)
                    if keep is not None:
                        with sp.Fori(0, NCH) as c:
                            wait_apart(sp, added, c + 2)
                            sp.dma_start(by_tile(keep)[:, tiles(c), :], X[:, tiles(c), :]).then_inc(stored, 16)
                        sp.wait_ge(stored, 16 * NCH)

                @block.gpsimd
                def _(pool):
                    with pool.Fori(0, NCH) as c:
                        wait_apart(pool, turned, c + 1)
                        nc.gpsimd.tensor_copy(As[:, :, :], A[:, tiles(c), :]).then_inc(staged, 1)

                @block.scalar
                def _(act):
                    with act.Fori(0, NCH) as c:
                        act.wait_ge(turned, c + 2)
                        act.wait_ge(product, c + 1)
                        for k in range(KD):
                            nc.scalar.copy(aT[:, k, :], ps_t[:, k, :]).then_inc(aT_ready, 1)

                @block.vector
                def _(dve):
                    dve.nop().then_inc(added, 1)
                    with dve.Fori(0, NCH) as c:
                        dve.wait_ge(product, c + 2)
                        dve.wait_ge(added, c + 1)
                        if gain is None:
                            dve.wait_ge(loaded, c * 16 + 16)
                            nc.vector.tensor_tensor(X[:, tiles(c), :], ps_o[:, :, :], X[:, tiles(c), :], ALU.add).then_inc(added, 1)
                        else:
                            nc.vector.tensor_tensor(gain_out[:, :, :], ps_o[:, :, :], row_bcast(gain, TPC), ALU.mult).then_inc(gained, 1)
                            dve.wait_ge(gained, c + 1)
                            dve.wait_ge(loaded, c * 16 + 16)
                            nc.vector.tensor_tensor(X[:, tiles(c), :], gain_out[:, :, :], X[:, tiles(c), :], ALU.add).then_inc(added, 1)

                @block.tensor
                def _(pe):
                    pe.nop().then_inc(turned, 1)
                    pe.nop().then_inc(product, 1)
                    pe.wait_ge(w_in, 16)
                    with pe.Fori(0, NCH) as c:
                        pe.wait_ge(staged, c + 1)
                        for k in range(KD):
                            for j in range(TPC):
                                tr = nc.tensor.transpose(ps_t[:, k, j * P:(j + 1) * P], As[:, j, k * P:(k + 1) * P], ident_f[:, :])
                        tr.then_inc(turned, 1)
                        pe.wait_ge(aT_ready, c * KD + KD)
                        pe.wait_ge(added, c + 1)
                        for j in range(TPC):
                            for k in range(KD):
                                mm = nc.tensor.matmul(ps_o[:, j, :], aT[:, k, j * P:(j + 1) * P], W[:, k, :], start=(k == 0), stop=(k == KD - 1))
                        mm.then_inc(product, 1)

    def router(name, Y, comb, lower_dram):
        with Space(name) as s:
            Wg = s.sb("Wg", [P, KD, E])
            lower_t = s.sb("lower_t", [P, E * E])
            Ys = s.sb("Ys", [P, TPC, D])
            ltok = s.sb("ltok", [E, CHUNK])
            top = s.sb("top", [P, TPC])
            shifted, probs, ex, pm = (s.sb(n, [P, TPC, E]) for n in ("shifted", "probs", "ex", "pm"))
            total, rtotal, psum_, rsum = (s.sb(n, [P, TPC]) for n in ("total", "rtotal", "psum_", "rsum"))
            above, equal, ahead = (s.sb(n, [P, TPC, E, E]) for n in ("above", "equal", "ahead"))
            rank = s.sb("rank", [P, TPC, E])
            ps_t = s.ps("ps_t", [P, KD, CHUNK])
            ps_l = s.ps("ps_l", [E, CHUNK])
            ps_g = s.ps("ps_g", [P, TPC, E])
            w_in, staged, turned, yT_ready = s.sem("w_in"), s.sem("staged"), s.sem("turned"), s.sem("yT_ready")
            logits, logits_out, logits_tok, exped, step = s.sem("logits"), s.sem("logits_out"), s.sem("logits_tok"), s.sem("exped"), s.sem("step")
            logits_tok_used = s.sem("logits_tok_used")
            STEPS = 13
            with nc.Block() as block:

                @block.sync
                def _(sp):
                    sp.dma_start(Wg[:, :, :], gate.rearrange("(k p) e -> p k e", p=P)).then_inc(w_in, 16)
                    sp.dma_start(lower_t[:, :], lower_dram).then_inc(w_in, 16)

                @block.gpsimd
                def _(pool):
                    with pool.Fori(0, NCH) as c:
                        wait_apart(pool, turned, c + 1)
                        nc.gpsimd.tensor_copy(Ys[:, :, :], Y[:, tiles(c), :]).then_inc(staged, 1)

                @block.scalar
                def _(act):
                    with act.Fori(0, NCH) as c:
                        act.wait_ge(turned, c + 2)
                        for k in range(KD):
                            nc.scalar.copy(feature_major(Y, c, k), ps_t[:, k, :]).then_inc(yT_ready, 1)
                        act.wait_ge(logits, c + 1)
                        nc.scalar.copy(ltok[:, :], ps_l[:, :]).then_inc(logits_out, 1)
                        act.wait_ge(step, c * STEPS + 2)
                        nc.scalar.activation(ex[:, :, :], shifted[:, :, :], ACT.Exp).then_inc(exped, 1)

                @block.vector
                def _(dve):
                    dve.nop().then_inc(logits_tok_used, 1)
                    dve.wait_ge(w_in, 32)
                    with dve.Fori(0, NCH) as c:
                        def after(n):
                            dve.wait_ge(step, c * STEPS + n)

                        dve.wait_ge(logits_tok, c + 1)
                        nc.vector.reduce_max(top[:, :], ps_g[:, :, :], AX.X).then_inc(step, 1)
                        after(1)
                        nc.vector.tensor_tensor(shifted[:, :, :], ps_g[:, :, :], col_bcast(top[:, :], E), ALU.subtract).then_inc(step, 1)
                        dve.wait_ge(exped, c + 1)
                        nc.vector.reduce_sum(total[:, :], ex[:, :, :], AX.X).then_inc(step, 1)
                        after(3)
                        nc.vector.reciprocal(rtotal[:, :], total[:, :]).then_inc(step, 1)
                        after(4)
                        nc.vector.tensor_tensor(probs[:, :, :], ex[:, :, :], col_bcast(rtotal[:, :], E), ALU.mult).then_inc(step, 1)
                        after(5)
                        mine = probs[:, :, :].unsqueeze(3).to_broadcast([P, TPC, E, E])
                        other = probs[:, :, :].unsqueeze(2).to_broadcast([P, TPC, E, E])
                        nc.vector.tensor_tensor(above[:, :, :, :], other, mine, ALU.is_gt).then_inc(step, 1)
                        nc.vector.tensor_tensor(equal[:, :, :, :], other, mine, ALU.is_equal).then_inc(step, 1)
                        after(7)
                        nc.vector.tensor_tensor(ahead[:, :, :, :].rearrange("p q a b -> p q (a b)"), equal[:, :, :, :].rearrange("p q a b -> p q (a b)"),
                                                row_bcast(lower_t[:, :], TPC), ALU.mult).then_inc(step, 1)
                        after(8)
                        nc.vector.tensor_tensor(above[:, :, :, :], above[:, :, :, :], ahead[:, :, :, :], ALU.add).then_inc(step, 1)
                        after(9)
                        nc.vector.reduce_sum(rank[:, :, :], above[:, :, :, :], AX.X).then_inc(step, 1)
                        after(10)
                        nc.vector.scalar_tensor_tensor(out=pm[:, :, :], in0=rank[:, :, :], scalar=2.0, in1=probs[:, :, :],
                                                       op0=ALU.is_lt, op1=ALU.mult).then_inc(step, 1)
                        after(11)
                        nc.vector.reduce_sum(psum_[:, :], pm[:, :, :], AX.X).then_inc(step, 1)
                        after(12)
                        nc.vector.reciprocal(rsum[:, :], psum_[:, :]).then_inc(step, 1)
                        after(13)
                        nc.vector.tensor_tensor(comb[:, tiles(c), :], pm[:, :, :], col_bcast(rsum[:, :], E), ALU.mult).then_inc(logits_tok_used, 1)

                @block.tensor
                def _(pe):
                    pe.nop().then_inc(turned, 1)
                    pe.wait_ge(w_in, 32)
                    with pe.Fori(0, NCH) as c:
                        pe.wait_ge(staged, c + 1)
                        for k in range(KD):
                            for j in range(TPC):
                                tr = nc.tensor.transpose(ps_t[:, k, j * P:(j + 1) * P], Ys[:, j, k * P:(k + 1) * P], ident_f[:, :])
                        tr.then_inc(turned, 1)
                        pe.wait_ge(yT_ready, c * KD + KD)
                        for k in range(KD):
                            mm = nc.tensor.matmul(ps_l[:, :], Wg[:, k, :], feature_major(Y, c, k), start=(k == 0), stop=(k == KD - 1))
                        mm.then_inc(logits, 1)
                        wait_apart(pe, logits_out, c + 1)
                        pe.wait_ge(logits_tok_used, c + 1)
                        for j in range(TPC):
                            tr = nc.tensor.transpose(ps_g[:, j, :], ltok[:, j * P:(j + 1) * P], ident_f[0:E, 0:E])
                        tr.then_inc(logits_tok, 1)

    def experts(name, YT, comb, Fx, gain):
        with Space(name) as s:
            W1 = s.sb("W1", [P, E, KD, HID])
            W3 = s.sb("W3", [P, E, KD, HID])
            W2 = s.sb("W2", [P, E, HB, D])
            x1 = s.sb("x1", [P, TPC, D])
            gated = s.sb("gated", [P, 2, CHUNK])
            hT = s.sb("hT", [P, 2, HB, CHUNK])
            acc = s.sb("acc", [P, TPC, D])
            ps_1 = [s.ps(f"ps_1{n}", [P, CHUNK]) for n in range(2)]
            ps_3 = [s.ps(f"ps_3{n}", [P, CHUNK]) for n in range(2)]
            ps_y = [s.ps(f"ps_y{n}", [P, TPC, D]) for n in range(2)]
            w_in = [s.sem(f"w_in{e}") for e in range(E)]
            x1_in, stored = s.sem("x1_in"), s.sem("stored")
            up_ready, silu_done, h_ready = s.sem("up_ready"), s.sem("silu_done"), s.sem("h_ready")
            down_ready, down_taken, gained, final = s.sem("down_ready"), s.sem("down_taken"), s.sem("gained"), s.sem("final")
            with nc.Block() as block:

                @block.sync
                def _(sp):
                    for e in range(E):
                        sp.dma_start(W1[:, e, :, :], w1[e].rearrange("(k p) n -> p k n", p=P)).then_inc(w_in[e], 16)
                        sp.dma_start(W3[:, e, :, :], w3[e].rearrange("(k p) n -> p k n", p=P)).then_inc(w_in[e], 16)
                        sp.dma_start(W2[:, e, :, :], w2[e].rearrange("(k p) n -> p k n", p=P)).then_inc(w_in[e], 16)
                    sp.nop().then_inc(stored, 16)
                    with sp.Fori(0, NCH) as c:
                        wait_apart(sp, final, c + 1)
                        sp.dma_start(x1[:, :, :], by_tile(x1_dram)[:, tiles(c), :]).then_inc(x1_in, 16)
                        wait_apart(sp, final, c + 2)
                        sp.dma_start(by_tile(out)[:, tiles(c), :], acc[:, :, :]).then_inc(stored, 16)
                    sp.wait_ge(stored, 16 * NCH + 16)

                @block.scalar
                def _(act):
                    act.nop().then_inc(silu_done, 2)
                    with act.Fori(0, NCH) as c:
                        for u in range(E * HB):
                            U = c * (E * HB) + u
                            act.wait_ge(up_ready, U + 1)
                            act.wait_ge(h_ready, U + 1)
                            nc.scalar.activation(gated[:, u % 2, :], ps_1[u % 2][:, :], ACT.Silu).then_inc(silu_done, 1)

                @block.vector
                def _(dve):
                    def weigh(c, e):
                        n = c * E + e
                        dve.wait_ge(down_ready, n + 3)
                        for j in range(TPC):
                            i = bass.ds(c * TPC + j, 1)
                            f = Fx[:, i, :].rearrange("p a f -> p (a f)")
                            w = comb[:, i, e:e + 1].rearrange("p a f -> p (a f)")
                            dve.wait_ge(down_taken, (n + 1) * TPC + j + 1)
                            op = nc.vector.scalar_tensor_tensor(out=f, in0=ps_y[e % 2][:, j, :], scalar=w, in1=f, op0=ALU.mult, op1=ALU.add)
                            op.then_inc(down_taken, 1)

                    dve.nop().then_inc(h_ready, 2)
                    dve.nop().then_inc(down_taken, 2 * TPC)
                    dve.nop().then_inc(final, 1)
                    with dve.Fori(0, NCH) as c:
                        for e in range(E):
                            for hb in range(HB):
                                u = e * HB + hb
                                U = c * (E * HB) + u
                                dve.wait_ge(silu_done, U + 3)
                                dve.wait_ge(down_ready, c * E + e + 1)
                                nc.vector.tensor_tensor(hT[:, e % 2, hb, :], gated[:, u % 2, :], ps_3[u % 2][:, :], ALU.mult).then_inc(h_ready, 1)
                            if e:
                                weigh(c, e - 1)
                        weigh(c, E - 1)
                        dve.wait_ge(down_taken, (c + 1) * E * TPC + 2 * TPC)
                        dve.wait_ge(stored, c * 16 + 16)
                        nc.vector.tensor_tensor(acc[:, :, :], Fx[:, tiles(c), :], row_bcast(gain, TPC), ALU.mult).then_inc(gained, 1)
                        dve.wait_ge(gained, c + 1)
                        dve.wait_ge(x1_in, c * 16 + 16)
                        nc.vector.tensor_tensor(acc[:, :, :], acc[:, :, :], x1[:, :, :], ALU.add).then_inc(final, 1)

                @block.tensor
                def _(pe):
                    def down(c, e):
                        n = c * E + e
                        pe.wait_ge(h_ready, (n + 1) * HB + 2)
                        pe.wait_ge(down_taken, (n + 1) * TPC)
                        for j in range(TPC):
                            for hb in range(HB):
                                mm = nc.tensor.matmul(ps_y[e % 2][:, j, :], hT[:, e % 2, hb, j * P:(j + 1) * P], W2[:, e, hb, :],
                                                      start=(hb == 0), stop=(hb == HB - 1))
                        mm.then_inc(down_ready, 1)

                    pe.nop().then_inc(down_ready, 2)
                    for e in range(E):
                        pe.wait_ge(w_in[e], 48)
                    with pe.Fori(0, NCH) as c:
                        for e in range(E):
                            for hb in range(HB):
                                u = e * HB + hb
                                U = c * (E * HB) + u
                                pe.wait_ge(h_ready, U + 1)
                                for bank, W in ((ps_1, W1), (ps_3, W3)):
                                    for k in range(KD):
                                        mm = nc.tensor.matmul(bank[u % 2][:, :], W[:, e, k, hb * P:(hb + 1) * P], feature_major(YT, c, k),
                                                              start=(k == 0), stop=(k == KD - 1))
                                mm.then_inc(up_ready, 1)
                                if hb == 0 and e:
                                    down(c, e - 1)
                        down(c, E - 1)

    stack = ExitStack()

    def keep_sb(where, name, shape, dt=F32):
        return where.enter_context(nc.sbuf_tensor(name, shape, dt))

    with stack:
        begun = stack.enter_context(nc.semaphore("begun"))
        ident_f = keep_sb(stack, "ident_f", [P, P])
        ident_b = keep_sb(stack, "ident_b", [P, P], BF16)
        neg_ident_b = keep_sb(stack, "neg_ident_b", [P, P], BF16)
        mask_k = keep_sb(stack, "mask_k", [P, P], BF16)
        mask_q = keep_sb(stack, "mask_q", [P, P], BF16)
        mod = keep_sb(stack, "mod", [P, 6, D])
        gains = keep_sb(stack, "gains", [P, 2, D])
        neg_half = keep_sb(stack, "neg_half", [P, TPC])
        setup(ident_f, ident_b, neg_ident_b, mask_k, mask_q, mod, gains, neg_half)

        tok_a = keep_sb(stack, "tok_a", [P, NT, D])
        tok_b = keep_sb(stack, "tok_b", [P, NT, D])
        shift_a, scale_a, gain_a, shift_b, scale_b, gain_b = (mod[:, v, :] for v in range(6))

        norms("ln1", tok_a, x, shift_a, scale_a, None, None, None, neg_half)
        projections("qkv1", tok_a, wqkv[0], rope[0], tok_b, KVH[0])
        attention("att1", tok_b, tok_a, KVH[0])
        out_projection("out1", tok_a, wo[0], gain_a, x, tok_b, x1_dram)
        norms("ln2", tok_b, None, shift_b, scale_b, gains[:, 0, :], tok_a, h2_dram, neg_half)
        projections("qkv2", tok_a, wqkv[1], rope[1], tok_b, KVH[1])
        attention("att2", tok_b, tok_a, KVH[1])
        out_projection("out2", tok_a, wo[1], None, h2_dram, tok_b, None)
        norms("rms2", tok_b, None, None, None, gains[:, 1, :], tok_a, None, neg_half)
        with ExitStack() as last:
            comb = keep_sb(last, "comb", [P, NT, E])
            router("router", tok_a, comb, lower)
            experts("moe", tok_a, comb, tok_b, gain_b)


def shape_constants(T, D):
    import numpy as np

    f32 = np.float32
    pos = np.arange(T, dtype=f32)
    half = np.arange(DH // 2, dtype=f32)
    theta = (f32(10000.0) ** (f32(-2.0) * half / f32(DH))).astype(f32)
    inv_freq = (f32(1.0) / f32(10000.0) ** (f32(2.0) * half / f32(DH))).astype(f32)
    rows = np.arange(P) % DH
    rope = np.zeros((2, 2, P, T), f32)
    for n, (freq, of_row, sign) in enumerate((
        (theta, rows // 2, np.where(rows % 2 == 0, -1.0, 1.0)),
        (inv_freq, rows % (DH // 2), np.where(rows < DH // 2, -1.0, 1.0)),
    )):
        angle = (pos[:, None] * freq[None, :]).astype(f32)
        rope[n, 0] = np.cos(angle).astype(f32).T[of_row]
        rope[n, 1] = np.sin(angle).astype(f32).T[of_row] * sign.astype(f32)[:, None]
    ident = np.eye(P, dtype=f32)
    a, b = np.arange(P)[:, None], np.arange(P)[None, :]
    masks = np.stack([np.where(a > b, HIDDEN_NEG, 0.0), np.where(b > a, HIDDEN_NEG, 0.0)]).astype(f32)
    return rope, ident, masks


def kernel(L0_attn_X, L0_attn_W_q, L0_attn_W_k, L0_attn_W_v, L0_attn_W_o, L0_ffn_g1, L0_ffn_g2, L0_ffn_wq, L0_ffn_wk,
           L0_ffn_wv, L0_ffn_wo, L0_ffn_gate, L0_ffn_w1, L0_ffn_w2, L0_ffn_w3, L0_c, L0_wmod):
    import numpy as np
    import concourse.bacc as bacc
    from concourse.bass_utils import run_bass_kernel_spmd as run

    X = np.asarray(L0_attn_X)
    _, T, D = X.shape
    E = np.asarray(L0_ffn_gate).shape[1]
    rope, ident, masks = shape_constants(T, D)
    pairs = np.arange(D) ^ 1
    halves = np.arange(D) ^ (DH // 2)
    q1, k1, v1 = (np.asarray(w).T for w in (L0_attn_W_q, L0_attn_W_k, L0_attn_W_v))
    q2, k2, v2 = (np.asarray(w) for w in (L0_ffn_wq, L0_ffn_wk, L0_ffn_wv))
    nk = k2.shape[1]
    arrays = {
        "x": X[0],
        "wqkv_1": np.concatenate([q1, k1, q1[:, pairs], k1[:, pairs], v1], axis=1),
        "wqkv_2": np.concatenate([q2, k2, q2[:, halves], k2[:, halves[:nk]], v2], axis=1),
        "rope": rope,
        "wo_1": np.asarray(L0_attn_W_o).T,
        "wo_2": np.asarray(L0_ffn_wo),
        "g12": np.concatenate([np.asarray(L0_ffn_g1), np.asarray(L0_ffn_g2)])[None, :],
        "wmod": np.asarray(L0_wmod),
        "c_col": np.asarray(L0_c)[0].reshape(D // P, P).T,
        "gate": np.asarray(L0_ffn_gate),
        "w1": np.asarray(L0_ffn_w1),
        "w2": np.asarray(L0_ffn_w2),
        "w3": np.asarray(L0_ffn_w3),
        "ident": ident,
        "masks": masks,
        "lower": np.ascontiguousarray(np.broadcast_to(np.tril(np.ones((E, E), np.float32), -1).reshape(1, E * E), (P, E * E))),
    }
    arrays = {n: np.ascontiguousarray(a) for n, a in arrays.items()}
    nc = bacc.Bacc("TRN2", target_bir_lowering=False, num_devices=1)
    t = {n: nc.dram_tensor(n, a.shape, mybir.dt.from_np(a.dtype), kind="ExternalInput").ap() for n, a in arrays.items()}
    out = nc.dram_tensor("out", (T, D), F32, kind="ExternalOutput").ap()
    adaln_program(nc, t["x"], (t["wqkv_1"], t["wqkv_2"]), t["rope"], (t["wo_1"], t["wo_2"]), t["g12"], t["wmod"], t["c_col"],
                  t["gate"], t["w1"], t["w2"], t["w3"], t["ident"], t["masks"], t["lower"], out)
    r = run(nc, [arrays], core_ids=[0])
    return r.results[0]["out"].reshape(1, T, D)
```

```python
from contextlib import ExitStack

import concourse.bass as bass
from concourse import mybir

P = 128
F32 = mybir.dt.float32
BF16 = mybir.dt.bfloat16
ACT = mybir.ActivationFunctionType
ALU = mybir.AluOpType
AX = mybir.AxisListType

HEADS = 16
DH = 16
GROUP = 4
PARTS = 3
Q_PART = (0, 0, 0, 1, 1, 2)
K_PART = (0, 1, 2, 0, 1, 0)
ROWS = len(Q_PART) * DH
ROWS_M = ROWS + 2
CHUNK = 512
LN_EPS = 1e-5
RMS_EPS = 1.1920928955078125e-07
PAIR_OF_ONES = 1.0 + 0x3F80 / 2.0 ** 23
HIDDEN_NEG = -1e30


class Blocks:

    def __init__(self, supers, more):
        self.supers, self.more = supers, more

    def of(self, each, plus):
        return self.supers * (CHUNK // P * each) + (self.more * each + plus)


def adaln_program(nc, x, wqkv, rope, wo, g12, wmod, c_col, gate, w1, w2, w3, ident, masks, lower, out):
    T, D = x.shape
    NT = T // P
    NCH = T // CHUNK
    TPC = CHUNK // P
    KD = D // P
    E = gate.shape[1]
    HID = w1.shape[2]
    HB = HID // P
    NGROUPS = HEADS // GROUP
    KVH = (HEADS, NGROUPS)

    x1_dram = nc.dram_tensor("x1_dram", (T, D), F32, kind="Internal").ap()
    h2_dram = nc.dram_tensor("h2_dram", (T, D), F32, kind="Internal").ap()
    q_dram = nc.dram_tensor("q_dram", (PARTS, D, T), BF16, kind="Internal").ap()
    k_dram = nc.dram_tensor("k_dram", (PARTS, D, T), BF16, kind="Internal").ap()

    def wait_apart(eng, sem, value):
        if not isinstance(value, int):
            value = eng.to_reg(value)
            eng.wait_ge(begun, 1)
        eng.wait_ge(sem, value)

    def by_tile(dram):
        return dram.rearrange("(i p) f -> p i f", p=P)

    def tiles(c):
        return bass.ds(c * TPC, TPC)

    def cols(c):
        return bass.ds(c * CHUNK, CHUNK)

    def feature_major(a, c, k):
        return a[:, bass.ds(c * TPC + k * (TPC // KD), TPC // KD), :].rearrange("p a f -> p (a f)")

    def row_bcast(row, n):
        return row.unsqueeze(1).to_broadcast([P, n, row.shape[1]])

    def col_bcast(a, w):
        return a.unsqueeze(2).to_broadcast([P, a.shape[1], w])

    class Space:

        def __init__(self, name):
            self.name = name
            self.sems = []

        def __enter__(self):
            self.stack = ExitStack()
            return self

        def __exit__(self, *a):
            if a[0] is None:
                with nc.Block() as block:

                    @block.sync
                    def _(sp):
                        for handle in self.sems:
                            sp.sem_clear(handle)

            self.stack.close()

        def sb(self, name, shape, dt=F32):
            return self.stack.enter_context(nc.sbuf_tensor(f"{self.name}_{name}", shape, dt))

        def ps(self, name, shape, dt=F32):
            return self.stack.enter_context(nc.psum_tensor(f"{self.name}_{name}", shape, dt))

        def sem(self, name):
            self.sems.append(self.stack.enter_context(nc.semaphore(f"{self.name}_{name}")))
            return self.sems[-1]

    def setup(ident_f, ident_b, neg_ident_b, mask_k, mask_q, mod, gains, neg_half):
        with Space("set") as s:
            msk = s.sb("msk", [P, 2, P])
            cc = s.sb("cc", [P, KD])
            sc = s.sb("sc", [P, KD])
            scb = s.sb("scb", [P, KD, P])
            ones = s.sb("ones", [P, P])
            wm = s.sb("wm", [P, KD, 6 * D])
            grow = s.sb("grow", [1, 2 * D])
            raw = s.sb("raw", [P, 6 * D])
            sign = s.sb("sign", [P, 2, D])
            pm = [s.ps(f"pm{n}", [P, CHUNK]) for n in range(4)]
            loaded, ones_set, silu_done = s.sem("loaded"), s.sem("ones_set"), s.sem("silu_done")
            bc_done, mod_done, raw_done, dve = s.sem("bc_done"), s.sem("mod_done"), s.sem("raw_done"), s.sem("dve")
            ident_in = s.sem("ident_in")
            with nc.Block() as block:

                @block.sync
                def _(sp):
                    sp.nop().then_inc(begun, 1)
                    sp.dma_start(ident_f[:, :], ident).then_inc(ident_in, 16)
                    sp.dma_start(msk[:, :, :], masks.rearrange("a p n -> p a n")).then_inc(ident_in, 16)
                    sp.dma_start(cc[:, :], c_col).then_inc(loaded, 16)
                    sp.dma_start(grow[:, :], g12).then_inc(loaded, 16)
                    sp.dma_start(wm[:, :, :], wmod.rearrange("(k p) n -> p k n", p=P)).then_inc(loaded, 16)
                    sp.wait_ge(loaded, 48)

                @block.scalar
                def _(act):
                    act.wait_ge(loaded, 48)
                    nc.scalar.activation(sc[:, :], cc[:, :], ACT.Silu).then_inc(silu_done, 1)
                    for n in range(4):
                        act.wait_ge(mod_done, n + 1)
                        if n < 3:
                            nc.scalar.copy(raw[:, cols(n)], pm[n][:, :]).then_inc(raw_done, 1)
                        else:
                            nc.scalar.copy(gains[:, :, :].rearrange("p a f -> p (a f)"), pm[n][:, :]).then_inc(raw_done, 1)

                @block.vector
                def _(dve_e):
                    nc.vector.memset(ones[:, :], 1.0).then_inc(ones_set, 1)
                    nc.vector.memset(neg_half[:, :], -0.5).then_inc(ones_set, 1)
                    dve_e.wait_ge(ones_set, 1)
                    dve_e.wait_ge(silu_done, 1)
                    for k in range(KD):
                        nc.vector.tensor_scalar(scb[:, k, :], ones[:, :], sc[:, k:k + 1], None, ALU.mult).then_inc(bc_done, 1)
                    dve_e.wait_ge(ident_in, 32)
                    nc.vector.tensor_copy(ident_b[:, :], ident_f[:, :])
                    nc.vector.tensor_scalar(neg_ident_b[:, :], ident_f[:, :], -1.0, None, ALU.mult)
                    nc.vector.tensor_copy(mask_k[:, :], msk[:, 0, :])
                    nc.vector.tensor_copy(mask_q[:, :], msk[:, 1, :])
                    dve_e.wait_ge(raw_done, 4)
                    r = raw[:, :].rearrange("p (v f) -> p v f", v=6)
                    for v in (0, 3):
                        nc.vector.tensor_copy(mod[:, v, :], r[:, v, :])
                    for v in (1, 4):
                        nc.vector.tensor_scalar(mod[:, v, :], r[:, v, :], 1.0, None, ALU.add)
                    for n, v in enumerate((2, 5)):
                        nc.vector.tensor_scalar(sign[:, n, :], r[:, v, :], 0.0, 2.0, ALU.is_ge, ALU.mult).then_inc(dve, 1)
                        dve_e.wait_ge(dve, 4 * n + 1)
                        nc.vector.tensor_scalar(sign[:, n, :], sign[:, n, :], -1.0, None, ALU.add).then_inc(dve, 1)
                        nc.vector.scalar_tensor_tensor(out=mod[:, v, :], in0=r[:, v, :], scalar=-1.0, in1=r[:, v, :],
                                                       op0=ALU.mult, op1=ALU.max).then_inc(dve, 1)
                        dve_e.wait_ge(dve, 4 * n + 3)
                        nc.vector.scalar_tensor_tensor(out=mod[:, v, :], in0=mod[:, v, :], scalar=0.25, in1=sign[:, n, :],
                                                       op0=ALU.max, op1=ALU.mult).then_inc(dve, 1)
                    dve_e.wait_ge(dve, 8)

                @block.tensor
                def _(pe):
                    pe.wait_ge(bc_done, KD)
                    for n in range(3):
                        for k in range(KD):
                            mm = nc.tensor.matmul(pm[n][:, :], scb[:, k, :], wm[:, k, cols(n)], start=(k == 0), stop=(k == KD - 1))
                        mm.then_inc(mod_done, 1)
                    nc.tensor.matmul(pm[3][:, :], ones[0:1, :], grow[:, :], start=True, stop=True).then_inc(mod_done, 1)

    def norms(name, X, src, shift, scale, rms_gain, Y, keep, neg_half):
        with Space(name) as s:
            st = s.sb("st", [P, TPC, 6])
            mv = s.sb("mv", [P, TPC, 2])
            var = s.sb("var", [P, TPC])
            rstd = s.sb("rstd", [P, TPC])
            sq = s.sb("sq", [P, 2, D])
            ssq = s.sb("ssq", [P, TPC])
            ms = s.sb("ms", [P, TPC])
            rrms = s.sb("rrms", [P, TPC])
            loaded = s.sem("loaded")
            stats_done, aggr_done, var_done, rstd_done = s.sem("stats_done"), s.sem("aggr_done"), s.sem("var_done"), s.sem("rstd_done")
            centred, scaled, shifted = s.sem("centred"), s.sem("scaled"), s.sem("shifted")
            squared, ms_done, rrms_done, rms_out, stored = s.sem("squared"), s.sem("ms_done"), s.sem("rrms_done"), s.sem("rms_out"), s.sem("stored")
            ln = scale is not None
            with nc.Block() as block:

                @block.sync
                def _(sp):
                    if src is not None:
                        with sp.Fori(0, NCH) as c:
                            sp.dma_start(X[:, tiles(c), :], by_tile(src)[:, tiles(c), :]).then_inc(loaded, 16)
                            wait_apart(sp, loaded, c * 16 + 16)
                    if keep is not None:
                        with sp.Fori(0, NCH) as c:
                            wait_apart(sp, shifted, c + 1)
                            sp.dma_start(by_tile(keep)[:, tiles(c), :], X[:, tiles(c), :]).then_inc(stored, 16)
                            wait_apart(sp, stored, c * 16 + 16)

                @block.vector
                def _(dve):
                    if rms_gain is not None:
                        dve.nop().then_inc(rms_out, TPC)
                    with dve.Fori(0, NCH) as c:
                        if ln:
                            if src is not None:
                                dve.wait_ge(loaded, c * 16 + 16)
                            for j in range(TPC):
                                nc.vector.bn_stats(st[:, j, :], X[:, bass.ds(c * TPC + j, 1), :].rearrange("p a f -> p (a f)")).then_inc(stats_done, 1)
                            for j in range(TPC):
                                wait_apart(dve, stats_done, c * TPC + j + 1)
                                nc.vector.bn_aggr(mv[:, j, :], st[:, j, :]).then_inc(aggr_done, 1)
                            dve.wait_ge(rstd_done, c + 1)
                            for j in range(TPC):
                                xt = X[:, bass.ds(c * TPC + j, 1), :].rearrange("p a f -> p (a f)")
                                nc.vector.tensor_scalar(xt, xt, mv[:, j, 0:1], rstd[:, j:j + 1], ALU.subtract, ALU.mult).then_inc(centred, 1)
                            dve.wait_ge(centred, c * TPC + TPC)
                            nc.vector.tensor_tensor(X[:, tiles(c), :], X[:, tiles(c), :], row_bcast(scale, TPC), ALU.mult).then_inc(scaled, 1)
                        if rms_gain is not None:
                            dve.wait_ge(rrms_done, c + 1)
                            for j in range(TPC):
                                i = bass.ds(c * TPC + j, 1)
                                nc.vector.scalar_tensor_tensor(
                                    out=Y[:, i, :].rearrange("p a f -> p (a f)"), in0=X[:, i, :].rearrange("p a f -> p (a f)"),
                                    scalar=rrms[:, j:j + 1], in1=rms_gain, op0=ALU.mult, op1=ALU.mult).then_inc(rms_out, 1)

                @block.gpsimd
                def _(pool):
                    if rms_gain is not None:
                        pool.nop().then_inc(ms_done, 1)
                    with pool.Fori(0, NCH) as c:
                        if ln:
                            wait_apart(pool, aggr_done, c * TPC + TPC)
                            nc.gpsimd.tensor_scalar(var[:, :], mv[:, :, 1], LN_EPS, None, ALU.add).then_inc(var_done, 1)
                            pool.wait_ge(var_done, c + 1)
                            nc.gpsimd.tensor_tensor(rstd[:, :], var[:, :], neg_half[:, 0:TPC], ALU.pow).then_inc(rstd_done, 1)
                            pool.wait_ge(scaled, c + 1)
                            nc.gpsimd.tensor_tensor(X[:, tiles(c), :], X[:, tiles(c), :], row_bcast(shift, TPC), ALU.add).then_inc(shifted, 1)
                        if rms_gain is not None:
                            wait_apart(pool, squared, c * TPC + TPC + 2)
                            wait_apart(pool, rms_out, c * TPC + TPC)
                            nc.gpsimd.tensor_scalar(ms[:, :], ssq[:, :], 1.0 / D, RMS_EPS, ALU.mult, ALU.add).then_inc(ms_done, 1)
                            pool.wait_ge(ms_done, c + 2)
                            nc.gpsimd.tensor_tensor(rrms[:, :], ms[:, :], neg_half[:, 0:TPC], ALU.pow).then_inc(rrms_done, 1)

                if rms_gain is not None:

                    @block.scalar
                    def _(act):
                        act.nop().then_inc(squared, 2)
                        with act.Fori(0, NCH) as c:
                            if ln:
                                act.wait_ge(shifted, c + 1)
                            act.wait_ge(ms_done, c + 1)
                            for j in range(TPC):
                                act.wait_ge(squared, c * TPC + j + 1)
                                nc.scalar.activation(sq[:, j % 2, :], X[:, bass.ds(c * TPC + j, 1), :].rearrange("p a f -> p (a f)"),
                                                     ACT.Square, accum_out=ssq[:, j:j + 1]).then_inc(squared, 1)


    def projections(name, H, w_dram, rope_dram, V, kv_heads):
        KV = kv_heads * DH
        q_units = [("q", n, P) for n in range(KD)]
        k_units = [("k", n, min(KV, P)) for n in range(max(1, KV // P))]
        rope_units = q_units + k_units
        NV, VW = max(1, KV // P), min(KV, P)
        NR = len(rope_units)
        U = NV + NR
        assert U % 2 == 0
        off_k, off_qs, off_ks, off_v = D, D + KV, 2 * D + KV, 2 * D + 2 * KV
        with Space(name) as s:
            W = s.sb("W", [P, KD, 2 * D + 3 * KV])
            cos, sin = s.sb("cos", [P, T]), s.sb("sin", [P, T])
            Hs = s.sb("Hs", [P, TPC, D])
            hT = s.sb("hT", [P, KD, CHUNK])
            vT = s.sb("vT", [P, NV, CHUNK])
            direct, crossed = s.sb("direct", [P, 2, CHUNK]), s.sb("crossed", [P, 2, CHUNK])
            turned, rest = s.sb("turned", [P, 2, CHUNK]), s.sb("rest", [P, 2, CHUNK])
            parts = s.sb("parts", [P, NR, PARTS, CHUNK], BF16)
            ps_t = s.ps("ps_t", [P, KD, CHUNK])
            ps_a = [s.ps(f"ps_a{n}", [P, CHUNK]) for n in range(2)]
            ps_b = [s.ps(f"ps_b{n}", [P, CHUNK]) for n in range(2)]
            ps_v = s.ps("ps_v", [P, TPC, D])
            w_in, tab_in = s.sem("w_in"), s.sem("tab_in")
            staged, h_turned, hT_ready = s.sem("staged"), s.sem("h_turned"), s.sem("hT_ready")
            unit_ready, v_evac, rope_taken = s.sem("unit_ready"), s.sem("v_evac"), s.sem("rope_taken")
            v_turned, v_placed = s.sem("v_turned"), s.sem("v_placed")
            summed, part1, rest_done, part2, part3 = s.sem("summed"), s.sem("part1"), s.sem("rest_done"), s.sem("part2"), s.sem("part3")
            stored = [s.sem(f"stored{r}") for r in range(NR)]

            def slot_user(r):
                if r >= 2:
                    return r - 2 + 1 + 2
                q = NR - 1 if (NR - 1) % 2 == r % 2 else NR - 2
                return q - NR + 1 + 2

            with nc.Block() as block:

                @block.sync
                def _(sp):
                    sp.dma_start(W[:, :, :], w_dram.rearrange("(k p) n -> p k n", p=P)).then_inc(w_in, 16)
                    sp.dma_start(cos[:, :], rope_dram[0]).then_inc(tab_in, 16)
                    sp.dma_start(sin[:, :], rope_dram[1]).then_inc(tab_in, 16)
                    for r in range(NR):
                        sp.nop().then_inc(stored[r], 16)
                    with sp.Fori(0, NCH) as c:
                        for r, (kind, n, M) in enumerate(rope_units):
                            dst = (q_dram if kind == "q" else k_dram)[:, n * P:n * P + M, cols(c)]
                            wait_apart(sp, part3, c * NR + r + 1 + 2)
                            sp.dma_start(dst.rearrange("a f t -> f a t"), parts[0:M, r, :, :]).then_inc(stored[r], 16)
                    for r in range(NR):
                        sp.wait_ge(stored[r], 16 * NCH + 16)

                @block.gpsimd
                def _(pool):
                    pool.nop().then_inc(summed, 2)
                    pool.nop().then_inc(part3, 2)
                    with pool.Fori(0, NCH) as c:
                        wait_apart(pool, h_turned, c + 1)
                        nc.gpsimd.tensor_copy(Hs[:, :, :], H[:, tiles(c), :]).then_inc(staged, 1)
                        for r in range(NR + 1):
                            if r < NR:
                                M = rope_units[r][2]
                                pool.wait_ge(rope_taken, c * NR + r + 1 + 2)
                                pool.wait_ge(rest_done, c * NR + slot_user(r))
                                nc.gpsimd.tensor_tensor(turned[0:M, r % 2, :], direct[0:M, r % 2, :], crossed[0:M, r % 2, :],
                                                        ALU.add).then_inc(summed, 1)
                            if r >= 1:
                                M = rope_units[r - 1][2]
                                pool.wait_ge(part2, c * NR + r)
                                nc.gpsimd.tensor_tensor(parts[0:M, r - 1, 2, :], rest[0:M, (r - 1) % 2, :], parts[0:M, r - 1, 1, :],
                                                        ALU.subtract).then_inc(part3, 1)

                @block.scalar
                def _(act):
                    act.nop().then_inc(v_placed, 1)
                    with act.Fori(0, NCH) as c:
                        act.wait_ge(h_turned, c + 2)
                        act.wait_ge(v_turned, c + 1)
                        for k in range(KD):
                            nc.scalar.copy(hT[:, k, :], ps_t[:, k, :]).then_inc(hT_ready, 1)
                        for v in range(NV):
                            act.wait_ge(unit_ready, c * U + v + 1)
                            nc.scalar.copy(vT[0:VW, v, :], ps_a[v % 2][0:VW, :]).then_inc(v_evac, 1)
                        for r in range(NR + 1):
                            if r < NR:
                                M = rope_units[r][2]
                                act.wait_ge(summed, c * NR + r + 1 + 2)
                                act.wait_ge(stored[r], c * 16 + 16)
                                nc.scalar.copy(parts[0:M, r, 0, :], turned[0:M, r % 2, :]).then_inc(part1, 1)
                            if r >= 1:
                                M = rope_units[r - 1][2]
                                act.wait_ge(rest_done, c * NR + r + 2)
                                nc.scalar.copy(parts[0:M, r - 1, 1, :], rest[0:M, (r - 1) % 2, :]).then_inc(part2, 1)
                        act.wait_ge(v_turned, c + 2)
                        nc.scalar.copy(V[:, tiles(c), 0:KV], ps_v[:, :, 0:KV]).then_inc(v_placed, 1)

                @block.vector
                def _(dve):
                    dve.nop().then_inc(rope_taken, 2)
                    dve.nop().then_inc(rest_done, 2)
                    dve.wait_ge(tab_in, 32)
                    with dve.Fori(0, NCH) as c:
                        for r in range(NR + 1):
                            if r < NR:
                                M, slot = rope_units[r][2], (NV + r) % 2
                                dve.wait_ge(unit_ready, c * U + NV + r + 1)
                                dve.wait_ge(summed, c * NR + slot_user(r))
                                nc.vector.tensor_tensor(direct[0:M, r % 2, :], ps_a[slot][0:M, :], cos[0:M, cols(c)], ALU.mult)
                                nc.vector.tensor_tensor(crossed[0:M, r % 2, :], ps_b[slot][0:M, :], sin[0:M, cols(c)], ALU.mult).then_inc(rope_taken, 1)
                            if r >= 1:
                                M = rope_units[r - 1][2]
                                dve.wait_ge(part1, c * NR + r)
                                dve.wait_ge(part3, c * NR + slot_user(r - 1))
                                nc.vector.tensor_tensor(rest[0:M, (r - 1) % 2, :], turned[0:M, (r - 1) % 2, :], parts[0:M, r - 1, 0, :],
                                                        ALU.subtract).then_inc(rest_done, 1)

                @block.tensor
                def _(pe):
                    pe.nop().then_inc(h_turned, 1)
                    pe.nop().then_inc(v_turned, 1)
                    pe.wait_ge(w_in, 16)
                    with pe.Fori(0, NCH) as c:
                        pe.wait_ge(staged, c + 1)
                        for k in range(KD):
                            for j in range(TPC):
                                tr = nc.tensor.transpose(ps_t[:, k, j * P:(j + 1) * P], Hs[:, j, k * P:(k + 1) * P], ident_f[:, :])
                        tr.then_inc(h_turned, 1)
                        pe.wait_ge(hT_ready, c * KD + KD)
                        for u in range(U):
                            if u < 2:
                                pe.wait_ge(rope_taken, c * NR + u - 1 + 2)
                            elif u - 2 < NV:
                                pe.wait_ge(v_evac, c * NV + u - 2 + 1)
                            else:
                                pe.wait_ge(rope_taken, c * NR + u - 2 - NV + 1 + 2)
                            if u < NV:
                                todo = [(ps_a[u % 2], off_v + u * P, VW)]
                            else:
                                kind, n, M = rope_units[u - NV]
                                a, b = (0, off_qs) if kind == "q" else (off_k, off_ks)
                                todo = [(ps_a[u % 2], a + n * P, M), (ps_b[u % 2], b + n * P, M)]
                            for bank, at, M in todo:
                                for k in range(KD):
                                    mm = nc.tensor.matmul(bank[0:M, :], W[:, k, at:at + M], hT[:, k, :], start=(k == 0), stop=(k == KD - 1))
                            mm.then_inc(unit_ready, 1)
                        wait_apart(pe, v_evac, c * NV + NV)
                        pe.wait_ge(v_placed, c + 1)
                        for j in range(TPC):
                            for v in range(NV):
                                tr = nc.tensor.transpose(ps_v[:, j, v * P:v * P + VW], vT[0:VW, v, j * P:(j + 1) * P], ident_f[0:VW, 0:VW])
                        tr.then_inc(v_turned, 1)

    def attention(name, V, A, kv_heads):
        KH = GROUP if kv_heads == HEADS else 1
        VC = KH * DH
        LAST = NCH - 1
        super0 = [c * (c + 1) // 2 for c in range(NCH + 1)]
        SUPERS = super0[NCH]
        LEAD = NCH + 1
        PAIRS = GROUP // 2
        n_qdma = len(Q_PART)
        places = [(c, k) for c in range(NCH) for k in range(c + 1)]
        places += [(NCH + c, k) for c, k in places[:LEAD]]

        class Step:

            def __init__(self, index, units, waiting):
                self.index, self.count = index, 1
                self.c, self.k = places[index] if index is not None else (None, None)
                self.units = [units[len(units) * i // TPC:len(units) * (i + 1) // TPC] for i in range(TPC)]
                self.turned, self.ends = [], False
                for block in self.units:
                    self.turned.append(waiting)
                    waiting = None
                    for m, j in block:
                        if ends_chunk(m, j):
                            waiting, self.ends = places[m][0], True
                self.waiting = waiting

            def follows(self, other):
                if self.index is None or self.ends or other.ends or any(t is not None for t in self.turned + other.turned):
                    return False
                n = other.count
                if self.c != other.c or other.k == 0 or [len(u) for u in self.units] != [len(u) for u in other.units]:
                    return False
                pairs = [(a, b) for x, y in zip(self.units, other.units) for a, b in zip(x, y)]
                return all(a[0] == b[0] + n and a[1] == b[1] and places[a[0]][0] == places[b[0]][0] and places[b[0]][1] > 0
                           for a, b in pairs)

        def ends_chunk(m, j):
            c, k = places[m]
            return k == c % NCH and j == TPC - 1

        def max_beside(index, more):
            last_chunk = super0[LAST]
            if index == last_chunk - 1:
                return []
            found = [index + LEAD - 1] if index == last_chunk else []
            return [m for m in found + [index + LEAD] if more or m < SUPERS]

        def group_steps(more):
            steps, waiting = [], None
            for index in range(SUPERS):
                step = Step(index, [(m, j) for m in max_beside(index, more) for j in range(TPC)], waiting)
                waiting = step.waiting
                if steps and step.follows(steps[-1]):
                    steps[-1].count += 1
                else:
                    steps.append(step)
            return steps

        def first_steps():
            steps, waiting = [], None
            for m in range(LEAD):
                steps.append(Step(None, [(m, j) for j in range(TPC)], waiting))
                waiting = steps[-1].waiting
            return steps

        def run(eng, group):
            with eng.Fori(0, NGROUPS - 1) as g:
                group(g, True)
            group(NGROUPS - 1, False)

        def over(eng, step, supers, body):
            if step.count == 1:
                body(supers, 0)
            else:
                with eng.Fori(0, step.count) as i:
                    body(eng.snap(supers + i), i)

        def reg(eng, value):
            return value if isinstance(value, int) else eng.snap(value)

        def own(eng, value, most):
            if isinstance(value, int):
                return value
            r = eng.alloc_register()
            eng.reg_mov(r, value)
            return eng.snap(r, donate=True, min_val=0, max_val=most)

        first_turns = sum(t is not None for step in first_steps() for t in step.turned)
        group_turns = sum(t is not None for step in group_steps(True) for t in step.turned) + NCH

        class Turns:

            def __init__(self, base, count):
                self.base, self.count = base, count

            def before(self):
                self.count += 1
                return self.base + (self.count - 1)

        with Space(name) as s:
            K = s.sb("K", [ROWS_M, 2 * KH, T], BF16)
            Q = s.sb("Q", [ROWS_M, NCH * GROUP, CHUNK], BF16)
            prob = s.sb("prob", [P, 2, GROUP, CHUNK])
            v_now = s.sb("v_now", [P, 2, KH, 32])
            o_sb = s.sb("o_sb", [P, CHUNK])
            part_max = s.sb("part_max", [P, GROUP, TPC, NCH])
            row_max = s.sb("row_max", [P, GROUP * TPC])
            max_hl = s.sb("max_hl", [P, 2, GROUP * TPC], BF16)
            rows_sb = s.sb("rows_sb", [2 * GROUP * TPC, P], BF16)
            recip = s.sb("recip", [P, TPC, GROUP])
            sT = [s.ps(f"sT{n}", [P, 2, CHUNK]) for n in range(PAIRS)]
            s_max = [s.ps(f"s_max{n}", [P, CHUNK]) for n in range(2)]
            o_acc = s.ps("o_acc", [P, CHUNK])
            tok = s.ps("tok", [P, TPC, P])
            k_in, q_in = s.sem("k_in"), s.sem("q_in")
            ones_set, v_clear, v_staged = s.sem("ones_set"), s.sem("v_clear"), s.sem("v_staged")
            scores_ready, exp_done, pv_done = s.sem("scores_ready"), s.sem("exp_done"), s.sem("pv_done")
            max_scores, max_taken, max_final = s.sem("max_scores"), s.sem("max_taken"), s.sem("max_final")
            hi_done, max_split, rows_turned, rows_in = s.sem("hi_done"), s.sem("max_split"), s.sem("rows_turned"), s.sem("rows_in")
            o_copied, o_turned, recip_done, tok_used = s.sem("o_copied"), s.sem("o_turned"), s.sem("recip_done"), s.sem("tok_used")

            def kh(h):
                return h if KH == GROUP else 0

            with nc.Block() as block:

                @block.sync
                def _(sp):
                    def load_k(g, slot):
                        for b, part in enumerate(K_PART):
                            src = k_dram[part].rearrange("(h d) t -> d h t", d=DH)[:, bass.ds(g * KH, KH), :]
                            sp.dma_start(K[b * DH:(b + 1) * DH, bass.ds(slot * KH, KH), :], src).then_inc(k_in, 16)

                    def load_q(g, c):
                        for b, part in enumerate(Q_PART):
                            src = q_dram[part].rearrange("(h d) t -> d h t", d=DH)[:, bass.ds(g * GROUP, GROUP), c * CHUNK:(c + 1) * CHUNK]
                            sp.dma_start(Q[b * DH:(b + 1) * DH, c * GROUP:(c + 1) * GROUP, :], src).then_inc(q_in, 16)

                    def place_rows(n, c, turns):
                        if not isinstance(n, int) or n:
                            wait_apart(sp, rows_in, n * 32)
                        wait_apart(sp, tok_used, turns.before() + 2)
                        for part in range(2):
                            rows = rows_sb[part * GROUP * TPC:(part + 1) * GROUP * TPC, :]
                            dst = Q[ROWS + part:ROWS + part + 1, c * GROUP:(c + 1) * GROUP, :].rearrange("a h (q t) -> a (h q) t", q=TPC)
                            sp.dma_start(dst, rows).then_inc(rows_in, 16)

                    load_q(0, 0)
                    load_k(0, 0)
                    for c in range(1, NCH):
                        sp.wait_ge(q_in, c * 16 * n_qdma)
                        load_q(0, c)
                    turns = Turns(0, 0)
                    for step in first_steps():
                        for c in step.turned:
                            if c is not None:
                                place_rows(c, c, turns)

                    def group(g, more):
                        turns = Turns(reg(sp, g * group_turns), first_turns)
                        if more:
                            wait_apart(sp, k_in, (g + 1) * 16 * len(K_PART))
                            load_k(g + 1, (g + 1) % 2)
                        for step in group_steps(more):
                            if step.k == 0 and step.c:
                                turns.before()
                                if more:
                                    reload_q(g, step.c - 1)
                            for c in step.turned:
                                if c is not None:
                                    place_rows(g * NCH + c, c % NCH, turns)
                        if more:
                            reload_q(g, LAST)

                    def reload_q(g, c):
                        n = g * NCH + c
                        wait_apart(sp, o_copied, n + 2)
                        wait_apart(sp, q_in, (n + NCH) * 16 * n_qdma)
                        load_q(g + 1, c)

                    run(sp, group)

                @block.gpsimd
                def _(pool):
                    nc.gpsimd.memset(v_now[:, :, :, :], 0.0).then_inc(v_clear, 1)
                    pool.wait_ge(v_clear, 1)
                    nc.gpsimd.memset(v_now[:, :, :, DH:DH + 1], 1.0).then_inc(v_clear, 1)
                    pool.wait_ge(v_clear, 2)

                    def stage_v(g, block_of_keys, slot, unit):
                        wait_apart(pool, pv_done, unit.of(1, 1))
                        nc.gpsimd.tensor_copy(
                            v_now[:, slot, :, 0:DH],
                            V[:, bass.ds(block_of_keys, 1), bass.ds(g * VC, VC)].rearrange("p a (h d) -> p (a h) d", d=DH)).then_inc(v_staged, 1)

                    with pool.Fori(0, NGROUPS) as g:
                        for c in range(NCH):
                            supers = pool.snap(g * SUPERS + super0[c])
                            for n in range(TPC):
                                stage_v(g, TPC * c + TPC - 1 - n, n % 2, Blocks(supers, n))
                            if c:
                                with pool.Fori(0, c) as sb:
                                    now = pool.snap(supers + sb)
                                    for j in range(TPC):
                                        stage_v(g, sb * TPC + j, j % 2, Blocks(now, TPC + j))

                @block.scalar
                def _(act):
                    def exps(unit, slot, off):
                        for p in range(PAIRS):
                            act.wait_ge(scores_ready, unit.of(PAIRS, p + 1))
                            act.wait_ge(pv_done, unit.of(1, 1))
                            nc.scalar.activation(prob[:, slot, 2 * p:2 * p + 2, off:CHUNK], sT[p][:, :, off:CHUNK], ACT.Exp,
                                                 scale=DH ** -0.5).then_inc(exp_done, 1)

                    act.nop().then_inc(o_copied, 1)
                    act.nop().then_inc(exp_done, PAIRS)
                    with act.Fori(0, NGROUPS) as g:
                        for c in range(NCH):
                            supers, chunks = act.snap(g * SUPERS + super0[c]), act.snap(g * NCH + c)
                            for n in range(TPC):
                                exps(Blocks(supers, n), n % 2, (TPC - 1 - n) * P)
                            if c:
                                with act.Fori(0, c) as sb:
                                    now = act.snap(supers + sb)
                                    for j in range(TPC):
                                        exps(Blocks(now, TPC + j), j % 2, 0)
                            act.wait_ge(pv_done, Blocks(supers, TPC * (c + 1)).of(1, 2))
                            act.wait_ge(o_turned, chunks + 1)
                            nc.scalar.copy(o_sb[:, :], o_acc[:, :]).then_inc(o_copied, 1)

                @block.vector
                def _(dve):
                    def max_unit(supers, i, chunks, m, j):
                        c, k = places[m]
                        width, sb = ((j + 1) * P, c % NCH) if k == 0 else (CHUNK, i + k - 1)
                        for h in range(GROUP):
                            dve.wait_ge(max_scores, Blocks(supers, TPC * m + j).of(GROUP, h + 1))
                            nc.vector.reduce_max(part_max[:, h, j, bass.ds(sb, 1)], s_max[h % 2][:, 0:width], AX.X).then_inc(max_taken, 1)
                        if ends_chunk(m, j):
                            n = chunks + c
                            dve.wait_ge(max_taken, Blocks(supers, TPC * (m + 1)).of(GROUP, 2))
                            dve.wait_ge(rows_turned, n + 1)
                            nc.vector.reduce_max(row_max[:, :], part_max[:, :, :, 0:c % NCH + 1].rearrange("p h q s -> p (h q) s"),
                                                 AX.X).then_inc(max_final, 1)
                            dve.wait_ge(max_final, n + 1)
                            nc.vector.tensor_copy(max_hl[:, 0, :], row_max[:, :]).then_inc(hi_done, 1)
                            dve.wait_ge(hi_done, n + 1)
                            nc.vector.tensor_tensor(max_hl[:, 1, :], row_max[:, :], max_hl[:, 0, :], ALU.subtract).then_inc(max_split, 1)

                    def take_rows(n):
                        dve.wait_ge(rows_turned, n + 2)
                        if not isinstance(n, int) or n:
                            dve.wait_ge(rows_in, n * 32)
                        nc.vector.tensor_copy(rows_sb[:, :], tok[0:2 * GROUP * TPC, 0, :]).then_inc(tok_used, 1)

                    def place_o(n, g, c):
                        dve.wait_ge(o_turned, n + 2)
                        o = tok[:, :, :].rearrange("p q (h d) -> p q h d", h=GROUP)
                        nc.vector.reciprocal(recip[:, :, :], o[:, :, :, DH]).then_inc(recip_done, 1)
                        dve.wait_ge(recip_done, n + 1)
                        dst = A[:, c * TPC:(c + 1) * TPC, bass.ds(g * GROUP * DH, GROUP * DH)].rearrange("p q (h d) -> p q h d", h=GROUP)
                        nc.vector.tensor_tensor(dst, o[:, :, :, 0:DH], recip[:, :, :].unsqueeze(3).to_broadcast([P, TPC, GROUP, DH]),
                                                ALU.mult).then_inc(tok_used, 1)

                    def blocks(supers, i, g, chunks, step):
                        for b in range(TPC):
                            for m, j in step.units[b]:
                                max_unit(supers, i, chunks, m, j)
                            if step.k == 0 and step.c and b == 0:
                                place_o(chunks + (step.c - 1), g, step.c - 1)
                            if step.turned[b] is not None:
                                take_rows(chunks + step.turned[b])

                    dve.nop().then_inc(max_taken, 2)
                    dve.nop().then_inc(tok_used, 1)
                    nc.vector.memset(K[ROWS:ROWS_M, :, :].bitcast(F32), PAIR_OF_ONES).then_inc(ones_set, 1)
                    for step in first_steps():
                        blocks(0, 0, 0, 0, step)

                    def group(g, more):
                        for step in group_steps(more):
                            supers, chunks = reg(dve, g * SUPERS), reg(dve, g * NCH)
                            if any(step.units) or step.k == 0 or any(t is not None for t in step.turned):
                                over(dve, step, supers, lambda now, i: blocks(now, i, g, chunks, step))
                        place_o(chunks + LAST, g, LAST)

                    run(dve, group)

                @block.tensor
                def _(pe):
                    def max_tile(k_slots, supers, i, m, j, h):
                        c, k = places[m]
                        q = Q[0:ROWS, c % NCH * GROUP + h, j * P:(j + 1) * P]
                        width, sb = ((j + 1) * P, c % NCH) if k == 0 else (CHUNK, i + k - 1)
                        keys = K[0:ROWS, bass.ds(k_slots[c // NCH] + kh(h), 1), bass.ds(sb * CHUNK, width)].rearrange("r a k -> r (a k)")
                        pe.wait_ge(max_taken, Blocks(supers, TPC * m + j).of(GROUP, h + 1))
                        mm = nc.tensor.matmul(s_max[h % 2][:, 0:width], q, keys, start=True, stop=k > 0)
                        if k == 0:
                            mm = nc.tensor.matmul(s_max[h % 2][:, width - P:width], ident_b[:, :], mask_q[:, :], start=False, stop=True)
                        mm.then_inc(max_scores, 1)

                    def scores(k_slot, unit, c, block_of_keys, off, p, diag):
                        pe.wait_ge(exp_done, unit.of(PAIRS, p + 1))
                        for hh in range(2):
                            h = 2 * p + hh
                            k = K[:, bass.ds(k_slot + kh(h), 1), bass.ds(block_of_keys * P, P)].rearrange("r a k -> r (a k)")
                            mm = nc.tensor.matmul(sT[p][:, hh, off:CHUNK], k, Q[:, c * GROUP + h, off:CHUNK], start=True, stop=not diag)
                            if diag:
                                mm = nc.tensor.matmul(sT[p][:, hh, off:off + P], ident_b[:, :], mask_k[:, :], start=False, stop=True)
                        mm.then_inc(scores_ready, 1)

                    def values(unit, slot, a, b, first, last):
                        if first is not None:
                            pe.wait_ge(o_copied, first + 1)
                        pe.wait_ge(exp_done, unit.of(PAIRS, PAIRS + 2))
                        pe.wait_ge(v_staged, unit.of(1, 1))
                        for h in range(GROUP):
                            mm = nc.tensor.matmul(o_acc[32 * h:32 * h + 32, a:b], v_now[:, slot, kh(h), :], prob[:, slot, h, a:b],
                                                  start=first is not None, stop=True, skip_group_check=True)
                        if last:
                            mm.then_inc(pv_done, 1)

                    def blocks(supers, i, chunks, k_slots, step):
                        for b in range(TPC):
                            tiles_beside = [(m, j, h) for m, j in step.units[b] for h in range(GROUP)]
                            for m, j, h in tiles_beside:
                                c, k = places[m]
                                if (k, j, h) == (0, 0, 0):
                                    pe.wait_ge(q_in, (chunks + c) * (16 * n_qdma) + 16 * n_qdma)
                                    if c == NCH:
                                        pe.wait_ge(k_in, (chunks + c) * (16 * len(K_PART) // NCH) + 16 * len(K_PART))

                            def maxima(quarter):
                                n = len(tiles_beside)
                                for m, j, h in tiles_beside[n * quarter // 4:n * (quarter + 1) // 4]:
                                    max_tile(k_slots, supers, i, m, j, h)

                            if step.index is None:
                                for quarter in range(4):
                                    maxima(quarter)
                            else:
                                unit = TPC * step.index + b
                                diag = step.k == 0
                                key_block = step.c * TPC + TPC - 1 - b if diag else i * TPC + (TPC * (step.k - 1) + b)
                                off = (TPC - 1 - b) * P if diag else 0
                                has_before = b > 0 or not diag
                                before_off = off + P if diag else 0
                                mid = CHUNK // 2 if before_off < CHUNK // 2 else CHUNK
                                first = chunks + step.c if diag and b == 1 else None
                                maxima(0)
                                scores(k_slots[0], Blocks(supers, unit), step.c, key_block, off, 0, diag)
                                maxima(1)
                                if has_before:
                                    values(Blocks(supers, unit - 1), (b + 1) % 2, before_off, mid, first, mid == CHUNK)
                                maxima(2)
                                scores(k_slots[0], Blocks(supers, unit), step.c, key_block, off, 1, diag)
                                maxima(3)
                                if has_before and mid < CHUNK:
                                    values(Blocks(supers, unit - 1), (b + 1) % 2, mid, CHUNK, None, True)
                                if diag and step.c and b == 0:
                                    turn_o(chunks + (step.c - 1))
                            if step.turned[b] is not None:
                                turn_rows(chunks + step.turned[b])

                    def turn_rows(n):
                        pe.wait_ge(max_split, n + 1)
                        pe.wait_ge(tok_used, turns.before() + 1)
                        nc.tensor.matmul(tok[0:2 * GROUP * TPC, 0, :], max_hl[:, :, :].rearrange("p a n -> p (a n)"), neg_ident_b[:, :],
                                         start=True, stop=True).then_inc(rows_turned, 1)

                    def turn_o(n):
                        pe.wait_ge(o_copied, n + 2)
                        pe.wait_ge(tok_used, turns.before() + 1)
                        for q in range(TPC):
                            tr = nc.tensor.transpose(tok[:, q, :], o_sb[:, q * P:(q + 1) * P], ident_f[:, :])
                        tr.then_inc(o_turned, 1)

                    pe.nop().then_inc(rows_turned, 1)
                    pe.nop().then_inc(pv_done, 2)
                    pe.nop().then_inc(o_turned, 1)
                    pe.wait_ge(ones_set, 1)
                    pe.wait_ge(k_in, 16 * len(K_PART))
                    turns = Turns(0, 0)
                    for step in first_steps():
                        blocks(0, 0, 0, (0, KH), step)

                    def group(g, more):
                        nonlocal turns
                        turns = Turns(reg(pe, g * group_turns), first_turns)
                        for step in group_steps(more):
                            supers, chunks = reg(pe, g * SUPERS), reg(pe, g * NCH)
                            k_slots = own(pe, g % 2 * KH, KH), own(pe, (g + 1) % 2 * KH, KH)
                            if step.k == 0:
                                pe.wait_ge(rows_in, (chunks + step.c) * 32 + 32)
                            over(pe, step, supers, lambda now, i: blocks(now, i, chunks, k_slots, step))
                            if step.k + step.count - 1 == step.c:
                                end = Blocks(supers, TPC * super0[step.c + 1] - 1)
                                values(end, (TPC - 1) % 2, 0, CHUNK // 2, None, False)
                                values(end, (TPC - 1) % 2, CHUNK // 2, CHUNK, None, True)
                        turn_o(chunks + LAST)

                    run(pe, group)

    def out_projection(name, A, w_dram, gain, base_dram, X, keep):
        with Space(name) as s:
            W = s.sb("W", [P, KD, D])
            As = s.sb("As", [P, TPC, D])
            aT = s.sb("aT", [P, KD, CHUNK])
            ps_t = s.ps("ps_t", [P, KD, CHUNK])
            ps_o = s.ps("ps_o", [P, TPC, D])
            w_in, loaded, staged, turned, aT_ready = s.sem("w_in"), s.sem("loaded"), s.sem("staged"), s.sem("turned"), s.sem("aT_ready")
            product, gained, added, stored = s.sem("product"), s.sem("gained"), s.sem("added"), s.sem("stored")
            gain_out = s.sb("gain_out", [P, TPC, D])
            with nc.Block() as block:

                @block.sync
                def _(sp):
                    sp.dma_start(W[:, :, :], w_dram.rearrange("(k p) n -> p k n", p=P)).then_inc(w_in, 16)
                    with sp.Fori(0, NCH) as c:
                        sp.dma_start(X[:, tiles(c), :], by_tile(base_dram)[:, tiles(c), :]).then_inc(loaded, 16)
                        wait_apart(sp, loaded, c * 16 + 16)
                    if keep is not None:
                        with sp.Fori(0, NCH) as c:
                            wait_apart(sp, added, c + 2)
                            sp.dma_start(by_tile(keep)[:, tiles(c), :], X[:, tiles(c), :]).then_inc(stored, 16)
                        sp.wait_ge(stored, 16 * NCH)

                @block.gpsimd
                def _(pool):
                    with pool.Fori(0, NCH) as c:
                        wait_apart(pool, turned, c + 1)
                        nc.gpsimd.tensor_copy(As[:, :, :], A[:, tiles(c), :]).then_inc(staged, 1)

                @block.scalar
                def _(act):
                    with act.Fori(0, NCH) as c:
                        act.wait_ge(turned, c + 2)
                        act.wait_ge(product, c + 1)
                        for k in range(KD):
                            nc.scalar.copy(aT[:, k, :], ps_t[:, k, :]).then_inc(aT_ready, 1)

                @block.vector
                def _(dve):
                    dve.nop().then_inc(added, 1)
                    with dve.Fori(0, NCH) as c:
                        dve.wait_ge(product, c + 2)
                        dve.wait_ge(added, c + 1)
                        if gain is None:
                            dve.wait_ge(loaded, c * 16 + 16)
                            nc.vector.tensor_tensor(X[:, tiles(c), :], ps_o[:, :, :], X[:, tiles(c), :], ALU.add).then_inc(added, 1)
                        else:
                            nc.vector.tensor_tensor(gain_out[:, :, :], ps_o[:, :, :], row_bcast(gain, TPC), ALU.mult).then_inc(gained, 1)
                            dve.wait_ge(gained, c + 1)
                            dve.wait_ge(loaded, c * 16 + 16)
                            nc.vector.tensor_tensor(X[:, tiles(c), :], gain_out[:, :, :], X[:, tiles(c), :], ALU.add).then_inc(added, 1)

                @block.tensor
                def _(pe):
                    pe.nop().then_inc(turned, 1)
                    pe.nop().then_inc(product, 1)
                    pe.wait_ge(w_in, 16)
                    with pe.Fori(0, NCH) as c:
                        pe.wait_ge(staged, c + 1)
                        for k in range(KD):
                            for j in range(TPC):
                                tr = nc.tensor.transpose(ps_t[:, k, j * P:(j + 1) * P], As[:, j, k * P:(k + 1) * P], ident_f[:, :])
                        tr.then_inc(turned, 1)
                        pe.wait_ge(aT_ready, c * KD + KD)
                        pe.wait_ge(added, c + 1)
                        for j in range(TPC):
                            for k in range(KD):
                                mm = nc.tensor.matmul(ps_o[:, j, :], aT[:, k, j * P:(j + 1) * P], W[:, k, :], start=(k == 0), stop=(k == KD - 1))
                        mm.then_inc(product, 1)

    def router(name, Y, comb, lower_dram):
        with Space(name) as s:
            Wg = s.sb("Wg", [P, KD, E])
            lower_t = s.sb("lower_t", [P, E * E])
            Ys = s.sb("Ys", [P, TPC, D])
            ltok = s.sb("ltok", [E, CHUNK])
            top = s.sb("top", [P, TPC])
            shifted, probs, ex, pm = (s.sb(n, [P, TPC, E]) for n in ("shifted", "probs", "ex", "pm"))
            total, rtotal, psum_, rsum = (s.sb(n, [P, TPC]) for n in ("total", "rtotal", "psum_", "rsum"))
            above, equal, ahead = (s.sb(n, [P, TPC, E, E]) for n in ("above", "equal", "ahead"))
            rank = s.sb("rank", [P, TPC, E])
            ps_t = s.ps("ps_t", [P, KD, CHUNK])
            ps_l = s.ps("ps_l", [E, CHUNK])
            ps_g = s.ps("ps_g", [P, TPC, E])
            w_in, staged, turned, yT_ready = s.sem("w_in"), s.sem("staged"), s.sem("turned"), s.sem("yT_ready")
            logits, logits_out, logits_tok, exped, step = s.sem("logits"), s.sem("logits_out"), s.sem("logits_tok"), s.sem("exped"), s.sem("step")
            logits_tok_used = s.sem("logits_tok_used")
            STEPS = 13
            with nc.Block() as block:

                @block.sync
                def _(sp):
                    sp.dma_start(Wg[:, :, :], gate.rearrange("(k p) e -> p k e", p=P)).then_inc(w_in, 16)
                    sp.dma_start(lower_t[:, :], lower_dram).then_inc(w_in, 16)

                @block.gpsimd
                def _(pool):
                    with pool.Fori(0, NCH) as c:
                        wait_apart(pool, turned, c + 1)
                        nc.gpsimd.tensor_copy(Ys[:, :, :], Y[:, tiles(c), :]).then_inc(staged, 1)

                @block.scalar
                def _(act):
                    with act.Fori(0, NCH) as c:
                        act.wait_ge(turned, c + 2)
                        for k in range(KD):
                            nc.scalar.copy(feature_major(Y, c, k), ps_t[:, k, :]).then_inc(yT_ready, 1)
                        act.wait_ge(logits, c + 1)
                        nc.scalar.copy(ltok[:, :], ps_l[:, :]).then_inc(logits_out, 1)
                        act.wait_ge(step, c * STEPS + 2)
                        nc.scalar.activation(ex[:, :, :], shifted[:, :, :], ACT.Exp).then_inc(exped, 1)

                @block.vector
                def _(dve):
                    dve.nop().then_inc(logits_tok_used, 1)
                    dve.wait_ge(w_in, 32)
                    with dve.Fori(0, NCH) as c:
                        def after(n):
                            dve.wait_ge(step, c * STEPS + n)

                        dve.wait_ge(logits_tok, c + 1)
                        nc.vector.reduce_max(top[:, :], ps_g[:, :, :], AX.X).then_inc(step, 1)
                        after(1)
                        nc.vector.tensor_tensor(shifted[:, :, :], ps_g[:, :, :], col_bcast(top[:, :], E), ALU.subtract).then_inc(step, 1)
                        dve.wait_ge(exped, c + 1)
                        nc.vector.reduce_sum(total[:, :], ex[:, :, :], AX.X).then_inc(step, 1)
                        after(3)
                        nc.vector.reciprocal(rtotal[:, :], total[:, :]).then_inc(step, 1)
                        after(4)
                        nc.vector.tensor_tensor(probs[:, :, :], ex[:, :, :], col_bcast(rtotal[:, :], E), ALU.mult).then_inc(step, 1)
                        after(5)
                        mine = probs[:, :, :].unsqueeze(3).to_broadcast([P, TPC, E, E])
                        other = probs[:, :, :].unsqueeze(2).to_broadcast([P, TPC, E, E])
                        nc.vector.tensor_tensor(above[:, :, :, :], other, mine, ALU.is_gt).then_inc(step, 1)
                        nc.vector.tensor_tensor(equal[:, :, :, :], other, mine, ALU.is_equal).then_inc(step, 1)
                        after(7)
                        nc.vector.tensor_tensor(ahead[:, :, :, :].rearrange("p q a b -> p q (a b)"), equal[:, :, :, :].rearrange("p q a b -> p q (a b)"),
                                                row_bcast(lower_t[:, :], TPC), ALU.mult).then_inc(step, 1)
                        after(8)
                        nc.vector.tensor_tensor(above[:, :, :, :], above[:, :, :, :], ahead[:, :, :, :], ALU.add).then_inc(step, 1)
                        after(9)
                        nc.vector.reduce_sum(rank[:, :, :], above[:, :, :, :], AX.X).then_inc(step, 1)
                        after(10)
                        nc.vector.scalar_tensor_tensor(out=pm[:, :, :], in0=rank[:, :, :], scalar=2.0, in1=probs[:, :, :],
                                                       op0=ALU.is_lt, op1=ALU.mult).then_inc(step, 1)
                        after(11)
                        nc.vector.reduce_sum(psum_[:, :], pm[:, :, :], AX.X).then_inc(step, 1)
                        after(12)
                        nc.vector.reciprocal(rsum[:, :], psum_[:, :]).then_inc(step, 1)
                        after(13)
                        nc.vector.tensor_tensor(comb[:, tiles(c), :], pm[:, :, :], col_bcast(rsum[:, :], E), ALU.mult).then_inc(logits_tok_used, 1)

                @block.tensor
                def _(pe):
                    pe.nop().then_inc(turned, 1)
                    pe.wait_ge(w_in, 32)
                    with pe.Fori(0, NCH) as c:
                        pe.wait_ge(staged, c + 1)
                        for k in range(KD):
                            for j in range(TPC):
                                tr = nc.tensor.transpose(ps_t[:, k, j * P:(j + 1) * P], Ys[:, j, k * P:(k + 1) * P], ident_f[:, :])
                        tr.then_inc(turned, 1)
                        pe.wait_ge(yT_ready, c * KD + KD)
                        for k in range(KD):
                            mm = nc.tensor.matmul(ps_l[:, :], Wg[:, k, :], feature_major(Y, c, k), start=(k == 0), stop=(k == KD - 1))
                        mm.then_inc(logits, 1)
                        wait_apart(pe, logits_out, c + 1)
                        pe.wait_ge(logits_tok_used, c + 1)
                        for j in range(TPC):
                            tr = nc.tensor.transpose(ps_g[:, j, :], ltok[:, j * P:(j + 1) * P], ident_f[0:E, 0:E])
                        tr.then_inc(logits_tok, 1)

    def experts(name, YT, comb, Fx, gain):
        with Space(name) as s:
            W1 = s.sb("W1", [P, E, KD, HID])
            W3 = s.sb("W3", [P, E, KD, HID])
            W2 = s.sb("W2", [P, E, HB, D])
            x1 = s.sb("x1", [P, TPC, D])
            gated = s.sb("gated", [P, 2, CHUNK])
            hT = s.sb("hT", [P, 2, HB, CHUNK])
            acc = s.sb("acc", [P, TPC, D])
            ps_1 = [s.ps(f"ps_1{n}", [P, CHUNK]) for n in range(2)]
            ps_3 = [s.ps(f"ps_3{n}", [P, CHUNK]) for n in range(2)]
            ps_y = [s.ps(f"ps_y{n}", [P, TPC, D]) for n in range(2)]
            w_in = [s.sem(f"w_in{e}") for e in range(E)]
            x1_in, stored = s.sem("x1_in"), s.sem("stored")
            up_ready, silu_done, h_ready = s.sem("up_ready"), s.sem("silu_done"), s.sem("h_ready")
            down_ready, down_taken, gained, final = s.sem("down_ready"), s.sem("down_taken"), s.sem("gained"), s.sem("final")
            with nc.Block() as block:

                @block.sync
                def _(sp):
                    for e in range(E):
                        sp.dma_start(W1[:, e, :, :], w1[e].rearrange("(k p) n -> p k n", p=P)).then_inc(w_in[e], 16)
                        sp.dma_start(W3[:, e, :, :], w3[e].rearrange("(k p) n -> p k n", p=P)).then_inc(w_in[e], 16)
                        sp.dma_start(W2[:, e, :, :], w2[e].rearrange("(k p) n -> p k n", p=P)).then_inc(w_in[e], 16)
                    sp.nop().then_inc(stored, 16)
                    with sp.Fori(0, NCH) as c:
                        wait_apart(sp, final, c + 1)
                        sp.dma_start(x1[:, :, :], by_tile(x1_dram)[:, tiles(c), :]).then_inc(x1_in, 16)
                        wait_apart(sp, final, c + 2)
                        sp.dma_start(by_tile(out)[:, tiles(c), :], acc[:, :, :]).then_inc(stored, 16)
                    sp.wait_ge(stored, 16 * NCH + 16)

                @block.scalar
                def _(act):
                    act.nop().then_inc(silu_done, 2)
                    with act.Fori(0, NCH) as c:
                        for u in range(E * HB):
                            U = c * (E * HB) + u
                            act.wait_ge(up_ready, U + 1)
                            act.wait_ge(h_ready, U + 1)
                            nc.scalar.activation(gated[:, u % 2, :], ps_1[u % 2][:, :], ACT.Silu).then_inc(silu_done, 1)

                @block.vector
                def _(dve):
                    def weigh(c, e):
                        n = c * E + e
                        dve.wait_ge(down_ready, n + 3)
                        for j in range(TPC):
                            i = bass.ds(c * TPC + j, 1)
                            f = Fx[:, i, :].rearrange("p a f -> p (a f)")
                            w = comb[:, i, e:e + 1].rearrange("p a f -> p (a f)")
                            dve.wait_ge(down_taken, (n + 1) * TPC + j + 1)
                            op = nc.vector.scalar_tensor_tensor(out=f, in0=ps_y[e % 2][:, j, :], scalar=w, in1=f, op0=ALU.mult, op1=ALU.add)
                            op.then_inc(down_taken, 1)

                    dve.nop().then_inc(h_ready, 2)
                    dve.nop().then_inc(down_taken, 2 * TPC)
                    dve.nop().then_inc(final, 1)
                    with dve.Fori(0, NCH) as c:
                        for e in range(E):
                            for hb in range(HB):
                                u = e * HB + hb
                                U = c * (E * HB) + u
                                dve.wait_ge(silu_done, U + 3)
                                dve.wait_ge(down_ready, c * E + e + 1)
                                nc.vector.tensor_tensor(hT[:, e % 2, hb, :], gated[:, u % 2, :], ps_3[u % 2][:, :], ALU.mult).then_inc(h_ready, 1)
                            if e:
                                weigh(c, e - 1)
                        weigh(c, E - 1)
                        dve.wait_ge(down_taken, (c + 1) * E * TPC + 2 * TPC)
                        dve.wait_ge(stored, c * 16 + 16)
                        nc.vector.tensor_tensor(acc[:, :, :], Fx[:, tiles(c), :], row_bcast(gain, TPC), ALU.mult).then_inc(gained, 1)
                        dve.wait_ge(gained, c + 1)
                        dve.wait_ge(x1_in, c * 16 + 16)
                        nc.vector.tensor_tensor(acc[:, :, :], acc[:, :, :], x1[:, :, :], ALU.add).then_inc(final, 1)

                @block.tensor
                def _(pe):
                    def down(c, e):
                        n = c * E + e
                        pe.wait_ge(h_ready, (n + 1) * HB + 2)
                        pe.wait_ge(down_taken, (n + 1) * TPC)
                        for j in range(TPC):
                            for hb in range(HB):
                                mm = nc.tensor.matmul(ps_y[e % 2][:, j, :], hT[:, e % 2, hb, j * P:(j + 1) * P], W2[:, e, hb, :],
                                                      start=(hb == 0), stop=(hb == HB - 1))
                        mm.then_inc(down_ready, 1)

                    pe.nop().then_inc(down_ready, 2)
                    for e in range(E):
                        pe.wait_ge(w_in[e], 48)
                    with pe.Fori(0, NCH) as c:
                        for e in range(E):
                            for hb in range(HB):
                                u = e * HB + hb
                                U = c * (E * HB) + u
                                pe.wait_ge(h_ready, U + 1)
                                for bank, W in ((ps_1, W1), (ps_3, W3)):
                                    for k in range(KD):
                                        mm = nc.tensor.matmul(bank[u % 2][:, :], W[:, e, k, hb * P:(hb + 1) * P], feature_major(YT, c, k),
                                                              start=(k == 0), stop=(k == KD - 1))
                                mm.then_inc(up_ready, 1)
                                if hb == 0 and e:
                                    down(c, e - 1)
                        down(c, E - 1)

    stack = ExitStack()

    def keep_sb(where, name, shape, dt=F32):
        return where.enter_context(nc.sbuf_tensor(name, shape, dt))

    with stack:
        begun = stack.enter_context(nc.semaphore("begun"))
        ident_f = keep_sb(stack, "ident_f", [P, P])
        ident_b = keep_sb(stack, "ident_b", [P, P], BF16)
        neg_ident_b = keep_sb(stack, "neg_ident_b", [P, P], BF16)
        mask_k = keep_sb(stack, "mask_k", [P, P], BF16)
        mask_q = keep_sb(stack, "mask_q", [P, P], BF16)
        mod = keep_sb(stack, "mod", [P, 6, D])
        gains = keep_sb(stack, "gains", [P, 2, D])
        neg_half = keep_sb(stack, "neg_half", [P, TPC])
        setup(ident_f, ident_b, neg_ident_b, mask_k, mask_q, mod, gains, neg_half)

        tok_a = keep_sb(stack, "tok_a", [P, NT, D])
        tok_b = keep_sb(stack, "tok_b", [P, NT, D])
        shift_a, scale_a, gain_a, shift_b, scale_b, gain_b = (mod[:, v, :] for v in range(6))

        norms("ln1", tok_a, x, shift_a, scale_a, None, None, None, neg_half)
        projections("qkv1", tok_a, wqkv[0], rope[0], tok_b, KVH[0])
        attention("att1", tok_b, tok_a, KVH[0])
        out_projection("out1", tok_a, wo[0], gain_a, x, tok_b, x1_dram)
        norms("ln2", tok_b, None, shift_b, scale_b, gains[:, 0, :], tok_a, h2_dram, neg_half)
        projections("qkv2", tok_a, wqkv[1], rope[1], tok_b, KVH[1])
        attention("att2", tok_b, tok_a, KVH[1])
        out_projection("out2", tok_a, wo[1], None, h2_dram, tok_b, None)
        norms("rms2", tok_b, None, None, None, gains[:, 1, :], tok_a, None, neg_half)
        with ExitStack() as last:
            comb = keep_sb(last, "comb", [P, NT, E])
            router("router", tok_a, comb, lower)
            experts("moe", tok_a, comb, tok_b, gain_b)


def shape_constants(T, D):
    import numpy as np

    f32 = np.float32
    pos = np.arange(T, dtype=f32)
    half = np.arange(DH // 2, dtype=f32)
    theta = (f32(10000.0) ** (f32(-2.0) * half / f32(DH))).astype(f32)
    inv_freq = (f32(1.0) / f32(10000.0) ** (f32(2.0) * half / f32(DH))).astype(f32)
    rows = np.arange(P) % DH
    rope = np.zeros((2, 2, P, T), f32)
    for n, (freq, of_row, sign) in enumerate((
        (theta, rows // 2, np.where(rows % 2 == 0, -1.0, 1.0)),
        (inv_freq, rows % (DH // 2), np.where(rows < DH // 2, -1.0, 1.0)),
    )):
        angle = (pos[:, None] * freq[None, :]).astype(f32)
        rope[n, 0] = np.cos(angle).astype(f32).T[of_row]
        rope[n, 1] = np.sin(angle).astype(f32).T[of_row] * sign.astype(f32)[:, None]
    ident = np.eye(P, dtype=f32)
    a, b = np.arange(P)[:, None], np.arange(P)[None, :]
    masks = np.stack([np.where(a > b, HIDDEN_NEG, 0.0), np.where(b > a, HIDDEN_NEG, 0.0)]).astype(f32)
    return rope, ident, masks


def kernel(L0_attn_X, L0_attn_W_q, L0_attn_W_k, L0_attn_W_v, L0_attn_W_o, L0_ffn_g1, L0_ffn_g2, L0_ffn_wq, L0_ffn_wk,
           L0_ffn_wv, L0_ffn_wo, L0_ffn_gate, L0_ffn_w1, L0_ffn_w2, L0_ffn_w3, L0_c, L0_wmod):
    import numpy as np
    import concourse.bacc as bacc
    from concourse.bass_utils import run_bass_kernel_spmd as run

    X = np.asarray(L0_attn_X)
    _, T, D = X.shape
    E = np.asarray(L0_ffn_gate).shape[1]
    rope, ident, masks = shape_constants(T, D)
    pairs = np.arange(D) ^ 1
    halves = np.arange(D) ^ (DH // 2)
    q1, k1, v1 = (np.asarray(w).T for w in (L0_attn_W_q, L0_attn_W_k, L0_attn_W_v))
    q2, k2, v2 = (np.asarray(w) for w in (L0_ffn_wq, L0_ffn_wk, L0_ffn_wv))
    nk = k2.shape[1]
    arrays = {
        "x": X[0],
        "wqkv_1": np.concatenate([q1, k1, q1[:, pairs], k1[:, pairs], v1], axis=1),
        "wqkv_2": np.concatenate([q2, k2, q2[:, halves], k2[:, halves[:nk]], v2], axis=1),
        "rope": rope,
        "wo_1": np.asarray(L0_attn_W_o).T,
        "wo_2": np.asarray(L0_ffn_wo),
        "g12": np.concatenate([np.asarray(L0_ffn_g1), np.asarray(L0_ffn_g2)])[None, :],
        "wmod": np.asarray(L0_wmod),
        "c_col": np.asarray(L0_c)[0].reshape(D // P, P).T,
        "gate": np.asarray(L0_ffn_gate),
        "w1": np.asarray(L0_ffn_w1),
        "w2": np.asarray(L0_ffn_w2),
        "w3": np.asarray(L0_ffn_w3),
        "ident": ident,
        "masks": masks,
        "lower": np.ascontiguousarray(np.broadcast_to(np.tril(np.ones((E, E), np.float32), -1).reshape(1, E * E), (P, E * E))),
    }
    arrays = {n: np.ascontiguousarray(a) for n, a in arrays.items()}
    nc = bacc.Bacc("TRN2", target_bir_lowering=False, num_devices=1)
    t = {n: nc.dram_tensor(n, a.shape, mybir.dt.from_np(a.dtype), kind="ExternalInput").ap() for n, a in arrays.items()}
    out = nc.dram_tensor("out", (T, D), F32, kind="ExternalOutput").ap()
    adaln_program(nc, t["x"], (t["wqkv_1"], t["wqkv_2"]), t["rope"], (t["wo_1"], t["wo_2"]), t["g12"], t["wmod"], t["c_col"],
                  t["gate"], t["w1"], t["w2"], t["w3"], t["ident"], t["masks"], t["lower"], out)
    r = run(nc, [arrays], core_ids=[0])
    return r.results[0]["out"].reshape(1, T, D)
```

```python
from contextlib import ExitStack

import concourse.bass as bass
from concourse import mybir

P = 128
F32 = mybir.dt.float32
BF16 = mybir.dt.bfloat16
F32R = mybir.dt.float32r
ACT = mybir.ActivationFunctionType
ALU = mybir.AluOpType
AX = mybir.AxisListType

HEADS = 16
DH = 16
GROUP = 4
PARTS = 3
Q_PART = (0, 0, 0, 1, 1, 2)
K_PART = (0, 1, 2, 0, 1, 0)
ROWS = len(Q_PART) * DH
ROWS_M = ROWS + 2
CHUNK = 512
LN_EPS = 1e-5
RMS_EPS = 1.1920928955078125e-07
PAIR_OF_ONES = 1.0 + 0x3F80 / 2.0 ** 23
HIDDEN_NEG = -1e30


class Blocks:

    def __init__(self, supers, more):
        self.supers, self.more = supers, more

    def of(self, each, plus):
        return self.supers * (CHUNK // P * each) + (self.more * each + plus)


def adaln_program(nc, x, wqkv, rope, wo, g12, wmod, c_col, gate, w_all, ident, masks, lower, out):
    T, D = x.shape
    NT = T // P
    NCH = T // CHUNK
    TPC = CHUNK // P
    KD = D // P
    E = gate.shape[1]
    HID = w_all.shape[2] // (3 * KD)
    PIECE = w_all.shape[2] // NCH
    HB = HID // P
    NGROUPS = HEADS // GROUP
    KVH = (HEADS, NGROUPS)

    x1_dram = nc.dram_tensor("x1_dram", (T, D), F32, kind="Internal").ap()
    h2_dram = nc.dram_tensor("h2_dram", (T, D), F32, kind="Internal").ap()
    q_dram = nc.dram_tensor("q_dram", (PARTS, D, T), BF16, kind="Internal").ap()
    k_dram = nc.dram_tensor("k_dram", (PARTS, D, T), BF16, kind="Internal").ap()

    def wait_apart(eng, sem, value):
        if not isinstance(value, int):
            value = eng.to_reg(value)
            eng.wait_ge(begun, 1)
        eng.wait_ge(sem, value)

    def by_tile(dram):
        return dram.rearrange("(i p) f -> p i f", p=P)

    def tiles(c):
        return bass.ds(c * TPC, TPC)

    def cols(c):
        return bass.ds(c * CHUNK, CHUNK)

    def row_bcast(row, n):
        return row.unsqueeze(1).to_broadcast([P, n, row.shape[1]])

    def col_bcast(a, w):
        return a.unsqueeze(2).to_broadcast([P, a.shape[1], w])

    def by_pairs(eng, period, full):
        with eng.Fori(0, full // 2) as pair:
            for par in range(2):
                period(pair * 2 + par, par, True)
        for c in range(full, NCH):
            period(c, c % 2, False)

    def exists(c, whole, ahead):
        return whole or c + ahead < NCH

    class Space:

        def __init__(self, name):
            self.name = name
            self.sems = []

        def __enter__(self):
            self.stack = ExitStack()
            return self

        def __exit__(self, *a):
            if a[0] is None:
                with nc.Block() as block:

                    @block.sync
                    def _(sp):
                        for handle in self.sems:
                            sp.sem_clear(handle)

            self.stack.close()

        def sb(self, name, shape, dt=F32):
            return self.stack.enter_context(nc.sbuf_tensor(f"{self.name}_{name}", shape, dt))

        def ps(self, name, shape, dt=F32):
            return self.stack.enter_context(nc.psum_tensor(f"{self.name}_{name}", shape, dt))

        def sem(self, name):
            self.sems.append(self.stack.enter_context(nc.semaphore(f"{self.name}_{name}")))
            return self.sems[-1]

    def setup(ident_f, ident_b, neg_ident_b, mask_k, mask_q, mod, gains, neg_half):
        with Space("set") as s:
            msk = s.sb("msk", [P, 2, P])
            cc = s.sb("cc", [P, KD])
            sc = s.sb("sc", [P, KD])
            scb = s.sb("scb", [P, KD, P])
            ones = s.sb("ones", [P, P])
            wm = s.sb("wm", [P, KD, 6 * D])
            grow = s.sb("grow", [1, 2 * D])
            raw = s.sb("raw", [P, 6 * D])
            sign = s.sb("sign", [P, 2, D])
            pm = [s.ps(f"pm{n}", [P, CHUNK]) for n in range(4)]
            loaded, ones_set, silu_done = s.sem("loaded"), s.sem("ones_set"), s.sem("silu_done")
            bc_done, mod_done, raw_done, dve = s.sem("bc_done"), s.sem("mod_done"), s.sem("raw_done"), s.sem("dve")
            ident_in = s.sem("ident_in")
            with nc.Block() as block:

                @block.sync
                def _(sp):
                    sp.nop().then_inc(begun, 1)
                    sp.dma_start(ident_f[:, :], ident).then_inc(ident_in, 16)
                    sp.dma_start(msk[:, :, :], masks.rearrange("a p n -> p a n")).then_inc(ident_in, 16)
                    sp.dma_start(cc[:, :], c_col).then_inc(loaded, 16)
                    sp.dma_start(grow[:, :], g12).then_inc(loaded, 16)
                    sp.dma_start(wm[:, :, :], wmod.rearrange("(k p) n -> p k n", p=P)).then_inc(loaded, 16)
                    sp.wait_ge(loaded, 48)

                @block.scalar
                def _(act):
                    act.wait_ge(loaded, 48)
                    nc.scalar.activation(sc[:, :], cc[:, :], ACT.Silu).then_inc(silu_done, 1)
                    for n in range(4):
                        act.wait_ge(mod_done, n + 1)
                        if n < 3:
                            nc.scalar.copy(raw[:, cols(n)], pm[n][:, :]).then_inc(raw_done, 1)
                        else:
                            nc.scalar.copy(gains[:, :, :].rearrange("p a f -> p (a f)"), pm[n][:, :]).then_inc(raw_done, 1)

                @block.vector
                def _(dve_e):
                    nc.vector.memset(ones[:, :], 1.0).then_inc(ones_set, 1)
                    nc.vector.memset(neg_half[:, :], -0.5).then_inc(ones_set, 1)
                    dve_e.wait_ge(ones_set, 1)
                    dve_e.wait_ge(silu_done, 1)
                    for k in range(KD):
                        nc.vector.tensor_scalar(scb[:, k, :], ones[:, :], sc[:, k:k + 1], None, ALU.mult).then_inc(bc_done, 1)
                    dve_e.wait_ge(ident_in, 32)
                    nc.vector.tensor_copy(ident_b[:, :], ident_f[:, :])
                    nc.vector.tensor_scalar(neg_ident_b[:, :], ident_f[:, :], -1.0, None, ALU.mult)
                    nc.vector.tensor_copy(mask_k[:, :], msk[:, 0, :])
                    nc.vector.tensor_copy(mask_q[:, :], msk[:, 1, :])
                    dve_e.wait_ge(raw_done, 4)
                    r = raw[:, :].rearrange("p (v f) -> p v f", v=6)
                    for v in (0, 3):
                        nc.vector.tensor_copy(mod[:, v, :], r[:, v, :])
                    for v in (1, 4):
                        nc.vector.tensor_scalar(mod[:, v, :], r[:, v, :], 1.0, None, ALU.add)
                    for n, v in enumerate((2, 5)):
                        nc.vector.tensor_scalar(sign[:, n, :], r[:, v, :], 0.0, 2.0, ALU.is_ge, ALU.mult).then_inc(dve, 1)
                        dve_e.wait_ge(dve, 4 * n + 1)
                        nc.vector.tensor_scalar(sign[:, n, :], sign[:, n, :], -1.0, None, ALU.add).then_inc(dve, 1)
                        nc.vector.scalar_tensor_tensor(out=mod[:, v, :], in0=r[:, v, :], scalar=-1.0, in1=r[:, v, :],
                                                       op0=ALU.mult, op1=ALU.max).then_inc(dve, 1)
                        dve_e.wait_ge(dve, 4 * n + 3)
                        nc.vector.scalar_tensor_tensor(out=mod[:, v, :], in0=mod[:, v, :], scalar=0.25, in1=sign[:, n, :],
                                                       op0=ALU.max, op1=ALU.mult).then_inc(dve, 1)
                    dve_e.wait_ge(dve, 8)

                @block.tensor
                def _(pe):
                    pe.wait_ge(bc_done, KD)
                    for n in range(3):
                        for k in range(KD):
                            mm = nc.tensor.matmul(pm[n][:, :], scb[:, k, :], wm[:, k, cols(n)], start=(k == 0), stop=(k == KD - 1))
                        mm.then_inc(mod_done, 1)
                    nc.tensor.matmul(pm[3][:, :], ones[0:1, :], grow[:, :], start=True, stop=True).then_inc(mod_done, 1)

    def project(name, src, shift, scale, rms_gain, keep, w_dram, rope_dram, V, kv_heads, neg_half):
        KV = kv_heads * DH
        WK = max(KV, P)
        rope_units = [("q", n, P) for n in range(KD)] + [("k", n, min(KV, P)) for n in range(WK // P)]
        NR = len(rope_units)
        WN = w_dram.shape[1]
        off_k, off_qs, off_ks, off_v = D, D + WK, 2 * D + WK, 2 * D + 2 * WK
        products = ((0, 0), (0, 1), (1, 0))
        rms = rms_gain is not None
        with Space(name) as s:
            W = s.sb("W", [P, KD, WN])
            Wh, Wl = s.sb("Wh", [P, KD, WN], F32R), s.sb("Wl", [P, KD, WN], F32R)
            cos, sin = s.sb("cos", [P, T]), s.sb("sin", [P, T])
            xb, hb = s.sb("xb", [P, TPC, D]), s.sb("hb", [P, TPC, D])
            yb = s.sb("yb", [P, TPC, D]) if rms else hb
            st, mv = s.sb("st", [P, TPC, 6]), s.sb("mv", [P, TPC, 2])
            var, rstd, ssq, ms, rrms = (s.sb(n, [P, TPC]) for n in ("var", "rstd", "ssq", "ms", "rrms"))
            sq = s.sb("sq", [P, 2, D])
            hT = s.sb("hT", [P, KD, CHUNK])
            hTh, hTl = s.sb("hTh", [P, 2, KD, CHUNK], F32R), s.sb("hTl", [P, 2, KD, CHUNK], F32R)
            direct, crossed = s.sb("direct", [P, 2, CHUNK]), s.sb("crossed", [P, 2, CHUNK])
            turned, rest = s.sb("turned", [P, 2, CHUNK]), s.sb("rest", [P, 2, CHUNK])
            parts = s.sb("parts", [P, NR, PARTS, CHUNK], BF16)
            ps_t = s.ps("ps_t", [P, KD, CHUNK])
            ps_a = [s.ps(f"ps_a{n}", [P, CHUNK]) for n in range(2)]
            ps_b = [s.ps(f"ps_b{n}", [P, CHUNK]) for n in range(2)]
            ps_v = s.ps("ps_v", [P, TPC, D])
            w_in, tab_in, w_hi, w_lo = s.sem("w_in"), s.sem("tab_in"), s.sem("w_hi"), s.sem("w_lo")
            loaded, stats_done, aggr_done, var_done, rstd_done = (s.sem(n) for n in ("loaded", "stats_done", "aggr_done", "var_done", "rstd_done"))
            centred, scaled, shifted, kept = s.sem("centred"), s.sem("scaled"), s.sem("shifted"), s.sem("kept")
            squared, ms_done, rrms_done, normed = s.sem("squared"), s.sem("ms_done"), s.sem("rrms_done"), s.sem("normed")
            h_turned, h_out, h_hi, h_lo = s.sem("h_turned"), s.sem("h_out"), s.sem("h_hi"), s.sem("h_lo")
            unit_ready, rope_taken, v_ready, v_placed = s.sem("unit_ready"), s.sem("rope_taken"), s.sem("v_ready"), s.sem("v_placed")
            summed, part1, rest_done, part2, part3 = s.sem("summed"), s.sem("part1"), s.sem("rest_done"), s.sem("part2"), s.sem("part3")
            stored = [s.sem(f"stored{r}") for r in range(NR)]

            with nc.Block() as block:

                @block.sync
                def _(sp):
                    def load(c):
                        wait_apart(sp, centred, c * TPC + TPC)
                        sp.dma_start(xb[:, :, :], by_tile(src)[:, tiles(c), :]).then_inc(loaded, 16)

                    def load_tables(pair):
                        if pair:
                            sp.wait_ge(tab_in, pair * 32)
                        there = slice(pair * 2 * CHUNK, (pair + 1) * 2 * CHUNK)
                        sp.dma_start(cos[:, there], rope_dram[0][:, there]).then_inc(tab_in, 16)
                        sp.dma_start(sin[:, there], rope_dram[1][:, there]).then_inc(tab_in, 16)

                    def keep_h(c):
                        wait_apart(sp, shifted, c + 1)
                        sp.dma_start(by_tile(keep)[:, tiles(c), :], hb[:, :, :]).then_inc(kept, 16)

                    def period(c, par, whole):
                        for r, (kind, n, M) in enumerate(rope_units):
                            dst = (q_dram if kind == "q" else k_dram)[:, n * P:n * P + M, cols(c)]
                            wait_apart(sp, part3, c * NR + r + 3)
                            sp.dma_start(dst.rearrange("a f t -> f a t"), parts[0:M, r, :, :]).then_inc(stored[r], 16)
                            if r == 0 and exists(c, whole, 3):
                                load(c + 3)
                            if r == 1 and keep is not None and exists(c, whole, 2):
                                keep_h(c + 2)

                    load(0)
                    sp.dma_start(W[:, :, :], w_dram.rearrange("(k p) n -> p k n", p=P)).then_inc(w_in, 16)
                    load(1)
                    if keep is not None:
                        keep_h(0)
                    for r in range(NR):
                        sp.nop().then_inc(stored[r], 16)
                    load_tables(0)
                    load(2)
                    if keep is not None:
                        keep_h(1)
                    for pair in range(1, NCH // 2):
                        load_tables(pair)
                    by_pairs(sp, period, NCH // 2)
                    for r in range(NR):
                        sp.wait_ge(stored[r], 16 * NCH + 16)
                    if keep is not None:
                        sp.wait_ge(kept, 16 * NCH)

                @block.gpsimd
                def _(pool):
                    def deviation(c):
                        wait_apart(pool, aggr_done, c * TPC + TPC)
                        nc.gpsimd.tensor_scalar(var[:, :], mv[:, :, 1], LN_EPS, None, ALU.add).then_inc(var_done, 1)
                        pool.wait_ge(var_done, c + 1)
                        nc.gpsimd.tensor_tensor(rstd[:, :], var[:, :], neg_half[:, 0:TPC], ALU.pow).then_inc(rstd_done, 1)

                    def add_shift(c):
                        pool.wait_ge(scaled, c + 1)
                        nc.gpsimd.tensor_tensor(hb[:, :, :], hb[:, :, :], row_bcast(shift, TPC), ALU.add).then_inc(shifted, 1)

                    def root(c):
                        if rms:
                            wait_apart(pool, squared, c * TPC + TPC + 2)
                            wait_apart(pool, normed, c * TPC + TPC)
                            nc.gpsimd.tensor_scalar(ms[:, :], ssq[:, :], 1.0 / D, RMS_EPS, ALU.mult, ALU.add).then_inc(ms_done, 1)
                            pool.wait_ge(ms_done, c + 2)
                            nc.gpsimd.tensor_tensor(rrms[:, :], ms[:, :], neg_half[:, 0:TPC], ALU.pow).then_inc(rrms_done, 1)

                    def period(c, par, whole):
                        ahead = exists(c, whole, 2)
                        if ahead:
                            deviation(c + 2)
                        for r in range(NR + 1):
                            if r < NR:
                                M, slot, N = rope_units[r][2], (par * NR + r) % 2, c * NR + r
                                pool.wait_ge(rope_taken, N + 3)
                                pool.wait_ge(rest_done, N + 1)
                                nc.gpsimd.tensor_tensor(turned[0:M, slot, :], direct[0:M, slot, :], crossed[0:M, slot, :], ALU.add).then_inc(summed, 1)
                            if r == 0 and ahead:
                                add_shift(c + 2)
                            if r == 2 and ahead:
                                root(c + 2)
                            if r >= 1:
                                M, slot, N = rope_units[r - 1][2], (par * NR + r - 1) % 2, c * NR + r - 1
                                pool.wait_ge(part2, N + 1)
                                nc.gpsimd.tensor_tensor(parts[0:M, r - 1, 2, :], rest[0:M, slot, :], parts[0:M, r - 1, 1, :],
                                                        ALU.subtract).then_inc(part3, 1)

                    pool.nop().then_inc(summed, 2)
                    pool.nop().then_inc(part3, 2)
                    if rms:
                        pool.nop().then_inc(ms_done, 1)
                    for c in range(2):
                        deviation(c)
                        add_shift(c)
                        root(c)
                    by_pairs(pool, period, NCH - 2)

                @block.scalar
                def _(act):
                    def squares(c):
                        if rms:
                            act.wait_ge(shifted, c + 1)
                            act.wait_ge(ms_done, c + 1)
                            for j in range(TPC):
                                act.wait_ge(squared, c * TPC + j + 1)
                                nc.scalar.activation(sq[:, j % 2, :], hb[:, j, :], ACT.Square, accum_out=ssq[:, j:j + 1]).then_inc(squared, 1)

                    def split_high(c, par):
                        act.wait_ge(h_turned, c + 2)
                        act.wait_ge(h_lo, c + 1)
                        nc.scalar.copy(hT[:, :, :], ps_t[:, :, :]).then_inc(h_out, 1)
                        act.wait_ge(h_out, c + 2)
                        act.wait_ge(v_ready, c + 1)
                        nc.scalar.copy(hTh[:, par, :, :], hT[:, :, :]).then_inc(h_hi, 1)

                    def period(c, par, whole):
                        if exists(c, whole, 1):
                            split_high(c + 1, 1 - par)
                        for r in range(NR + 1):
                            if r < NR:
                                M, slot, N = rope_units[r][2], (par * NR + r) % 2, c * NR + r
                                act.wait_ge(summed, N + 3)
                                act.wait_ge(stored[r], c * 16 + 16)
                                nc.scalar.copy(parts[0:M, r, 0, :], turned[0:M, slot, :]).then_inc(part1, 1)
                            if r >= 1:
                                M, slot, N = rope_units[r - 1][2], (par * NR + r - 1) % 2, c * NR + r - 1
                                act.wait_ge(rest_done, N + 3)
                                nc.scalar.copy(parts[0:M, r - 1, 1, :], rest[0:M, slot, :]).then_inc(part2, 1)
                            if r == 1 and exists(c, whole, 2):
                                squares(c + 2)
                        act.wait_ge(v_ready, c + 3)
                        nc.scalar.copy(V[:, tiles(c), 0:KV], ps_v[:, :, 0:KV]).then_inc(v_placed, 1)

                    act.nop().then_inc(v_placed, 1)
                    act.nop().then_inc(h_out, 1)
                    if rms:
                        act.nop().then_inc(squared, 2)
                    act.wait_ge(w_in, 16)
                    nc.scalar.copy(Wh[:, :, :], W[:, :, :]).then_inc(w_hi, 1)
                    squares(0)
                    split_high(0, 0)
                    squares(1)
                    by_pairs(act, period, NCH - 2)

                @block.vector
                def _(dve):
                    def stats(c):
                        dve.wait_ge(loaded, c * 16 + 16)
                        for j in range(TPC):
                            nc.vector.bn_stats(st[:, j, :], xb[:, j, :]).then_inc(stats_done, 1)
                        for j in range(TPC):
                            wait_apart(dve, stats_done, c * TPC + j + 1)
                            nc.vector.bn_aggr(mv[:, j, :], st[:, j, :]).then_inc(aggr_done, 1)

                    def centre_and_scale(c):
                        dve.wait_ge(rstd_done, c + 1)
                        if rms:
                            dve.wait_ge(normed, c * TPC + TPC)
                            if not isinstance(c, int) or c:
                                dve.wait_ge(kept, c * 16)
                        else:
                            dve.wait_ge(h_turned, c + 1)
                        for j in range(TPC):
                            nc.vector.tensor_scalar(hb[:, j, :], xb[:, j, :], mv[:, j, 0:1], rstd[:, j:j + 1], ALU.subtract, ALU.mult).then_inc(centred, 1)
                        dve.wait_ge(centred, c * TPC + 2 * TPC)
                        nc.vector.tensor_tensor(hb[:, :, :], hb[:, :, :], row_bcast(scale, TPC), ALU.mult).then_inc(scaled, 1)

                    def apply_rms(c):
                        if rms:
                            dve.wait_ge(rrms_done, c + 1)
                            dve.wait_ge(h_turned, c + 1)
                            for j in range(TPC):
                                nc.vector.scalar_tensor_tensor(out=yb[:, j, :], in0=hb[:, j, :], scalar=rrms[:, j:j + 1], in1=rms_gain,
                                                               op0=ALU.mult, op1=ALU.mult).then_inc(normed, 1)

                    def split_low(c, par):
                        dve.wait_ge(h_hi, c + 1)
                        nc.vector.tensor_tensor(hTl[:, par, :, :], hT[:, :, :], hTh[:, par, :, :].bitcast(F32), ALU.subtract).then_inc(h_lo, 1)

                    def period(c, par, whole):
                        ahead = exists(c, whole, 2)
                        if exists(c, whole, 1):
                            apply_rms(c + 1)
                        if ahead:
                            stats(c + 2)
                        if par == 0:
                            dve.wait_ge(tab_in, c * 16 + 32)
                        for r in range(NR + 1):
                            if r < NR:
                                M, slot, N = rope_units[r][2], (par * NR + r) % 2, c * NR + r
                                dve.wait_ge(unit_ready, N + 1)
                                dve.wait_ge(summed, N + 1)
                                nc.vector.tensor_tensor(direct[0:M, slot, :], ps_a[slot][0:M, :], cos[0:M, cols(c)], ALU.mult)
                                nc.vector.tensor_tensor(crossed[0:M, slot, :], ps_b[slot][0:M, :], sin[0:M, cols(c)], ALU.mult).then_inc(rope_taken, 1)
                            if r == 0 and ahead:
                                centre_and_scale(c + 2)
                            if r == 2 and exists(c, whole, 1):
                                split_low(c + 1, 1 - par)
                            if r >= 1:
                                M, slot, N = rope_units[r - 1][2], (par * NR + r - 1) % 2, c * NR + r - 1
                                dve.wait_ge(part1, N + 1)
                                dve.wait_ge(part3, N + 1)
                                nc.vector.tensor_tensor(rest[0:M, slot, :], turned[0:M, slot, :], parts[0:M, r - 1, 0, :],
                                                        ALU.subtract).then_inc(rest_done, 1)

                    dve.nop().then_inc(rope_taken, 2)
                    dve.nop().then_inc(rest_done, 2)
                    dve.nop().then_inc(centred, TPC)
                    dve.nop().then_inc(h_lo, 1)
                    if rms:
                        dve.nop().then_inc(normed, TPC)
                    stats(0)
                    centre_and_scale(0)
                    dve.wait_ge(w_hi, 1)
                    nc.vector.tensor_tensor(Wl[:, :, :], W[:, :, :], Wh[:, :, :].bitcast(F32), ALU.subtract).then_inc(w_lo, 1)
                    apply_rms(0)
                    stats(1)
                    centre_and_scale(1)
                    split_low(0, 0)
                    by_pairs(dve, period, NCH - 2)

                @block.tensor
                def _(pe):
                    def turn(c):
                        if rms:
                            pe.wait_ge(normed, c * TPC + 2 * TPC)
                        else:
                            pe.wait_ge(shifted, c + 1)
                        pe.wait_ge(h_out, c + 1)
                        for k in range(KD):
                            for j in range(TPC):
                                tr = nc.tensor.transpose(ps_t[:, k, j * P:(j + 1) * P], yb[:, j, k * P:(k + 1) * P], ident_f[:, :])
                        tr.then_inc(h_turned, 1)

                    def split_product(out, lhs, rhs):
                        for k in range(KD):
                            for a, b in products:
                                mm = nc.tensor.matmul(out, lhs(a, k), rhs(b, k), start=(k == 0 and (a, b) == products[0]),
                                                      stop=(k == KD - 1 and (a, b) == products[-1]))
                        return mm

                    def period(c, par, whole):
                        pe.wait_ge(h_lo, c + 2)
                        for r, (kind, n, M) in enumerate(rope_units):
                            slot, N = (par * NR + r) % 2, c * NR + r
                            pe.wait_ge(rope_taken, N + 1)
                            for bank, at in ((ps_a, (0 if kind == "q" else off_k) + n * P), (ps_b, (off_qs if kind == "q" else off_ks) + n * P)):
                                mm = split_product(bank[slot][:, :], lambda a, k: (Wh, Wl)[a][:, k, at:at + P], lambda b, k: (hTh, hTl)[b][:, par, k, :])
                            mm.then_inc(unit_ready, 1)
                            if r == 0 and exists(c, whole, 1):
                                turn(c + 1)
                        pe.wait_ge(v_placed, c + 1)
                        for j in range(TPC):
                            mm = split_product(ps_v[:, j, 0:KV], lambda a, k: (hTh, hTl)[a][:, par, k, j * P:(j + 1) * P],
                                               lambda b, k: (Wh, Wl)[b][:, k, off_v:off_v + KV])
                        mm.then_inc(v_ready, 1)

                    pe.nop().then_inc(h_turned, 1)
                    pe.nop().then_inc(v_ready, 2)
                    turn(0)
                    pe.wait_ge(w_lo, 1)
                    by_pairs(pe, period, NCH - 2)

    def attention(name, V, A, kv_heads):
        KH = GROUP if kv_heads == HEADS else 1
        VC = KH * DH
        LAST = NCH - 1
        super0 = [c * (c + 1) // 2 for c in range(NCH + 1)]
        SUPERS = super0[NCH]
        LEAD = NCH + 1
        PAIRS = GROUP // 2
        n_qdma = len(Q_PART)
        places = [(c, k) for c in range(NCH) for k in range(c + 1)]
        places += [(NCH + c, k) for c, k in places[:LEAD]]

        class Step:

            def __init__(self, index, units, waiting):
                self.index, self.count = index, 1
                self.c, self.k = places[index] if index is not None else (None, None)
                self.units = [units[len(units) * i // TPC:len(units) * (i + 1) // TPC] for i in range(TPC)]
                self.turned, self.ends = [], False
                for block in self.units:
                    self.turned.append(waiting)
                    waiting = None
                    for m, j in block:
                        if ends_chunk(m, j):
                            waiting, self.ends = places[m][0], True
                self.waiting = waiting

            def follows(self, other):
                if self.index is None or self.ends or other.ends or any(t is not None for t in self.turned + other.turned):
                    return False
                n = other.count
                if self.c != other.c or other.k == 0 or [len(u) for u in self.units] != [len(u) for u in other.units]:
                    return False
                pairs = [(a, b) for x, y in zip(self.units, other.units) for a, b in zip(x, y)]
                return all(a[0] == b[0] + n and a[1] == b[1] and places[a[0]][0] == places[b[0]][0] and places[b[0]][1] > 0
                           for a, b in pairs)

        def ends_chunk(m, j):
            c, k = places[m]
            return k == c % NCH and j == TPC - 1

        def turns_output(step, b):
            return step.k == 0 and step.c > 0 and b == 1

        def max_beside(index, more):
            m = index + LEAD
            return [(m, j) for j in range(TPC)] if more or m < SUPERS else []

        def group_steps(more):
            steps, waiting = [], None
            for index in range(SUPERS):
                step = Step(index, max_beside(index, more), waiting)
                waiting = step.waiting
                if steps and step.follows(steps[-1]):
                    steps[-1].count += 1
                else:
                    steps.append(step)
            return steps

        def first_steps():
            steps, waiting = [], None
            for m in range(LEAD):
                steps.append(Step(None, [(m, j) for j in range(TPC)], waiting))
                waiting = steps[-1].waiting
            return steps

        def run(eng, group):
            with eng.Fori(0, NGROUPS - 1) as g:
                group(g, True)
            group(NGROUPS - 1, False)

        def over(eng, step, supers, body):
            if step.count == 1:
                body(supers, 0)
            else:
                with eng.Fori(0, step.count) as i:
                    body(eng.snap(supers + i), i)

        def reg(eng, value):
            return value if isinstance(value, int) else eng.snap(value)

        def own(eng, value, most):
            if isinstance(value, int):
                return value
            r = eng.alloc_register()
            eng.reg_mov(r, value)
            return eng.snap(r, donate=True, min_val=0, max_val=most)

        first_turns = sum(t is not None for step in first_steps() for t in step.turned)
        group_turns = sum(t is not None for step in group_steps(True) for t in step.turned) + NCH

        class Turns:

            def __init__(self, base, count):
                self.base, self.count = base, count

            def before(self):
                self.count += 1
                return self.base + (self.count - 1)

        with Space(name) as s:
            K = s.sb("K", [ROWS_M, 2 * KH, T], BF16)
            Q = s.sb("Q", [ROWS_M, NCH * GROUP, CHUNK], BF16)
            prob = s.sb("prob", [P, 2, GROUP, CHUNK])
            v_now = s.sb("v_now", [P, 2, KH, 32])
            o_sb = s.sb("o_sb", [P, CHUNK])
            part_max = s.sb("part_max", [P, GROUP, TPC, NCH])
            row_max = s.sb("row_max", [P, GROUP * TPC])
            max_hl = s.sb("max_hl", [P, 2, GROUP * TPC], BF16)
            rows_sb = s.sb("rows_sb", [2 * GROUP * TPC, P], BF16)
            recip = s.sb("recip", [P, TPC, GROUP])
            sT = [s.ps(f"sT{n}", [P, 2, CHUNK]) for n in range(PAIRS)]
            s_max = [s.ps(f"s_max{n}", [P, CHUNK]) for n in range(2)]
            o_acc = s.ps("o_acc", [P, CHUNK])
            tok = s.ps("tok", [P, TPC, P])
            k_in, q_in = s.sem("k_in"), s.sem("q_in")
            ones_set, v_clear, v_staged = s.sem("ones_set"), s.sem("v_clear"), s.sem("v_staged")
            scores_ready, exp_done, pv_done = s.sem("scores_ready"), s.sem("exp_done"), s.sem("pv_done")
            max_scores, max_taken, max_final = s.sem("max_scores"), s.sem("max_taken"), s.sem("max_final")
            hi_done, max_split, rows_turned, rows_in = s.sem("hi_done"), s.sem("max_split"), s.sem("rows_turned"), s.sem("rows_in")
            o_copied, o_turned, recip_done, tok_used = s.sem("o_copied"), s.sem("o_turned"), s.sem("recip_done"), s.sem("tok_used")

            def kh(h):
                return h if KH == GROUP else 0

            with nc.Block() as block:

                @block.sync
                def _(sp):
                    def load_k(g, slot, start, count):
                        for b, part in enumerate(K_PART):
                            src = k_dram[part].rearrange("(h d) t -> d h t", d=DH)[:, bass.ds(g * KH, KH), start:start + count]
                            sp.dma_start(K[b * DH:(b + 1) * DH, bass.ds(slot * KH, KH), start:start + count], src).then_inc(k_in, 16)

                    def load_q(g, c):
                        for b, part in enumerate(Q_PART):
                            src = q_dram[part].rearrange("(h d) t -> d h t", d=DH)[:, bass.ds(g * GROUP, GROUP), c * CHUNK:(c + 1) * CHUNK]
                            sp.dma_start(Q[b * DH:(b + 1) * DH, c * GROUP:(c + 1) * GROUP, :], src).then_inc(q_in, 16)

                    def place_rows(n, c, turns):
                        if not isinstance(n, int) or n:
                            wait_apart(sp, rows_in, n * 32)
                        wait_apart(sp, tok_used, turns.before() + 2)
                        for part in range(2):
                            rows = rows_sb[part * GROUP * TPC:(part + 1) * GROUP * TPC, :]
                            dst = Q[ROWS + part:ROWS + part + 1, c * GROUP:(c + 1) * GROUP, :].rearrange("a h (q t) -> a (h q) t", q=TPC)
                            sp.dma_start(dst, rows).then_inc(rows_in, 16)

                    turns = Turns(0, 0)
                    to_place = [c for step in first_steps() for c in step.turned if c is not None]
                    for c in range(NCH):
                        if c:
                            sp.wait_ge(q_in, c * 16 * n_qdma)
                            sp.wait_ge(k_in, c * 16 * len(K_PART))
                        load_k(0, 0, c * CHUNK, CHUNK)
                        load_q(0, c)
                        if c > places[LEAD - 1][0] and to_place:
                            place_rows(to_place[0], to_place[0], turns)
                            del to_place[0]
                    assert not to_place

                    def group(g, more):
                        turns = Turns(reg(sp, g * group_turns), first_turns)
                        if more:
                            wait_apart(sp, k_in, (g + NCH) * 16 * len(K_PART))
                            load_k(g + 1, (g + 1) % 2, 0, T)
                        for step in group_steps(more):
                            for b, c in enumerate(step.turned):
                                if turns_output(step, b):
                                    turns.before()
                                    if more:
                                        reload_q(g, step.c - 1)
                                if c is not None:
                                    place_rows(g * NCH + c, c % NCH, turns)
                        if more:
                            reload_q(g, LAST)

                    def reload_q(g, c):
                        n = g * NCH + c
                        wait_apart(sp, o_copied, n + 2)
                        wait_apart(sp, q_in, (n + NCH) * 16 * n_qdma)
                        load_q(g + 1, c)

                    run(sp, group)

                @block.gpsimd
                def _(pool):
                    nc.gpsimd.memset(v_now[:, :, :, :], 0.0).then_inc(v_clear, 1)
                    pool.wait_ge(v_clear, 1)
                    nc.gpsimd.memset(v_now[:, :, :, DH:DH + 1], 1.0).then_inc(v_clear, 1)
                    pool.wait_ge(v_clear, 2)
                    nc.gpsimd.memset(K[ROWS:ROWS_M, :, :].bitcast(F32), PAIR_OF_ONES).then_inc(ones_set, 1)
                    pool.wait_ge(ones_set, 1)

                    def stage_v(g, block_of_keys, slot, unit):
                        wait_apart(pool, pv_done, unit.of(1, 1))
                        nc.gpsimd.tensor_copy(
                            v_now[:, slot, :, 0:DH],
                            V[:, bass.ds(block_of_keys, 1), bass.ds(g * VC, VC)].rearrange("p a (h d) -> p (a h) d", d=DH)).then_inc(v_staged, 1)

                    with pool.Fori(0, NGROUPS) as g:
                        for c in range(NCH):
                            supers = pool.snap(g * SUPERS + super0[c])
                            for n in range(TPC):
                                stage_v(g, TPC * c + TPC - 1 - n, n % 2, Blocks(supers, n))
                            if c:
                                with pool.Fori(0, c) as sb:
                                    now = pool.snap(supers + sb)
                                    for j in range(TPC):
                                        stage_v(g, sb * TPC + j, j % 2, Blocks(now, TPC + j))

                @block.scalar
                def _(act):
                    def exps(unit, slot, off):
                        for p in range(PAIRS):
                            act.wait_ge(scores_ready, unit.of(PAIRS, p + 1))
                            act.wait_ge(pv_done, unit.of(1, 1))
                            nc.scalar.activation(prob[:, slot, 2 * p:2 * p + 2, off:CHUNK], sT[p][:, :, off:CHUNK], ACT.Exp,
                                                 scale=DH ** -0.5).then_inc(exp_done, 1)

                    def copy_o(n, end):
                        act.wait_ge(pv_done, end.of(1, 2))
                        act.wait_ge(o_turned, n + 1)
                        nc.scalar.copy(o_sb[:, :], o_acc[:, :]).then_inc(o_copied, 1)

                    act.nop().then_inc(o_copied, 1)
                    act.nop().then_inc(exp_done, PAIRS)
                    with act.Fori(0, NGROUPS) as g:
                        for c in range(NCH):
                            supers, chunks = act.snap(g * SUPERS + super0[c]), act.snap(g * NCH + c)
                            for n in range(TPC):
                                exps(Blocks(supers, n), n % 2, (TPC - 1 - n) * P)
                                if n == 0 and c:
                                    copy_o(chunks - 1, Blocks(supers, 0))
                            if c:
                                with act.Fori(0, c) as sb:
                                    now = act.snap(supers + sb)
                                    for j in range(TPC):
                                        exps(Blocks(now, TPC + j), j % 2, 0)
                        copy_o(chunks, Blocks(supers, TPC * NCH))

                @block.vector
                def _(dve):
                    def max_unit(supers, i, chunks, m, j):
                        c, k = places[m]
                        width, sb = ((j + 1) * P, c % NCH) if k == 0 else (CHUNK, i + k - 1)
                        for h in range(GROUP):
                            dve.wait_ge(max_scores, Blocks(supers, TPC * m + j).of(GROUP, h + 1))
                            nc.vector.reduce_max(part_max[:, h, j, bass.ds(sb, 1)], s_max[h % 2][:, 0:width], AX.X).then_inc(max_taken, 1)
                        if ends_chunk(m, j):
                            n = chunks + c
                            dve.wait_ge(max_taken, Blocks(supers, TPC * (m + 1)).of(GROUP, 2))
                            dve.wait_ge(rows_turned, n + 1)
                            nc.vector.reduce_max(row_max[:, :], part_max[:, :, :, 0:c % NCH + 1].rearrange("p h q s -> p (h q) s"),
                                                 AX.X).then_inc(max_final, 1)
                            dve.wait_ge(max_final, n + 1)
                            nc.vector.tensor_copy(max_hl[:, 0, :], row_max[:, :]).then_inc(hi_done, 1)
                            dve.wait_ge(hi_done, n + 1)
                            nc.vector.tensor_tensor(max_hl[:, 1, :], row_max[:, :], max_hl[:, 0, :], ALU.subtract).then_inc(max_split, 1)

                    def take_rows(n):
                        dve.wait_ge(rows_turned, n + 2)
                        if not isinstance(n, int) or n:
                            dve.wait_ge(rows_in, n * 32)
                        nc.vector.tensor_copy(rows_sb[:, :], tok[0:2 * GROUP * TPC, 0, :]).then_inc(tok_used, 1)

                    def place_o(n, g, c):
                        dve.wait_ge(o_turned, n + 2)
                        o = tok[:, :, :].rearrange("p q (h d) -> p q h d", h=GROUP)
                        nc.vector.reciprocal(recip[:, :, :], o[:, :, :, DH]).then_inc(recip_done, 1)
                        dve.wait_ge(recip_done, n + 1)
                        dst = A[:, c * TPC:(c + 1) * TPC, bass.ds(g * GROUP * DH, GROUP * DH)].rearrange("p q (h d) -> p q h d", h=GROUP)
                        nc.vector.tensor_tensor(dst, o[:, :, :, 0:DH], recip[:, :, :].unsqueeze(3).to_broadcast([P, TPC, GROUP, DH]),
                                                ALU.mult).then_inc(tok_used, 1)

                    def blocks(supers, i, g, chunks, step):
                        for b in range(TPC):
                            for m, j in step.units[b]:
                                max_unit(supers, i, chunks, m, j)
                            if turns_output(step, b):
                                place_o(chunks + (step.c - 1), g, step.c - 1)
                            if step.turned[b] is not None:
                                take_rows(chunks + step.turned[b])

                    dve.nop().then_inc(max_taken, 2)
                    dve.nop().then_inc(tok_used, 1)
                    for step in first_steps():
                        blocks(0, 0, 0, 0, step)

                    def group(g, more):
                        for step in group_steps(more):
                            supers, chunks = reg(dve, g * SUPERS), reg(dve, g * NCH)
                            if any(step.units) or step.k == 0 or any(t is not None for t in step.turned):
                                over(dve, step, supers, lambda now, i: blocks(now, i, g, chunks, step))
                        place_o(chunks + LAST, g, LAST)

                    run(dve, group)

                @block.tensor
                def _(pe):
                    def max_tile(k_slots, supers, i, m, j, h):
                        c, k = places[m]
                        q = Q[0:ROWS, c % NCH * GROUP + h, j * P:(j + 1) * P]
                        width, sb = ((j + 1) * P, c % NCH) if k == 0 else (CHUNK, i + k - 1)
                        keys = K[0:ROWS, bass.ds(k_slots[c // NCH] + kh(h), 1), bass.ds(sb * CHUNK, width)].rearrange("r a k -> r (a k)")
                        pe.wait_ge(max_taken, Blocks(supers, TPC * m + j).of(GROUP, h + 1))
                        mm = nc.tensor.matmul(s_max[h % 2][:, 0:width], q, keys, start=True, stop=k > 0)
                        if k == 0:
                            mm = nc.tensor.matmul(s_max[h % 2][:, width - P:width], ident_b[:, :], mask_q[:, :], start=False, stop=True)
                        mm.then_inc(max_scores, 1)

                    def scores(k_slot, unit, c, block_of_keys, off, p, diag):
                        pe.wait_ge(exp_done, unit.of(PAIRS, p + 1))
                        for hh in range(2):
                            h = 2 * p + hh
                            k = K[:, bass.ds(k_slot + kh(h), 1), bass.ds(block_of_keys * P, P)].rearrange("r a k -> r (a k)")
                            mm = nc.tensor.matmul(sT[p][:, hh, off:CHUNK], k, Q[:, c * GROUP + h, off:CHUNK], start=True, stop=not diag)
                            if diag:
                                mm = nc.tensor.matmul(sT[p][:, hh, off:off + P], ident_b[:, :], mask_k[:, :], start=False, stop=True)
                        mm.then_inc(scores_ready, 1)

                    def values(unit, slot, a, b, first, last):
                        if first is not None:
                            pe.wait_ge(o_copied, first + 1)
                        pe.wait_ge(exp_done, unit.of(PAIRS, PAIRS + 2))
                        pe.wait_ge(v_staged, unit.of(1, 1))
                        for h in range(GROUP):
                            mm = nc.tensor.matmul(o_acc[32 * h:32 * h + 32, a:b], v_now[:, slot, kh(h), :], prob[:, slot, h, a:b],
                                                  start=first is not None, stop=True, skip_group_check=True)
                        if last:
                            mm.then_inc(pv_done, 1)

                    def blocks(supers, i, groups, chunks, k_slots, step):
                        for b in range(TPC):
                            tiles_beside = [(m, j, h) for m, j in step.units[b] for h in range(GROUP)]
                            for m, j, h in tiles_beside:
                                c, k = places[m]
                                if (k, j, h) == (0, 0, 0):
                                    pe.wait_ge(q_in, (chunks + c) * (16 * n_qdma) + 16 * n_qdma)
                                    if step.index is None:
                                        pe.wait_ge(k_in, (c + 1) * 16 * len(K_PART))
                                    elif c == NCH:
                                        pe.wait_ge(k_in, (groups + (NCH + 1)) * (16 * len(K_PART)))

                            def maxima(quarter):
                                n = len(tiles_beside)
                                for m, j, h in tiles_beside[n * quarter // 4:n * (quarter + 1) // 4]:
                                    max_tile(k_slots, supers, i, m, j, h)

                            if step.index is None:
                                for quarter in range(4):
                                    maxima(quarter)
                            else:
                                unit = TPC * step.index + b
                                diag = step.k == 0
                                key_block = step.c * TPC + TPC - 1 - b if diag else i * TPC + (TPC * (step.k - 1) + b)
                                off = (TPC - 1 - b) * P if diag else 0
                                has_before = b > 0 or not diag or step.c > 0
                                before_off = off + P if diag and b > 0 else 0
                                mid = CHUNK // 2 if before_off < CHUNK // 2 else CHUNK
                                first = chunks + step.c if diag and b == 1 else None
                                maxima(0)
                                scores(k_slots[0], Blocks(supers, unit), step.c, key_block, off, 0, diag)
                                maxima(1)
                                if has_before:
                                    values(Blocks(supers, unit - 1), (b + 1) % 2, before_off, mid, first, mid == CHUNK)
                                maxima(2)
                                scores(k_slots[0], Blocks(supers, unit), step.c, key_block, off, 1, diag)
                                maxima(3)
                                if has_before and mid < CHUNK:
                                    values(Blocks(supers, unit - 1), (b + 1) % 2, mid, CHUNK, None, True)
                                if turns_output(step, b):
                                    turn_o(chunks + (step.c - 1))
                            if step.turned[b] is not None:
                                turn_rows(chunks + step.turned[b])

                    def turn_rows(n):
                        pe.wait_ge(max_split, n + 1)
                        pe.wait_ge(tok_used, turns.before() + 1)
                        nc.tensor.matmul(tok[0:2 * GROUP * TPC, 0, :], max_hl[:, :, :].rearrange("p a n -> p (a n)"), neg_ident_b[:, :],
                                         start=True, stop=True).then_inc(rows_turned, 1)

                    def turn_o(n):
                        pe.wait_ge(o_copied, n + 2)
                        pe.wait_ge(tok_used, turns.before() + 1)
                        for q in range(TPC):
                            tr = nc.tensor.transpose(tok[:, q, :], o_sb[:, q * P:(q + 1) * P], ident_f[:, :])
                        tr.then_inc(o_turned, 1)

                    pe.nop().then_inc(rows_turned, 1)
                    pe.nop().then_inc(pv_done, 2)
                    pe.nop().then_inc(o_turned, 1)
                    turns = Turns(0, 0)
                    for step in first_steps():
                        blocks(0, 0, 0, 0, (0, KH), step)
                    pe.wait_ge(k_in, NCH * 16 * len(K_PART))
                    pe.wait_ge(ones_set, 1)

                    def group(g, more):
                        nonlocal turns
                        turns = Turns(reg(pe, g * group_turns), first_turns)
                        for step in group_steps(more):
                            supers, chunks = reg(pe, g * SUPERS), reg(pe, g * NCH)
                            k_slots = own(pe, g % 2 * KH, KH), own(pe, (g + 1) % 2 * KH, KH)
                            if step.k == 0:
                                pe.wait_ge(rows_in, (chunks + step.c) * 32 + 32)
                            over(pe, step, supers, lambda now, i: blocks(now, i, g, chunks, k_slots, step))
                        end = Blocks(supers, TPC * SUPERS - 1)
                        values(end, (TPC - 1) % 2, 0, CHUNK // 2, None, False)
                        values(end, (TPC - 1) % 2, CHUNK // 2, CHUNK, None, True)
                        turn_o(chunks + LAST)

                    run(pe, group)

    def out_projection(name, A, w_dram, gain, base_dram, X, keep):
        with Space(name) as s:
            W = s.sb("W", [P, KD, D])
            As = s.sb("As", [P, 2, TPC, D])
            aT = s.sb("aT", [P, 2, KD, CHUNK])
            gain_out = s.sb("gain_out", [P, TPC, D])
            ps_t = [s.ps(f"ps_t{n}", [P, KD, CHUNK]) for n in range(2)]
            ps_o = [s.ps(f"ps_o{n}", [P, TPC, D]) for n in range(2)]
            w_in, loaded, staged, turned, aT_ready = s.sem("w_in"), s.sem("loaded"), s.sem("staged"), s.sem("turned"), s.sem("aT_ready")
            product, taken, added, stored = s.sem("product"), s.sem("taken"), s.sem("added"), s.sem("stored")
            with nc.Block() as block:

                @block.sync
                def _(sp):
                    sp.dma_start(W[:, :, :], w_dram.rearrange("(k p) n -> p k n", p=P)).then_inc(w_in, 16)
                    with sp.Fori(0, NCH) as c:
                        sp.dma_start(X[:, tiles(c), :], by_tile(base_dram)[:, tiles(c), :]).then_inc(loaded, 16)
                        wait_apart(sp, loaded, c * 16 + 16)
                    if keep is not None:
                        with sp.Fori(0, NCH) as c:
                            wait_apart(sp, added, c + 2)
                            sp.dma_start(by_tile(keep)[:, tiles(c), :], X[:, tiles(c), :]).then_inc(stored, 16)
                        sp.wait_ge(stored, 16 * NCH)

                @block.gpsimd
                def _(pool):
                    def period(c, par, whole):
                        wait_apart(pool, turned, c + 1)
                        nc.gpsimd.tensor_copy(As[:, par, :, :], A[:, tiles(c), :]).then_inc(staged, 1)

                    by_pairs(pool, period, NCH)

                @block.scalar
                def _(act):
                    def period(c, par, whole):
                        act.wait_ge(turned, c + 3)
                        act.wait_ge(product, c + 1)
                        nc.scalar.copy(aT[:, par, :, :], ps_t[par][:, :, :]).then_inc(aT_ready, 1)

                    act.nop().then_inc(aT_ready, 2)
                    by_pairs(act, period, NCH)

                @block.vector
                def _(dve):
                    def period(c, par, whole):
                        dve.wait_ge(product, c + 3)
                        dve.wait_ge(added, c + 1)
                        if gain is not None:
                            nc.vector.tensor_tensor(gain_out[:, :, :], ps_o[par][:, :, :], row_bcast(gain, TPC), ALU.mult).then_inc(taken, 1)
                            dve.wait_ge(taken, c + 3)
                            dve.wait_ge(loaded, c * 16 + 16)
                            nc.vector.tensor_tensor(X[:, tiles(c), :], gain_out[:, :, :], X[:, tiles(c), :], ALU.add).then_inc(added, 1)
                        else:
                            dve.wait_ge(loaded, c * 16 + 16)
                            nc.vector.tensor_tensor(X[:, tiles(c), :], ps_o[par][:, :, :], X[:, tiles(c), :], ALU.add).then_inc(added, 1)

                    dve.nop().then_inc(added, 1)
                    if gain is not None:
                        dve.nop().then_inc(taken, 2)
                    by_pairs(dve, period, NCH)

                @block.tensor
                def _(pe):
                    def turn(c, par):
                        pe.wait_ge(staged, c + 1)
                        pe.wait_ge(aT_ready, c + 1)
                        for k in range(KD):
                            for j in range(TPC):
                                tr = nc.tensor.transpose(ps_t[par][:, k, j * P:(j + 1) * P], As[:, par, j, k * P:(k + 1) * P], ident_f[:, :])
                        tr.then_inc(turned, 1)

                    def period(c, par, whole):
                        if exists(c, whole, 1):
                            turn(c + 1, 1 - par)
                        pe.wait_ge(aT_ready, c + 3)
                        if gain is not None:
                            pe.wait_ge(taken, c + 1)
                        elif not isinstance(c, int) or c:
                            pe.wait_ge(added, c)
                        for j in range(TPC):
                            for k in range(KD):
                                mm = nc.tensor.matmul(ps_o[par][:, j, :], aT[:, par, k, j * P:(j + 1) * P], W[:, k, :], start=(k == 0), stop=(k == KD - 1))
                        mm.then_inc(product, 1)

                    pe.nop().then_inc(turned, 2)
                    pe.nop().then_inc(product, 2)
                    turn(0, 0)
                    pe.wait_ge(w_in, 16)
                    by_pairs(pe, period, NCH - 2)

    def router(name, X, rms_gain, Yh, Yl, Wh, Wl, comb, lower_dram, neg_half):
        with Space(name) as s:
            Wg = s.sb("Wg", [P, KD, E])
            lower_t = s.sb("lower_t", [P, E * E])
            raw = s.sb("raw", [P, PIECE])
            sq = s.sb("sq", [P, 2, D])
            ssq, ms, rrms = (s.sb(n, [P, TPC]) for n in ("ssq", "ms", "rrms"))
            Ys = s.sb("Ys", [P, TPC, D])
            yT = s.sb("yT", [P, 2, KD, CHUNK])
            top = s.sb("top", [P, NT])
            shifted, probs, ex, pm = (s.sb(n, [P, NT, E]) for n in ("shifted", "probs", "ex", "pm"))
            total, rtotal, psum_, rsum = (s.sb(n, [P, NT]) for n in ("total", "rtotal", "psum_", "rsum"))
            above, equal, ahead = (s.sb(n, [P, NT, E, E]) for n in ("above", "equal", "ahead"))
            rank = s.sb("rank", [P, NT, E])
            ps_t = s.ps("ps_t", [P, KD, CHUNK])
            ps_g = s.ps("ps_g", [P, NT, E])
            w_in, raw_in, w_hi, w_lo = s.sem("w_in"), s.sem("raw_in"), s.sem("w_hi"), s.sem("w_lo")
            squared, ms_done, rrms_done, normed = s.sem("squared"), s.sem("ms_done"), s.sem("rrms_done"), s.sem("normed")
            turned, yT_ready, hi_done, lo_done = s.sem("turned"), s.sem("yT_ready"), s.sem("hi_done"), s.sem("lo_done")
            logits, exped, step = s.sem("logits"), s.sem("exped"), s.sem("step")
            with nc.Block() as block:

                @block.sync
                def _(sp):
                    sp.dma_start(Wg[:, :, :], gate.rearrange("(k p) e -> p k e", p=P)).then_inc(w_in, 16)
                    sp.dma_start(lower_t[:, :], lower_dram).then_inc(w_in, 16)
                    with sp.Fori(0, NCH) as c:
                        wait_apart(sp, w_lo, c + 1)
                        sp.dma_start(raw[:, :], w_all[0][:, bass.ds(c * PIECE, PIECE)]).then_inc(raw_in, 16)

                @block.gpsimd
                def _(pool):
                    pool.nop().then_inc(ms_done, 1)
                    with pool.Fori(0, NCH) as c:
                        wait_apart(pool, squared, c * TPC + TPC + 2)
                        wait_apart(pool, normed, c * TPC + TPC)
                        nc.gpsimd.tensor_scalar(ms[:, :], ssq[:, :], 1.0 / D, RMS_EPS, ALU.mult, ALU.add).then_inc(ms_done, 1)
                        pool.wait_ge(ms_done, c + 2)
                        nc.gpsimd.tensor_tensor(rrms[:, :], ms[:, :], neg_half[:, 0:TPC], ALU.pow).then_inc(rrms_done, 1)

                @block.scalar
                def _(act):
                    def squares(c):
                        act.wait_ge(ms_done, c + 1)
                        for j in range(TPC):
                            act.wait_ge(squared, c * TPC + j + 1)
                            nc.scalar.activation(sq[:, j % 2, :], X[:, bass.ds(c * TPC + j, 1), :].rearrange("p a f -> p (a f)"),
                                                 ACT.Square, accum_out=ssq[:, j:j + 1]).then_inc(squared, 1)

                    def period(c, par, whole):
                        if exists(c, whole, 1):
                            squares(c + 1)
                        act.wait_ge(turned, c + 2)
                        act.wait_ge(logits, c + 1)
                        act.wait_ge(lo_done, c + 1)
                        nc.scalar.copy(yT[:, par, :, :], ps_t[:, :, :]).then_inc(yT_ready, 1)
                        act.wait_ge(raw_in, c * 16 + 16)
                        nc.scalar.copy(Wh[0][:, bass.ds(c * PIECE, PIECE)], raw[:, :]).then_inc(w_hi, 1)

                    act.nop().then_inc(squared, 2)
                    squares(0)
                    by_pairs(act, period, NCH - 2)
                    act.wait_ge(step, 2)
                    nc.scalar.activation(ex[:, :, :], shifted[:, :, :], ACT.Exp).then_inc(exped, 1)

                @block.vector
                def _(dve):
                    def norm(c):
                        dve.wait_ge(rrms_done, c + 1)
                        dve.wait_ge(turned, c + 1)
                        for j in range(TPC):
                            nc.vector.scalar_tensor_tensor(
                                out=Ys[:, j, :], in0=X[:, bass.ds(c * TPC + j, 1), :].rearrange("p a f -> p (a f)"),
                                scalar=rrms[:, j:j + 1], in1=rms_gain, op0=ALU.mult, op1=ALU.mult).then_inc(normed, 1)

                    def period(c, par, whole):
                        if exists(c, whole, 1):
                            norm(c + 1)
                        dve.wait_ge(yT_ready, c + 1)
                        nc.vector.tensor_copy(Yh[:, :, cols(c)], yT[:, par, :, :]).then_inc(hi_done, 1)
                        dve.wait_ge(hi_done, c + 1)
                        nc.vector.tensor_tensor(Yl[:, :, cols(c)], yT[:, par, :, :], Yh[:, :, cols(c)].bitcast(F32), ALU.subtract).then_inc(lo_done, 1)
                        there = bass.ds(c * PIECE, PIECE)
                        dve.wait_ge(w_hi, c + 1)
                        nc.vector.tensor_tensor(Wl[0][:, there], raw[:, :], Wh[0][:, there].bitcast(F32), ALU.subtract).then_inc(w_lo, 1)

                    dve.nop().then_inc(normed, TPC)
                    dve.nop().then_inc(lo_done, 2)
                    dve.nop().then_inc(w_lo, 1)
                    norm(0)
                    by_pairs(dve, period, NCH - 2)

                    def after(n):
                        dve.wait_ge(step, n)

                    dve.wait_ge(w_in, 32)
                    dve.wait_ge(logits, NCH + 2)
                    nc.vector.reduce_max(top[:, :], ps_g[:, :, :], AX.X).then_inc(step, 1)
                    after(1)
                    nc.vector.tensor_tensor(shifted[:, :, :], ps_g[:, :, :], col_bcast(top[:, :], E), ALU.subtract).then_inc(step, 1)
                    dve.wait_ge(exped, 1)
                    nc.vector.reduce_sum(total[:, :], ex[:, :, :], AX.X).then_inc(step, 1)
                    after(3)
                    nc.vector.reciprocal(rtotal[:, :], total[:, :]).then_inc(step, 1)
                    after(4)
                    nc.vector.tensor_tensor(probs[:, :, :], ex[:, :, :], col_bcast(rtotal[:, :], E), ALU.mult).then_inc(step, 1)
                    after(5)
                    mine = probs[:, :, :].unsqueeze(3).to_broadcast([P, NT, E, E])
                    other = probs[:, :, :].unsqueeze(2).to_broadcast([P, NT, E, E])
                    nc.vector.tensor_tensor(above[:, :, :, :], other, mine, ALU.is_gt).then_inc(step, 1)
                    nc.vector.tensor_tensor(equal[:, :, :, :], other, mine, ALU.is_equal).then_inc(step, 1)
                    after(7)
                    nc.vector.tensor_tensor(ahead[:, :, :, :].rearrange("p q a b -> p q (a b)"), equal[:, :, :, :].rearrange("p q a b -> p q (a b)"),
                                            row_bcast(lower_t[:, :], NT), ALU.mult).then_inc(step, 1)
                    after(8)
                    nc.vector.tensor_tensor(above[:, :, :, :], above[:, :, :, :], ahead[:, :, :, :], ALU.add).then_inc(step, 1)
                    after(9)
                    nc.vector.reduce_sum(rank[:, :, :], above[:, :, :, :], AX.X).then_inc(step, 1)
                    after(10)
                    nc.vector.scalar_tensor_tensor(out=pm[:, :, :], in0=rank[:, :, :], scalar=2.0, in1=probs[:, :, :],
                                                   op0=ALU.is_lt, op1=ALU.mult).then_inc(step, 1)
                    after(11)
                    nc.vector.reduce_sum(psum_[:, :], pm[:, :, :], AX.X).then_inc(step, 1)
                    after(12)
                    nc.vector.reciprocal(rsum[:, :], psum_[:, :]).then_inc(step, 1)
                    after(13)
                    nc.vector.tensor_tensor(comb[:, :, :], pm[:, :, :], col_bcast(rsum[:, :], E), ALU.mult)

                @block.tensor
                def _(pe):
                    pe.nop().then_inc(turned, 1)
                    pe.nop().then_inc(logits, 2)
                    pe.wait_ge(w_in, 32)

                    def turn(c):
                        pe.wait_ge(normed, c * TPC + TPC + TPC)
                        for k in range(KD):
                            for j in range(TPC):
                                tr = nc.tensor.transpose(ps_t[:, k, j * P:(j + 1) * P], Ys[:, j, k * P:(k + 1) * P], ident_f[:, :])
                        tr.then_inc(turned, 1)

                    def period(c, par, whole):
                        pe.wait_ge(yT_ready, c + 1)
                        if exists(c, whole, 1):
                            turn(c + 1)
                        for j in range(TPC):
                            for k in range(KD):
                                mm = nc.tensor.matmul(ps_g[:, bass.ds(c * TPC + j, 1), :].rearrange("p a e -> p (a e)"),
                                                      yT[:, par, k, j * P:(j + 1) * P], Wg[:, k, :], start=(k == 0), stop=(k == KD - 1))
                        mm.then_inc(logits, 1)

                    turn(0)
                    by_pairs(pe, period, NCH - 2)

    def experts(name, Yh, Yl, Wh, Wl, comb, Fx, gain):
        products = ((0, 0), (0, 1), (1, 0))
        with Space(name) as s:
            raw = s.sb("raw", [P, PIECE])
            x1 = s.sb("x1", [P, TPC, D])
            gated = s.sb("gated", [P, 2, CHUNK])
            h = s.sb("h", [P, 2, CHUNK])
            hh, hl = s.sb("hh", [P, 2, CHUNK], F32R), s.sb("hl", [P, 2, CHUNK], F32R)
            ps_1 = [s.ps(f"ps_1{n}", [P, CHUNK]) for n in range(2)]
            ps_3 = [s.ps(f"ps_3{n}", [P, CHUNK]) for n in range(2)]
            ps_y = s.ps("ps_y", [P, TPC, D])
            raw_in, w_hi, w_lo = s.sem("raw_in"), s.sem("w_hi"), s.sem("w_lo")
            x1_in, stored = s.sem("x1_in"), s.sem("stored")
            up_ready, silu_done, multiplied = s.sem("up_ready"), s.sem("silu_done"), s.sem("multiplied")
            hi_done, lo_done, down_done = s.sem("hi_done"), s.sem("lo_done"), s.sem("down_done")
            weighed, gained, final = s.sem("weighed"), s.sem("gained"), s.sem("final")

            def at(e, c):
                return c + e * NCH

            with nc.Block() as block:

                @block.sync
                def _(sp):
                    for e in range(1, E):
                        with sp.Fori(0, NCH) as c:
                            wait_apart(sp, w_lo, at(e - 1, c) + 1)
                            sp.dma_start(raw[:, :], w_all[e][:, bass.ds(c * PIECE, PIECE)]).then_inc(raw_in, 16)
                    with sp.Fori(0, NCH) as c:
                        wait_apart(sp, final, c + 1)
                        sp.dma_start(x1[:, :, :], by_tile(x1_dram)[:, tiles(c), :]).then_inc(x1_in, 16)
                        wait_apart(sp, final, c + 2)
                        sp.dma_start(by_tile(out)[:, tiles(c), :], Fx[:, tiles(c), :]).then_inc(stored, 16)
                    sp.wait_ge(stored, 16 * NCH)

                @block.gpsimd
                def _(pool):
                    pool.nop().then_inc(lo_done, 2)
                    with pool.Fori(0, E * NCH) as n:
                        for u in range(HB):
                            wait_apart(pool, hi_done, n * HB + u + 1)
                            nc.gpsimd.tensor_tensor(hl[:, u % 2, :], h[:, u % 2, :], hh[:, u % 2, :].bitcast(F32), ALU.subtract).then_inc(lo_done, 1)

                @block.scalar
                def _(act):
                    act.nop().then_inc(silu_done, 2)
                    for e in range(E):
                        with act.Fori(0, NCH) as c:
                            for u in range(HB):
                                n = at(e, c)
                                act.wait_ge(up_ready, n * HB + u + 1)
                                act.wait_ge(multiplied, n * HB + u + 1)
                                nc.scalar.activation(gated[:, u % 2, :], ps_1[u % 2][:, :], ACT.Silu).then_inc(silu_done, 1)
                                act.wait_ge(multiplied, n * HB + u + 3)
                                act.wait_ge(down_done, n * HB + u + 1)
                                nc.scalar.copy(hh[:, u % 2, :], h[:, u % 2, :]).then_inc(hi_done, 1)
                                if e + 1 < E and u == HB // 2:
                                    act.wait_ge(raw_in, n * 16 + 16)
                                    nc.scalar.copy(Wh[(e + 1) % 2][:, bass.ds(c * PIECE, PIECE)], raw[:, :]).then_inc(w_hi, 1)

                @block.vector
                def _(dve):
                    def weigh(e, c):
                        n = at(e, c)
                        dve.wait_ge(down_done, n * HB + HB + 2)
                        dve.wait_ge(weighed, n * TPC + TPC)
                        for j in range(TPC):
                            i = bass.ds(c * TPC + j, 1)
                            f = Fx[:, i, :].rearrange("p a f -> p (a f)")
                            w = comb[:, i, e:e + 1].rearrange("p a f -> p (a f)")
                            nc.vector.scalar_tensor_tensor(out=f, in0=ps_y[:, j, :], scalar=w, in1=f, op0=ALU.mult, op1=ALU.add).then_inc(weighed, 1)

                    def finish(e, c):
                        if e == E - 1:
                            dve.wait_ge(weighed, at(e, c) * TPC + 2 * TPC)
                            nc.vector.tensor_tensor(Fx[:, tiles(c), :], Fx[:, tiles(c), :], row_bcast(gain, TPC), ALU.mult).then_inc(gained, 1)
                            dve.wait_ge(gained, c + 1)
                            dve.wait_ge(x1_in, c * 16 + 16)
                            nc.vector.tensor_tensor(Fx[:, tiles(c), :], Fx[:, tiles(c), :], x1[:, :, :], ALU.add).then_inc(final, 1)

                    def chunk(e, c, before):
                        for u in range(HB):
                            U = at(e, c) * HB + u
                            dve.wait_ge(silu_done, U + 3)
                            dve.wait_ge(lo_done, U + 1)
                            nc.vector.tensor_tensor(h[:, u % 2, :], gated[:, u % 2, :], ps_3[u % 2][:, :], ALU.mult).then_inc(multiplied, 1)
                            if u == 0 and before is not None:
                                weigh(*before)
                            if u == HB // 2 and before is not None:
                                finish(*before)
                            if u == HB // 2 + 1 and e + 1 < E:
                                there = bass.ds(c * PIECE, PIECE)
                                dve.wait_ge(w_hi, at(e, c) + 1)
                                nc.vector.tensor_tensor(Wl[(e + 1) % 2][:, there], raw[:, :], Wh[(e + 1) % 2][:, there].bitcast(F32),
                                                        ALU.subtract).then_inc(w_lo, 1)

                    dve.nop().then_inc(multiplied, 2)
                    dve.nop().then_inc(w_lo, 1)
                    dve.nop().then_inc(weighed, TPC)
                    dve.nop().then_inc(final, 1)
                    for e in range(E):
                        chunk(e, 0, (e - 1, NCH - 1) if e else None)
                        with dve.Fori(1, NCH) as c:
                            chunk(e, c, (e, c - 1))
                    weigh(E - 1, NCH - 1)
                    finish(E - 1, NCH - 1)

                @block.tensor
                def _(pe):
                    def up(e, c, u):
                        pe.wait_ge(multiplied, at(e, c) * HB + u + 1)
                        for bank, off in ((ps_1, 0), (ps_3, KD * HID)):
                            for k in range(KD):
                                for a, b in products:
                                    w = (Wh, Wl)[a][e % 2][:, off + k * HID + u * P:off + k * HID + (u + 1) * P]
                                    mm = nc.tensor.matmul(bank[u % 2][:, :], w, (Yh, Yl)[b][:, k, cols(c)],
                                                          start=(k == 0 and (a, b) == products[0]), stop=(k == KD - 1 and (a, b) == products[-1]))
                        mm.then_inc(up_ready, 1)

                    def down(e, c, u):
                        pe.wait_ge(lo_done, at(e, c) * HB + u + 3)
                        if u == 0:
                            pe.wait_ge(weighed, at(e, c) * TPC + TPC)
                        off = 2 * KD * HID + u * D
                        for j in range(TPC):
                            for a, b in products:
                                first = u == 0 and j % (CHUNK // D) == 0 and (a, b) == products[0]
                                mm = nc.tensor.matmul(ps_y[:, j, :], (hh, hl)[a][:, u % 2, j * P:(j + 1) * P], (Wh, Wl)[b][e % 2][:, off:off + D],
                                                      start=first, stop=True, skip_group_check=True)
                        mm.then_inc(down_done, 1)

                    def chunk(e, c, before):
                        for u in range(HB):
                            up(e, c, u)
                            if u:
                                down(e, c, u - 1)
                            elif before is not None:
                                down(*before, HB - 1)

                    pe.nop().then_inc(down_done, 2)
                    for e in range(E):
                        if e:
                            pe.wait_ge(w_lo, e * NCH + 1)
                        chunk(e, 0, (e - 1, NCH - 1) if e else None)
                        with pe.Fori(1, NCH) as c:
                            chunk(e, c, (e, c - 1))
                    down(E - 1, NCH - 1, HB - 1)

    stack = ExitStack()

    def keep_sb(where, name, shape, dt=F32):
        return where.enter_context(nc.sbuf_tensor(name, shape, dt))

    with stack:
        begun = stack.enter_context(nc.semaphore("begun"))
        ident_f = keep_sb(stack, "ident_f", [P, P])
        ident_b = keep_sb(stack, "ident_b", [P, P], BF16)
        neg_ident_b = keep_sb(stack, "neg_ident_b", [P, P], BF16)
        mask_k = keep_sb(stack, "mask_k", [P, P], BF16)
        mask_q = keep_sb(stack, "mask_q", [P, P], BF16)
        mod = keep_sb(stack, "mod", [P, 6, D])
        gains = keep_sb(stack, "gains", [P, 2, D])
        neg_half = keep_sb(stack, "neg_half", [P, TPC])
        setup(ident_f, ident_b, neg_ident_b, mask_k, mask_q, mod, gains, neg_half)

        tok_b = keep_sb(stack, "tok_b", [P, NT, D])
        shift_a, scale_a, gain_a, shift_b, scale_b, gain_b = (mod[:, v, :] for v in range(6))
        with ExitStack() as first:
            tok_a = keep_sb(first, "tok_a", [P, NT, D])
            project("qkv1", x, shift_a, scale_a, None, None, wqkv[0], rope[0], tok_b, KVH[0], neg_half)
            attention("att1", tok_b, tok_a, KVH[0])
            out_projection("out1", tok_a, wo[0], gain_a, x, tok_b, x1_dram)
            project("qkv2", x1_dram, shift_b, scale_b, gains[:, 0, :], h2_dram, wqkv[1], rope[1], tok_b, KVH[1], neg_half)
            attention("att2", tok_b, tok_a, KVH[1])
            out_projection("out2", tok_a, wo[1], None, h2_dram, tok_b, None)
        with ExitStack() as last:
            comb = keep_sb(last, "comb", [P, NT, E])
            Yh, Yl = (keep_sb(last, n, [P, KD, T], F32R) for n in ("Yh", "Yl"))
            Wh, Wl = ([keep_sb(last, f"{n}{i}", [P, w_all.shape[2]], F32R) for i in range(2)] for n in ("Wh", "Wl"))
            router("router", tok_b, gains[:, 1, :], Yh, Yl, Wh, Wl, comb, lower, neg_half)
            experts("moe", Yh, Yl, Wh, Wl, comb, tok_b, gain_b)


def shape_constants(T, D):
    import numpy as np

    f32 = np.float32
    pos = np.arange(T, dtype=f32)
    half = np.arange(DH // 2, dtype=f32)
    theta = (f32(10000.0) ** (f32(-2.0) * half / f32(DH))).astype(f32)
    inv_freq = (f32(1.0) / f32(10000.0) ** (f32(2.0) * half / f32(DH))).astype(f32)
    rows = np.arange(P) % DH
    rope = np.zeros((2, 2, P, T), f32)
    for n, (freq, of_row, sign) in enumerate((
        (theta, rows // 2, np.where(rows % 2 == 0, -1.0, 1.0)),
        (inv_freq, rows % (DH // 2), np.where(rows < DH // 2, -1.0, 1.0)),
    )):
        angle = (pos[:, None] * freq[None, :]).astype(f32)
        rope[n, 0] = np.cos(angle).astype(f32).T[of_row]
        rope[n, 1] = np.sin(angle).astype(f32).T[of_row] * sign.astype(f32)[:, None]
    ident = np.eye(P, dtype=f32)
    a, b = np.arange(P)[:, None], np.arange(P)[None, :]
    masks = np.stack([np.where(a > b, HIDDEN_NEG, 0.0), np.where(b > a, HIDDEN_NEG, 0.0)]).astype(f32)
    return rope, ident, masks


def kernel(L0_attn_X, L0_attn_W_q, L0_attn_W_k, L0_attn_W_v, L0_attn_W_o, L0_ffn_g1, L0_ffn_g2, L0_ffn_wq, L0_ffn_wk,
           L0_ffn_wv, L0_ffn_wo, L0_ffn_gate, L0_ffn_w1, L0_ffn_w2, L0_ffn_w3, L0_c, L0_wmod):
    import numpy as np
    import concourse.bacc as bacc
    from concourse.bass_utils import run_bass_kernel_spmd as run

    X = np.asarray(L0_attn_X)
    _, T, D = X.shape
    E = np.asarray(L0_ffn_gate).shape[1]
    rope, ident, masks = shape_constants(T, D)
    pairs = np.arange(D) ^ 1
    halves = np.arange(D) ^ (DH // 2)
    q1, k1, v1 = (np.asarray(w).T for w in (L0_attn_W_q, L0_attn_W_k, L0_attn_W_v))
    q2, k2, v2 = (np.asarray(w) for w in (L0_ffn_wq, L0_ffn_wk, L0_ffn_wv))
    nk = k2.shape[1]
    twice = P // nk

    def by_rows(w):
        w = np.asarray(w)
        return w.reshape(E, -1, P, w.shape[2]).transpose(0, 2, 1, 3).reshape(E, P, -1)

    arrays = {
        "x": X[0],
        "wqkv_1": np.concatenate([q1, k1, q1[:, pairs], k1[:, pairs], v1], axis=1),
        "wqkv_2": np.concatenate([q2, *[k2] * twice, q2[:, halves], *[k2[:, halves[:nk]]] * twice, v2], axis=1),
        "rope": rope,
        "wo_1": np.asarray(L0_attn_W_o).T,
        "wo_2": np.asarray(L0_ffn_wo),
        "g12": np.concatenate([np.asarray(L0_ffn_g1), np.asarray(L0_ffn_g2)])[None, :],
        "wmod": np.asarray(L0_wmod),
        "c_col": np.asarray(L0_c)[0].reshape(D // P, P).T,
        "gate": np.asarray(L0_ffn_gate),
        "w_all": np.concatenate([by_rows(L0_ffn_w1), by_rows(L0_ffn_w3), by_rows(L0_ffn_w2)], axis=2),
        "ident": ident,
        "masks": masks,
        "lower": np.ascontiguousarray(np.broadcast_to(np.tril(np.ones((E, E), np.float32), -1).reshape(1, E * E), (P, E * E))),
    }
    arrays = {n: np.ascontiguousarray(a) for n, a in arrays.items()}
    nc = bacc.Bacc("TRN2", target_bir_lowering=False, num_devices=1)
    t = {n: nc.dram_tensor(n, a.shape, mybir.dt.from_np(a.dtype), kind="ExternalInput").ap() for n, a in arrays.items()}
    out = nc.dram_tensor("out", (T, D), F32, kind="ExternalOutput").ap()
    adaln_program(nc, t["x"], (t["wqkv_1"], t["wqkv_2"]), t["rope"], (t["wo_1"], t["wo_2"]), t["g12"], t["wmod"], t["c_col"],
                  t["gate"], t["w_all"], t["ident"], t["masks"], t["lower"], out)
    r = run(nc, [arrays], core_ids=[0])
    return r.results[0]["out"].reshape(1, T, D)
```
